# Optimizing a Trainium2 kernel written in Bass

```python
import numpy as np
import jax
import jax.numpy as jnp

def _softmax(x, axis=-1):
    return jax.nn.softmax(x, axis=axis)
def _gelu(x):
    return jax.nn.gelu(x, approximate=True)
def _silu(x):
    return jax.nn.silu(x)
def _sigmoid(x):
    return jax.nn.sigmoid(x)
def _layernorm(x, axis=-1, eps=1e-5):
    m = jnp.mean(x, axis=axis, keepdims=True)
    v = jnp.var(x, axis=axis, keepdims=True)
    return (x - m) / jnp.sqrt(v + eps)
def _scatter_add(tgt, idx, src, axis=0):
    return tgt.at[idx].add(src)
def _segment_sum(src, seg, n):
    return jax.ops.segment_sum(src, seg, n)

kernel_name = 'mk_conv_attn_hybrid_d2_conv_nchw128_708f45'

def setup_inputs(seed: int = 0):
    np.random.seed(seed)
    _w = jnp.asarray
    def _rec_inputs():
        import jax
        import jax.numpy as jnp
        _gk = jax.random.key(seed)
        x = -0.0005207 + 1.001 * jax.random.normal(jax.random.fold_in(_gk, 1), (4, 128, 64, 64), jnp.float32)
        return x
    x = _rec_inputs()
    def _L0_conv_setup():
        import jax, jax.numpy as jnp
        import numpy as np
        K = 7
        PAD = 3
        GROUPS = 8

        def _unfold(t, k, H, W):
            cols = [t[:, :, i:i + H, j:j + W] for i in range(k) for j in range(k)]
            p = jnp.stack(cols, axis=-1)
            return p.reshape(t.shape[0], t.shape[1], H, W, k, k)
        key = jax.random.key(seed)
        ks = jax.random.split(key, 6)
        B, C, O, H, Wd = (4, 128, 128, 64, 64)
        x = jax.random.normal(ks[0], (B, C, H, Wd), dtype=jnp.float32)
        scale = (2.0 / O) ** 0.5
        Wq = jax.random.normal(ks[1], (O, C), dtype=jnp.float32) * scale
        Wk = jax.random.normal(ks[2], (O, C), dtype=jnp.float32) * scale
        Wv = jax.random.normal(ks[3], (O, C), dtype=jnp.float32) * scale
        rel_h = jax.random.normal(ks[4], (O // 2, 1, 1, K, 1), dtype=jnp.float32)
        rel_w = jax.random.normal(ks[5], (O // 2, 1, 1, 1, K), dtype=jnp.float32)
        return {'x': x, 'Wq': Wq, 'Wk': Wk, 'Wv': Wv, 'rel_h': rel_h, 'rel_w': rel_w}
    _L0_conv_all = _L0_conv_setup()
    _L0_conv_in = {k: v for k, v in _L0_conv_all.items() if k in ('Wq', 'Wk', 'Wv', 'rel_h', 'rel_w', )}
    del _L0_conv_all

    def _L1_attn_setup():
        import jax, jax.numpy as jnp
        import numpy as np
        NUM_HEADS = 16
        N_QUBITS = 8
        LN_EPS = 1e-05

        def _layernorm(y, g, b):
            m = jnp.mean(y, axis=-1, keepdims=True)
            v = jnp.var(y, axis=-1, keepdims=True)
            return (y - m) * jax.lax.rsqrt(v + LN_EPS) * g + b

        def _quantum_attn(x, theta):
            B, S, E = x.shape
            a = x.reshape(B, S, NUM_HEADS, N_QUBITS) + theta
            cp = jnp.cumprod(jnp.cos(a), axis=-1)
            out = jnp.concatenate([cp[..., -1:], cp[..., 1:]], axis=-1)
            return out.reshape(B, S, E)

        def _quantum_ffn(x, phi):
            return jnp.cos(phi) * jnp.cos(x[..., :N_QUBITS])
        key = jax.random.key(seed)
        ks = jax.random.split(key, 8)
        B, S, E, F = (8, 4096, 128, 2048)
        return {'x': jax.random.normal(ks[0], (B, S, E), dtype=jnp.float32), 'theta_attn': jax.random.normal(ks[1], (N_QUBITS,), dtype=jnp.float32), 'phi_ffn': jax.random.normal(ks[2], (N_QUBITS,), dtype=jnp.float32), 'w1': jax.random.normal(ks[3], (F, N_QUBITS), dtype=jnp.float32) * (1.0 / np.sqrt(N_QUBITS)), 'b1': jax.random.normal(ks[4], (F,), dtype=jnp.float32) * 0.01, 'w2': jax.random.normal(ks[5], (E, F), dtype=jnp.float32) * (1.0 / np.sqrt(F)), 'b2': jax.random.normal(ks[6], (E,), dtype=jnp.float32) * 0.01, 'gamma1': jnp.ones((E,), dtype=jnp.float32), 'beta1': jnp.zeros((E,), dtype=jnp.float32), 'gamma2': jnp.ones((E,), dtype=jnp.float32), 'beta2': jnp.zeros((E,), dtype=jnp.float32)}
    _L1_attn_all = _L1_attn_setup()
    _L1_attn_in = {k: v for k, v in _L1_attn_all.items() if k in ('theta_attn', 'phi_ffn', 'w1', 'b1', 'w2', 'b2', 'gamma1', 'beta1', 'gamma2', 'beta2', )}
    del _L1_attn_all

    def _L1_ffn_setup():
        import jax, jax.numpy as jnp
        import numpy as np
        PADDED_SL = 8192
        TEMPERATURE = 1.0
        SIGMA_POW = 0.25

        def _stu_conv(phi, u, n):
            b, sl, d = u.shape
            sgn = jnp.where(jnp.arange(sl) % 2 == 0, 1.0, -1.0).astype(u.dtype)
            sgn3 = sgn[None, :, None]
            Vf = jnp.fft.rfft(phi, n=n, axis=0)
            Uf_p = jnp.fft.rfft(u, n=n, axis=1)
            Uf_m = jnp.fft.rfft(u * sgn3, n=n, axis=1)
            U_plus = jnp.fft.irfft(Vf[None, :, :, None] * Uf_p[:, :, None, :], n=n, axis=1)[:, :sl]
            U_minus = jnp.fft.irfft(Vf[None, :, :, None] * Uf_m[:, :, None, :], n=n, axis=1)[:, :sl]
            U_minus = U_minus * sgn[None, :, None, None]
            return (U_plus, U_minus)

        def _compute_spectral(u, sigma, phi, Mpp, Mpm):
            U_plus, U_minus = _stu_conv(phi, u, PADDED_SL)
            s = sigma ** SIGMA_POW
            out = jnp.einsum('btkd,k,kde->bte', U_plus, s, Mpp)
            out = out + jnp.einsum('btkd,k,kde->bte', U_minus, s, Mpm)
            return out

        def _compute_ar_u(Mu, u):
            sl = u.shape[1]
            out = jnp.zeros(u.shape[:2] + (Mu.shape[-1],), dtype=u.dtype)
            for i in range(Mu.shape[0]):
                ui = jnp.pad(u, ((0, 0), (i, 0), (0, 0)))[:, :sl]
                out = out + jnp.einsum('btd,de->bte', ui, Mu[i])
            return out

        def _stu(u, sigma, phi, Mu, Mpp, Mpm):
            return _compute_spectral(u, sigma, phi, Mpp, Mpm) + _compute_ar_u(Mu, u)
        key = jax.random.key(seed)
        ks = jax.random.split(key, 8)
        b, sl, d, K, k_u = (2, 4096, 128, 16, 3)
        x = jax.random.normal(ks[0], (b, sl, d), dtype=jnp.float32)
        sigma = jax.random.uniform(ks[1], (K,), dtype=jnp.float32, minval=0.001, maxval=1.0)
        phi = jax.random.normal(ks[2], (sl, K), dtype=jnp.float32) / np.sqrt(sl)
        M_u = jax.random.normal(ks[3], (4, k_u, d, d), dtype=jnp.float32) * 0.02
        M_phi_plus = jax.random.normal(ks[4], (4, K, d, d), dtype=jnp.float32) * 0.02
        M_phi_minus = jax.random.normal(ks[5], (4, K, d, d), dtype=jnp.float32) * 0.02
        log_weights = jnp.ones((4,), dtype=jnp.float32)
        u01 = jax.random.uniform(ks[6], (4,), dtype=jnp.float32, minval=1e-06, maxval=1.0 - 1e-06)
        gumbel = -jnp.log(-jnp.log(u01))
        return {'x': x, 'sigma': sigma, 'phi': phi, 'M_u': M_u, 'M_phi_plus': M_phi_plus, 'M_phi_minus': M_phi_minus, 'log_weights': log_weights, 'gumbel': gumbel}
    _L1_ffn_all = _L1_ffn_setup()
    _L1_ffn_in = {k: v for k, v in _L1_ffn_all.items() if k in ('sigma', 'phi', 'M_u', 'M_phi_plus', 'M_phi_minus', 'log_weights', 'gumbel', )}
    del _L1_ffn_all

    return {
        "x": x,
        "L0_conv_Wq": _L0_conv_in["Wq"],
        "L0_conv_Wk": _L0_conv_in["Wk"],
        "L0_conv_Wv": _L0_conv_in["Wv"],
        "L0_conv_rel_h": _L0_conv_in["rel_h"],
        "L0_conv_rel_w": _L0_conv_in["rel_w"],
        "L1_attn_theta_attn": _L1_attn_in["theta_attn"],
        "L1_attn_phi_ffn": _L1_attn_in["phi_ffn"],
        "L1_attn_w1": _L1_attn_in["w1"],
        "L1_attn_b1": _L1_attn_in["b1"],
        "L1_attn_w2": _L1_attn_in["w2"],
        "L1_attn_b2": _L1_attn_in["b2"],
        "L1_attn_gamma1": _L1_attn_in["gamma1"],
        "L1_attn_beta1": _L1_attn_in["beta1"],
        "L1_attn_gamma2": _L1_attn_in["gamma2"],
        "L1_attn_beta2": _L1_attn_in["beta2"],
        "L1_ffn_sigma": _L1_ffn_in["sigma"],
        "L1_ffn_phi": _L1_ffn_in["phi"],
        "L1_ffn_M_u": _L1_ffn_in["M_u"],
        "L1_ffn_M_phi_plus": _L1_ffn_in["M_phi_plus"],
        "L1_ffn_M_phi_minus": _L1_ffn_in["M_phi_minus"],
        "L1_ffn_log_weights": _L1_ffn_in["log_weights"],
        "L1_ffn_gumbel": _L1_ffn_in["gumbel"],
    }

def reference(x, L0_conv_Wq, L0_conv_Wk, L0_conv_Wv, L0_conv_rel_h, L0_conv_rel_w, L1_attn_theta_attn, L1_attn_phi_ffn, L1_attn_w1, L1_attn_b1, L1_attn_w2, L1_attn_b2, L1_attn_gamma1, L1_attn_beta1, L1_attn_gamma2, L1_attn_beta2, L1_ffn_sigma, L1_ffn_phi, L1_ffn_M_u, L1_ffn_M_phi_plus, L1_ffn_M_phi_minus, L1_ffn_log_weights, L1_ffn_gumbel):
    import jax
    import jax.numpy as jnp
    def _L0_conv_ref(x, Wq, Wk, Wv, rel_h, rel_w):
        import jax, jax.numpy as jnp
        import numpy as np
        K = 7
        PAD = 3
        GROUPS = 8

        def _unfold(t, k, H, W):
            cols = [t[:, :, i:i + H, j:j + W] for i in range(k) for j in range(k)]
            p = jnp.stack(cols, axis=-1)
            return p.reshape(t.shape[0], t.shape[1], H, W, k, k)
        B, C, H, W = x.shape
        O = Wq.shape[0]
        g = GROUPS
        q = jnp.einsum('bchw,oc->bohw', x, Wq)
        xp = jnp.pad(x, ((0, 0), (0, 0), (PAD, PAD), (PAD, PAD)))
        k = jnp.einsum('bchw,oc->bohw', xp, Wk)
        v = jnp.einsum('bchw,oc->bohw', xp, Wv)
        kp = _unfold(k, K, H, W)
        vp = _unfold(v, K, H, W)
        kh, kw = jnp.split(kp, 2, axis=1)
        kp = jnp.concatenate([kh + rel_h, kw + rel_w], axis=1)
        kp = kp.reshape(B, g, O // g, H, W, K * K)
        vp = vp.reshape(B, g, O // g, H, W, K * K)
        qg = q.reshape(B, g, O // g, H, W, 1)
        scores = (qg * kp).sum(axis=2)
        attn = jax.nn.softmax(scores, axis=-1)
        out = jnp.einsum('bghwn,bgchwn->bgchw', attn, vp)
        return out.reshape(B, O, H, W)

    def _L1_attn_ref(x, theta_attn, phi_ffn, w1, b1, w2, b2, gamma1, beta1, gamma2, beta2):
        import jax, jax.numpy as jnp
        import numpy as np
        NUM_HEADS = 16
        N_QUBITS = 8
        LN_EPS = 1e-05

        def _layernorm(y, g, b):
            m = jnp.mean(y, axis=-1, keepdims=True)
            v = jnp.var(y, axis=-1, keepdims=True)
            return (y - m) * jax.lax.rsqrt(v + LN_EPS) * g + b

        def _quantum_attn(x, theta):
            B, S, E = x.shape
            a = x.reshape(B, S, NUM_HEADS, N_QUBITS) + theta
            cp = jnp.cumprod(jnp.cos(a), axis=-1)
            out = jnp.concatenate([cp[..., -1:], cp[..., 1:]], axis=-1)
            return out.reshape(B, S, E)

        def _quantum_ffn(x, phi):
            return jnp.cos(phi) * jnp.cos(x[..., :N_QUBITS])
        attn = _quantum_attn(x, theta_attn)
        x1 = _layernorm(x + attn, gamma1, beta1)
        q = _quantum_ffn(x1, phi_ffn)
        h = jax.nn.relu(jnp.einsum('bsq,fq->bsf', q, w1) + b1)
        ffn = jnp.einsum('bsf,ef->bse', h, w2) + b2
        return _layernorm(x1 + ffn, gamma2, beta2)

    def _L1_ffn_ref(x, sigma, phi, M_u, M_phi_plus, M_phi_minus, log_weights, gumbel):
        import jax, jax.numpy as jnp
        import numpy as np
        PADDED_SL = 8192
        TEMPERATURE = 1.0
        SIGMA_POW = 0.25

        def _stu_conv(phi, u, n):
            b, sl, d = u.shape
            sgn = jnp.where(jnp.arange(sl) % 2 == 0, 1.0, -1.0).astype(u.dtype)
            sgn3 = sgn[None, :, None]
            Vf = jnp.fft.rfft(phi, n=n, axis=0)
            Uf_p = jnp.fft.rfft(u, n=n, axis=1)
            Uf_m = jnp.fft.rfft(u * sgn3, n=n, axis=1)
            U_plus = jnp.fft.irfft(Vf[None, :, :, None] * Uf_p[:, :, None, :], n=n, axis=1)[:, :sl]
            U_minus = jnp.fft.irfft(Vf[None, :, :, None] * Uf_m[:, :, None, :], n=n, axis=1)[:, :sl]
            U_minus = U_minus * sgn[None, :, None, None]
            return (U_plus, U_minus)

        def _compute_spectral(u, sigma, phi, Mpp, Mpm):
            U_plus, U_minus = _stu_conv(phi, u, PADDED_SL)
            s = sigma ** SIGMA_POW
            out = jnp.einsum('btkd,k,kde->bte', U_plus, s, Mpp)
            out = out + jnp.einsum('btkd,k,kde->bte', U_minus, s, Mpm)
            return out

        def _compute_ar_u(Mu, u):
            sl = u.shape[1]
            out = jnp.zeros(u.shape[:2] + (Mu.shape[-1],), dtype=u.dtype)
            for i in range(Mu.shape[0]):
                ui = jnp.pad(u, ((0, 0), (i, 0), (0, 0)))[:, :sl]
                out = out + jnp.einsum('btd,de->bte', ui, Mu[i])
            return out

        def _stu(u, sigma, phi, Mu, Mpp, Mpm):
            return _compute_spectral(u, sigma, phi, Mpp, Mpm) + _compute_ar_u(Mu, u)
        T = x.shape[1]
        outs = []
        for i, frac in enumerate((1, 2, 4, 8)):
            xi = x[:, :T // frac]
            si = _stu(xi, sigma, phi, M_u[i], M_phi_plus[i], M_phi_minus[i])
            si = jnp.pad(si, ((0, 0), (0, T - si.shape[1]), (0, 0)))
            outs.append(si)
        y_soft = jax.nn.softmax((log_weights + gumbel) / TEMPERATURE)
        y_hard = jax.nn.one_hot(jnp.argmax(y_soft), 4, dtype=y_soft.dtype)
        weights = y_hard - jax.lax.stop_gradient(y_soft) + y_soft
        stacked = jnp.stack(outs, axis=-1)
        return jnp.sum(stacked * weights, axis=-1)

    def _gn(v, G=32, eps=1e-5):
        B_, C_, H_, W_ = v.shape
        g = v.reshape(B_, G, C_ // G, H_, W_)
        m = jnp.mean(g, axis=(2, 3, 4), keepdims=True)
        s = jnp.var(g, axis=(2, 3, 4), keepdims=True)
        return ((g - m) / jnp.sqrt(s + eps)).reshape(v.shape)

    def _ln_c(v, eps=1e-6):
        m = jnp.mean(v, axis=1, keepdims=True)
        s = jnp.var(v, axis=1, keepdims=True)
        return (v - m) / jnp.sqrt(s + eps)

    def _ln_t(v, eps=1e-5):
        m = jnp.mean(v, axis=-1, keepdims=True)
        s = jnp.var(v, axis=-1, keepdims=True)
        return (v - m) / jnp.sqrt(s + eps)

    def _to_tokens(v):
        B_, C_, H_, W_ = v.shape
        return v.reshape(B_, C_, H_ * W_).transpose(0, 2, 1)
    def _from_tokens(t, like):
        B_, C_, H_, W_ = like.shape
        return t.transpose(0, 2, 1).reshape(B_, C_, H_, W_)

    x = x + _L0_conv_ref(_gn(x), L0_conv_Wq, L0_conv_Wk, L0_conv_Wv, L0_conv_rel_h, L0_conv_rel_w)
    t = _to_tokens(x)
    t = t + _L1_attn_ref(_ln_t(t), L1_attn_theta_attn, L1_attn_phi_ffn, L1_attn_w1, L1_attn_b1, L1_attn_w2, L1_attn_b2, L1_attn_gamma1, L1_attn_beta1, L1_attn_gamma2, L1_attn_beta2)
    t = t + _L1_ffn_ref(_ln_t(t), L1_ffn_sigma, L1_ffn_phi, L1_ffn_M_u, L1_ffn_M_phi_plus, L1_ffn_M_phi_minus, L1_ffn_log_weights, L1_ffn_gumbel)
    x = _from_tokens(t, x)
    return x


_drawn_inputs = setup_inputs


def setup_inputs(seed=0):
    import zlib

    import numpy as np

    out = dict(_drawn_inputs(seed))
    spreads = {'L1_attn_gamma1': (1.0, 0.2),
     'L1_attn_beta1': (0.0, 0.1),
     'L1_attn_gamma2': (1.0, 0.2),
     'L1_attn_beta2': (0.0, 0.1),
     'L1_ffn_log_weights': (1.0, 0.2)}
    factors = {'L1_attn_b1': 22.347, 'L1_attn_b2': 8.0}
    for name, (base, spread) in spreads.items():
        noise = np.random.default_rng([zlib.crc32(name.encode()), seed]).standard_normal(out[name].shape)
        drawn = base * np.exp(spread * noise) if base else spread * noise
        out[name] = jnp.asarray(drawn.astype(out[name].dtype))
    for name, factor in factors.items():
        out[name] = (out[name] * factor).astype(out[name].dtype)
    return out
```

```python
import concourse.bass as bass
from concourse import mybir
from contextlib import ExitStack
import math

F32 = mybir.dt.float32
F16 = mybir.dt.float16
I32 = mybir.dt.int32
ALU = mybir.AluOpType
ACT = mybir.ActivationFunctionType
AX = mybir.AxisListType

B, C, HH, WW = 4, 128, 64, 64
T = HH * WW
P = 128
WIN, PAD = 7, 3
HEADS, HC = 8, C // 8
ROWS = 8
STRIPS = HH // ROWS
NSTRIP = B * STRIPS
KROWS, KCOLS = ROWS + WIN - 1, WW + 2 * PAD
PQ = 8
PK = PQ + WIN - 1
KEYS = PK * PK
HALF = KEYS // 2
NPAIR = WW // (2 * PQ)
STOK = ROWS * WW
QH, NQB = 16, 8
FF = 2048
FT = FF // P
NEG = -1.0e30
U_SCALE = 1024.0
TWO_PI = 2.0 * math.pi
TP1 = 6.28125
TP2 = TWO_PI - TP1
MAGIC = 1.5 * 2.0 ** 23
SIN_LO, SIN_HI = -1.5 * math.pi + 1e-6, 0.5 * math.pi - 1e-6


class Chain:

    def __init__(self, eng, sem, base=0):
        self.eng, self.sem, self.base, self.n = eng, sem, base, 0

    def then(self, ins):
        ins.then_inc(self.sem, 1)
        self.n += 1
        return self.n

    def link(self, ins):
        self.then(ins)
        self.eng.wait_ge(self.sem, self.base + self.n)

    def wait(self, n=None):
        self.eng.wait_ge(self.sem, self.base + (self.n if n is None else n))


def raw(ap, offset, dims):
    return bass.AP(tensor=ap.tensor, offset=ap.offset + offset, ap=dims)


def prepare(nc, pers, x, wq, wk, wv, rel_h, rel_w, phi_ffn, xn_strips):
    with ExitStack() as ctx:
        def sb(name, shape, dt=F32):
            return ctx.enter_context(nc.sbuf_tensor(name, shape, dt))

        def sem(name):
            return ctx.enter_context(nc.semaphore(name))

        xs = sb("pr_x", [P, B, T])
        xpad = [sb(f"pr_xpad{n}", [P, HH + 2 * PAD, KCOLS]) for n in range(2)]
        w_in = sb("pr_w", [P, 3, P])
        rel = sb("pr_rel", [P, WIN])
        gmask = sb("pr_gmask", [P, HEADS])
        relbd = sb("pr_relbd", [P, HEADS, WIN])
        gsum = sb("pr_gsum", [P, P])
        gsum_t = sb("pr_gsumt", [P, P])
        G = sb("pr_G", [P, HEADS, WIN])
        st = sb("pr_st", [P, B, 8, 6])
        mv = sb("pr_mv", [P, B, 2])
        gm = sb("pr_gm", [P, B])
        dd = sb("pr_dd", [P, B])
        var = sb("pr_var", [P, B])
        rs = sb("pr_rs", [P, B])
        ra = sb("pr_ra", [P, B])
        pidx = sb("pr_pidx", [P, 1], I32)
        pint = sb("pr_pint", [P, 4], I32)
        pf = sb("pr_pf", [P, 4])
        grid = sb("pr_grid", [P, KROWS, KCOLS])
        gridB = sb("pr_gridb", [P, KROWS, 5, 16])
        wgrid = sb("pr_wgrid", [P, 2, KEYS])
        wtmp = sb("pr_wtmp", [P, 3, KEYS])
        ph = sb("pr_ph", [P, 3, NQB])
        psT = ctx.enter_context(nc.psum_tensor("pr_psT", [P, 4, P], F32))
        psG = ctx.enter_context(nc.psum_tensor("pr_psG", [P, 512], F32))
        x_in = [sem(f"pr_x_in{b}") for b in range(B)]
        w_in_s, rel_in = sem("pr_w_in"), sem("pr_rel_in")
        consts, weights_t, g_done = sem("pr_consts"), sem("pr_weights_t"), sem("pr_g_done")
        relbd_ready, mean_ready, sq_ready = sem("pr_relbd"), sem("pr_mean"), sem("pr_sq")
        gstat, pad_ready, stored = sem("pr_gstat"), sem("pr_pad_ready"), [sem("pr_st0"), sem("pr_st1")]
        phi_in, dch, pch, cosd = sem("pr_phi_in"), sem("pr_dch"), sem("pr_pch"), sem("pr_cosd")
        phi_red = sem("pr_phi_red")
        block = ctx.enter_context(nc.Block())

        @block.sync
        def _(sp):
            sp.dma_start(w_in[:, 0, :], wq).then_inc(w_in_s, 16)
            sp.dma_start(w_in[:, 1, :], wk).then_inc(w_in_s, 16)
            sp.dma_start(w_in[:, 2, :], wv).then_inc(w_in_s, 16)
            half = C // 2
            sp.dma_start(rel[0:half, :], rel_h.rearrange("o a b k c -> o (a b k c)")).then_inc(rel_in, 16)
            sp.dma_start(rel[half:C, :], rel_w.rearrange("o a b c k -> o (a b c k)")).then_inc(rel_in, 16)
            for b in range(B):
                sp.dma_start(xs[:, b, :], x[b].rearrange("c h w -> c (h w)")).then_inc(x_in[b], 16)
            for b in range(B):
                sp.wait_ge(pad_ready, b + 1)
                flat = xpad[b % 2][:].rearrange("p h w -> p (h w)")
                for s in range(STRIPS):
                    a = s * ROWS * KCOLS
                    sp.dma_start(xn_strips[b * STRIPS + s, :, 0:KROWS * KCOLS],
                                 flat[:, a:a + KROWS * KCOLS]).then_inc(stored[b % 2], 16)
                sp.dma_start(xn_strips[b * STRIPS:(b + 1) * STRIPS, :, KROWS * KCOLS:].rearrange("s c n -> c s n"),
                             xs[:, b, :].rearrange("c (s n) -> c s n", n=STOK)).then_inc(stored[b % 2], 16)
            for n in range(2):
                sp.wait_ge(stored[n], 16 * (STRIPS + 1) * B // 2)

        @block.gpsimd
        def _(pool):
            ch = Chain(pool, pch)
            ident = pers["ident"]
            pool.dma_start(ph[:, 0, :], phi_ffn.partition_broadcast(P)).then_inc(phi_in, 16)
            ch.then(pool.memset(ident[:], 0.0))
            ch.then(pool.memset(gmask[:], 1.0))
            ch.then(pool.memset(gsum[:], 1.0 / 4))
            ch.then(pool.iota(pidx[:], pattern=[[0, 1]], base=0, channel_multiplier=1))
            ch.then(pool.iota(grid[:], pattern=[[1, KROWS], [0, KCOLS]], base=0, channel_multiplier=0,
                              allow_small_or_imprecise_dtypes=True))
            ch.then(pool.iota(gridB[:], pattern=[[0, KROWS], [0, 5], [1, 16]], base=0, channel_multiplier=0,
                              allow_small_or_imprecise_dtypes=True))
            ch.then(pool.iota(wgrid[:, 0, :], pattern=[[1, PK], [0, PK]], base=0, channel_multiplier=0,
                              allow_small_or_imprecise_dtypes=True))
            ch.link(pool.iota(wgrid[:, 1, :], pattern=[[0, PK], [1, PK]], base=0, channel_multiplier=0,
                              allow_small_or_imprecise_dtypes=True))
            ch.link(pool.affine_select(out=ident[:], in_=ident[:], compare_op=ALU.not_equal, fill=1.0,
                                       base=0, pattern=[[-1, P]], channel_multiplier=1))
            ch.link(pool.affine_select(out=gmask[:], in_=gmask[:], compare_op=ALU.is_ge, fill=0.0,
                                       base=0, pattern=[[-HC, HEADS]], channel_multiplier=1))
            ch.link(pool.affine_select(out=gmask[:], in_=gmask[:], compare_op=ALU.is_ge, fill=0.0,
                                       base=HC - 1, pattern=[[HC, HEADS]], channel_multiplier=-1))
            g4 = gsum[:].rearrange("p (g f) -> p g f", f=4)
            ch.link(pool.affine_select(out=g4, in_=g4, compare_op=ALU.is_ge, fill=0.0,
                                       base=0, pattern=[[-4, P // 4], [0, 4]], channel_multiplier=1))
            ch.link(pool.affine_select(out=g4, in_=g4, compare_op=ALU.is_ge, fill=0.0,
                                       base=3, pattern=[[4, P // 4], [0, 4]], channel_multiplier=-1))
            pool.memset(xpad[0][:], 0.0).then_inc(consts, 1)
            pool.memset(xpad[1][:], 0.0).then_inc(consts, 1)

        @block.tensor
        def _(pe):
            pe.wait_ge(pch, 13)
            pe.wait_ge(w_in_s, 48)
            for n in range(3):
                mm = pe.transpose(psT[:, n, :], w_in[:, n, :], pers["ident"][:])
            mm.then_inc(weights_t, 1)
            pe.wait_ge(relbd_ready, 1)
            pe.matmul(psG[:, 0:HEADS * WIN], w_in[:, 0, :], relbd[:].rearrange("p g k -> p (g k)"),
                      start=True, stop=True).then_inc(g_done, 1)
            pe.wait_ge(mean_ready, 1)
            pe.matmul(psT[:, 3, 0:B], gsum[:], gm[:], start=True, stop=True).then_inc(gstat, 1)
            pe.wait_ge(sq_ready, 1)
            pe.matmul(psT[:, 3, 8:8 + B], gsum[:], dd[:], start=True, stop=True).then_inc(gstat, 1)

        @block.scalar
        def _(act):
            act.wait_ge(phi_red, 1)
            act.activation(pers["cosphi"][:], ph[:, 2, :], ACT.Sin, bias=pers["halfpi"][:, 0:1]).then_inc(cosd, 1)

        @block.vector
        def _(v):
            ch = Chain(v, dch)
            ch.then(v.memset(pers["halfpi"][:], math.pi / 2))
            ch.then(v.memset(pers["wk"][:], 0.0))
            ch.then(v.memset(pers["LA"][:], 0.0))
            ch.link(v.memset(pers["LB"][:], 0.0))
            v.wait_ge(phi_in, 16)
            ch.link(v.tensor_scalar(ph[:, 1, :], ph[:, 0, :], 1.0 / TWO_PI, 0.25, ALU.mult, ALU.add))
            ch.link(v.tensor_scalar(ph[:, 1, :], ph[:, 1, :], MAGIC, MAGIC, ALU.add, ALU.subtract))
            ch.link(v.scalar_tensor_tensor(out=ph[:, 2, :], in0=ph[:, 1, :], scalar=-TP1, in1=ph[:, 0, :],
                                           op0=ALU.mult, op1=ALU.add))
            ch.link(v.scalar_tensor_tensor(out=ph[:, 2, :], in0=ph[:, 1, :], scalar=-TP2, in1=ph[:, 2, :],
                                           op0=ALU.mult, op1=ALU.add))
            v.tensor_scalar(ph[:, 2, :], ph[:, 2, :], SIN_LO, SIN_HI, ALU.max, ALU.min).then_inc(phi_red, 1)
            v.wait_ge(pch, 13)
            for n, (sh, mask) in enumerate(((0, 31), (3, 7), (0, 7))):
                ch.then(v.tensor_scalar(pint[:, n:n + 1], pidx[:], sh, mask, ALU.logical_shift_right,
                                        ALU.bitwise_and))
            ch.wait()
            ch.link(v.tensor_copy(pf[:, 0:3], pint[:, 0:3]))
            ch.link(v.tensor_scalar(pf[:, 3:4], pf[:, 0:1], -16.0, None, ALU.add))
            ch.link(v.tensor_scalar(pers["hotA"][:], grid[:], pf[:, 3:4], None, ALU.is_equal))
            ch.link(v.tensor_scalar(pers["hotB"][:], gridB[:].rearrange("p y a c -> p y (a c)")[:, :, 0:KCOLS], pf[:, 3:4], None, ALU.is_equal))
            for n in range(2):
                ch.link(v.tensor_scalar(wtmp[:, 2, :], wgrid[:, n, :], pf[:, 1 + n:2 + n], None, ALU.subtract))
                ch.link(v.tensor_scalar(wtmp[:, n, :], wtmp[:, 2, :], 0.0, None, ALU.is_ge))
                ch.link(v.tensor_scalar(wtmp[:, 2, :], wtmp[:, 2, :], float(WIN - 1), None, ALU.is_le))
                ch.link(v.tensor_tensor(wtmp[:, n, :], wtmp[:, n, :], wtmp[:, 2, :], ALU.mult))
            ch.link(v.tensor_tensor(wtmp[:, 2, :], wtmp[:, 0, :], wtmp[:, 1, :], ALU.mult))
            ch.link(v.tensor_scalar(pers["mask"][:], wtmp[:, 2, :], -NEG, NEG, ALU.mult, ALU.add))
            v.wait_ge(rel_in, 32)
            for g in range(HEADS):
                ins = v.tensor_scalar(relbd[:, g, :], rel[:], gmask[:, g:g + 1], None, ALU.mult)
            ins.then_inc(relbd_ready, 1)
            v.wait_ge(weights_t, 1)
            for s in range(2):
                src = psT[:, :, s * 64:s * 64 + 64].rearrange("p n (j i) -> p n j i", i=HC)
                v.tensor_copy(pers["wk"][:, s, :].rearrange("p (j i) -> p j i", i=32)[:, :, 0:HC], src[:, 1])
                for y in range(PQ):
                    if s == 0:
                        v.tensor_copy(pers["LA"][:, y, :].rearrange("p (j i) -> p j i", i=32)[:, :, 0:HC], src[:, 0])
                for y in range(16):
                    if s == 1:
                        v.tensor_copy(pers["LB"][:, y, :].rearrange("p (j i) -> p j i", i=32)[:, :, 0:HC], src[:, 0])
            v.tensor_copy(pers["wv"][:], psT[:, 2, :])
            v.wait_ge(g_done, 1)
            ch.link(v.tensor_copy(G[:].rearrange("p g k -> p (g k)"), psG[:, 0:HEADS * WIN]))
            for y in range(PQ):
                v.tensor_copy(pers["LA"][:, y, :].rearrange("p (j i) -> p j i", i=32)[:, :, HC + y:HC + y + WIN],
                              G[:, 0:4, :])
            for c in range(16):
                dst = pers["LB"][:, c, :].rearrange("p (j i) -> p j i", i=32)
                n = min(WIN, 16 - c)
                v.tensor_copy(dst[:, :, HC + c:HC + c + n], G[:, 4:8, 0:n])
                if n < WIN:
                    v.tensor_copy(dst[:, :, HC:HC + WIN - n], G[:, 4:8, n:WIN])
            for b in range(B):
                v.wait_ge(x_in[b], 16)
                for k in range(8):
                    ch.then(v.bn_stats(st[:, b, k, :], xs[:, b, 512 * k:512 * k + 512]))
                ch.wait()
                ch.then(v.bn_aggr(mv[:, b, :], st[:, b, :, :]))
            ch.wait()
            v.tensor_copy(gm[:], mv[:, :, 0]).then_inc(mean_ready, 1)
            v.wait_ge(gstat, 1)
            ch.link(v.tensor_copy(gm[:], psT[:, 3, 0:B]))
            ch.link(v.tensor_tensor(ra[:], mv[:, :, 0], gm[:], ALU.subtract))
            ch.link(v.tensor_tensor(rs[:], ra[:], ra[:], ALU.mult))
            v.tensor_tensor(dd[:], rs[:], mv[:, :, 1], ALU.add).then_inc(sq_ready, 1)
            v.wait_ge(gstat, 2)
            ch.link(v.tensor_scalar(var[:], psT[:, 3, 8:8 + B], 1e-5, None, ALU.add))
            rsqrt(v, ch, rs[:], var[:], ra[:])
            for b in range(B):
                if b < 2:
                    v.wait_ge(consts, 2)
                else:
                    v.wait_ge(stored[b % 2], 16 * (STRIPS + 1) * (b // 2))
                v.tensor_scalar(xpad[b % 2][:, PAD:PAD + HH, PAD:PAD + WW],
                                xs[:, b, :].rearrange("p (h w) -> p h w", w=WW), gm[:, b:b + 1], rs[:, b:b + 1],
                                ALU.subtract, ALU.mult).then_inc(pad_ready, 1)


def rsqrt(v, ch, y, x, tmp):
    ch.link(v.tensor_scalar(tmp.bitcast(I32), x.bitcast(I32), 1, None, ALU.arith_shift_right))
    ch.link(v.tensor_scalar(y.bitcast(I32), tmp.bitcast(I32), -1, 0x5F3759DF, ALU.mult, ALU.add))
    ch.link(v.tensor_scalar(x, x, -0.5, None, ALU.mult))
    for _ in range(4):
        ch.link(v.tensor_tensor(tmp, y, y, ALU.mult))
        ch.link(v.tensor_tensor(tmp, tmp, x, ALU.mult))
        ch.link(v.scalar_tensor_tensor(out=y, in0=tmp, scalar=1.5, in1=y, op0=ALU.add, op1=ALU.mult))


def load_token_weights(nc, tok, theta, w1, b1, w2, b2, g1, be1, g2, be2, ident):
    with ExitStack() as ctx:
        w1_in = ctx.enter_context(nc.sbuf_tensor("tw_w1", [P, FT, NQB], F32))
        w2_in = ctx.enter_context(nc.sbuf_tensor("tw_w2", [P, FT, P], F32))
        th = ctx.enter_context(nc.sbuf_tensor("tw_th", [P, NQB], F32))
        ps = [ctx.enter_context(nc.psum_tensor(f"tw_ps{n}", [P, 4, P], F32)) for n in range(8)]
        rows_in, w_in, w1t, w2t, done = (ctx.enter_context(nc.semaphore("tw_" + n))
                                         for n in ("rows_in", "w_in", "w1t", "w2t", "done"))
        block = ctx.enter_context(nc.Block())

        @block.sync
        def _(sp):
            sp.dma_start(w1_in[:], w1.rearrange("(k p) q -> p k q", p=P)).then_inc(w_in, 16)
            sp.dma_start(w2_in[:], w2.rearrange("e (k f) -> e k f", f=P)).then_inc(w_in, 16)
            sp.dma_start(tok["w1b"][NQB:NQB + 1, :], b1.rearrange("(a f) -> a f", a=1)).then_inc(rows_in, 16)
            sp.dma_start(th[:], theta.partition_broadcast(P)).then_inc(rows_in, 16)
            for name, row in (("b2", b2), ("g1", g1), ("be1", be1), ("g2", g2), ("be2", be2)):
                sp.dma_start(tok[name][:], row.partition_broadcast(P)).then_inc(rows_in, 16)
            sp.wait_ge(rows_in, 16 * 7)

        @block.tensor
        def _(pe):
            pe.wait_ge(w_in, 32)
            for k in range(FT):
                mm = pe.transpose(ps[k // 4][0:NQB, k % 4, :], w1_in[:, k, :], ident[:])
            mm.then_inc(w1t, 1)
            for k in range(FT):
                mm = pe.transpose(ps[4 + k // 4][:, k % 4, :], w2_in[:, k, :], ident[:])
            mm.then_inc(w2t, 1)

        @block.vector
        def _(v):
            v.wait_ge(w1t, 1)
            for n in range(4):
                v.tensor_copy(tok["w1b"][0:NQB, 512 * n:512 * n + 512].rearrange("p (k f) -> p k f", f=P),
                              ps[n][0:NQB, :, :])
            v.wait_ge(w2t, 1)
            for n in range(4):
                v.tensor_copy(tok["w2T"][:, 4 * n:4 * n + 4, :], ps[4 + n][:]).then_inc(done, 1)
            v.memset(tok["qT"][:], 1.0).then_inc(done, 1)
            v.wait_ge(rows_in, 16 * 7)
            v.tensor_copy(tok["theta"][:].rearrange("p (g j) -> p g j", j=NQB),
                          th[:].unsqueeze(1).to_broadcast([P, QH, NQB])).then_inc(done, 1)
            v.wait_ge(done, 6)


ATT_LINKS, MID_LINKS, FIN_LINKS = 4, 78, 59


def strips(nc, pers, tok, xn_strips, u_dram, t_dram):
    with ExitStack() as ctx:
        def sb(name, shape, dt=F32):
            return ctx.enter_context(nc.sbuf_tensor(name, shape, dt))

        def sem(name):
            return ctx.enter_context(nc.semaphore(name))

        NX = KROWS * KCOLS
        strip = sb("st_strip", [P, NX + STOK])
        xn3 = strip[:, 0:NX].rearrange("p (h w) -> p h w", w=KCOLS)
        xw = strip[:, NX:].rearrange("p (y r x) -> p r y x", y=ROWS, r=2 * NPAIR)
        xwin = sb("st_xwin", [P, 2 * NPAIR, KEYS])
        xpatch = sb("st_xpatch", [P, 2 * NPAIR, PQ * PQ])
        K = [sb(f"st_K{s}", [P, KROWS, KCOLS]) for s in range(2)]
        Q = [sb(f"st_Q{s}", [P, 2 * NPAIR, PQ * PQ]) for s in range(2)]
        V = sb("st_V", [HALF, 2 * 2 * NPAIR, P])
        Sm = [sb(f"st_Sm{s}", [P, 4, KEYS]) for s in range(2)]
        Pr = [sb(f"st_Pr{s}", [P, 4, KEYS]) for s in range(2)]
        nmax = [sb(f"st_nmax{s}", [P, 4]) for s in range(2)]
        den = [sb(f"st_den{s}", [P, HEADS]) for s in range(2)]
        rden = sb("st_rden", [P, HEADS])
        PT = [sb(f"st_PT{s}", [HALF, 8, P]) for s in range(2)]
        xt = sb("st_xt", [P, NPAIR, P])
        at = sb("st_at", [P, P])
        t0, t0m, t0f = (sb("st_" + n, [P, NPAIR, P]) for n in ("t0", "t0m", "t0f"))
        n0, arg, turns, c, x1, x1b = (sb("st_" + n, [P, NPAIR, P]) for n in ("n0", "arg", "turns", "c", "x1", "x1b"))
        y, tt_sb = sb("st_y", [P, NPAIR, P]), sb("st_tt", [P, STOK])
        tfin = sb("st_tfin", [P, NPAIR, P])
        uhl = sb("st_uhl", [P, NPAIR, 2, P], F16)
        stm, stf = sb("st_stm", [P, NPAIR, 6]), sb("st_stf", [P, NPAIR, 6])
        mvm, mvf = sb("st_mvm", [P, NPAIR, 2]), sb("st_mvf", [P, NPAIR, 2])
        vm, vf = sb("st_vm", [P, 3, NPAIR]), sb("st_vf", [P, 3, NPAIR])
        fq = sb("st_fq", [P, 4, NPAIR, NQB])
        cell, one_cell = sb("st_cell", [P, 1]), sb("st_one", [P, 1])
        h = sb("st_h", [P, FT, STOK])
        psS = [ctx.enter_context(nc.psum_tensor(f"st_psS{n}", [P, 512], F32)) for n in range(4)]
        psT = [ctx.enter_context(nc.psum_tensor(f"st_psT{n}", [P, 512], F32)) for n in range(2)]
        psO = ctx.enter_context(nc.psum_tensor("st_psO", [P, 512], F32))
        psM = ctx.enter_context(nc.psum_tensor("st_psM", [P, 512], F32))
        hbank = [psS[0], psS[1], psS[2], psS[3], psT[0], psT[1]]

        names = ("one win_ready strip_in k_ready q_ready v_ready xt_ready k_copied q_copied v_copied xt_copied "
                 "scores_ready scores_read probs_ready pt_ready pt_act pt_dve pv_done out_read t0_ready "
                 "t0_kept mid_read sin_in sin_out qf_ready qt_ready qt_copied h_ready relu_act relu_dve "
                 "ffn_done ffn_read t_ready tt_ready tt_copied tt_stored u_ready u_stored t0f_kept "
                 "ach mch fch").split()
        S = {n: sem("st_" + n) for n in names}

        def wait(eng, name, value):
            if not (isinstance(value, int) and value <= 0):
                eng.wait_ge(S[name], value)

        def gate(v, sem_, value):
            if not (isinstance(value, int) and value <= 0):
                v.wait_ge(sem_, value)
            if not isinstance(value, int):
                v.memset(cell[:], 0.0)

        def pool_copy(pool, out, in_):
            one = one_cell[:] if len(in_.shape) == 2 else one_cell[:].unsqueeze(1)
            return pool.tensor_tensor(out, in_, one.to_broadcast(list(in_.shape)), ALU.mult)

        def sp_load(sp, i):
            wait(sp, "q_ready", 2 * i)
            wait(sp, "win_ready", 1 * i)
            sp.dma_start(strip[:], xn_strips[bass.ds(i, 1)].rearrange("a c n -> (a c) n")).then_inc(S["strip_in"], 16)

        def sp_store(sp, i):
            sp.wait_ge(S["u_ready"], i + 1)
            for r in range(NPAIR):
                for q in range(2):
                    dst = u_dram[bass.ds(i, 1)].rearrange("a (y r q x) n -> (a r) q y x n", y=ROWS, r=NPAIR, q=2)
                    sp.dma_start(dst[r, q], uhl[64 * q:64 * q + 64, r].rearrange("p a b -> p (a b)"))\
                        .then_inc(S["u_stored"], 16)
            sp.wait_ge(S["tt_copied"], i + 1)
            sp.dma_start(t_dram[bass.ds(i, 1)].rearrange("a c n -> (a c) n"),
                         tt_sb[:]).then_inc(S["tt_stored"], 16)

        def pe_project(pe, i):
            pe.wait_ge(S["strip_in"], 16 * (i + 1))
            wait(pe, "scores_read", 8 * i)
            flat = strip[:, 0:NX]
            for s in range(2):
                for n in range(2):
                    mm = pe.matmul(psS[2 * s + n][:, 0:NX // 2], pers["wk"][:, s, :],
                                   flat[:, n * NX // 2:(n + 1) * NX // 2], start=True, stop=True)
                mm.then_inc(S["k_ready"], 1)
            wait(pe, "pt_act", 8 * i)
            for y_ in range(ROWS):
                mm = pe.matmul(psT[0][:, 64 * y_:64 * y_ + 64], pers["LA"][:, y_, :],
                               xn3[:, PAD + y_, PAD:PAD + WW], start=True, stop=True)
            mm.then_inc(S["q_ready"], 1)
            wait(pe, "pt_dve", 8 * i)
            qb = psT[1][:].rearrange("p (y a m) -> p m y a", y=ROWS, m=16)
            for m in range(16):
                mm = pe.matmul(qb[:, m], pers["LB"][:, m, :], xn3[:, PAD:PAD + ROWS, PAD + m:PAD + m + 49:16],
                               start=True, stop=True)
            mm.then_inc(S["q_ready"], 1)
            for w in range(2 * 2 * NPAIR):
                p, hf = w // 2, w % 2
                if w == 0:
                    pe.wait_ge(S["win_ready"], i + 1)
                if w % 4 == 0:
                    pe.wait_ge(S["k_copied"], 2 * i + 1 + (w >= 8))
                mm = pe.matmul(psS[w // 4][0:HALF, (w % 4) * P:(w % 4 + 1) * P],
                               xwin[:, p, HALF * hf:HALF * hf + HALF], pers["wv"][:], start=True, stop=True)
                if w % 4 == 3:
                    mm.then_inc(S["v_ready"], 1)
            wait(pe, "qt_copied", i - 1)
            for r in range(NPAIR):
                mm = pe.transpose(psM[:, r * P:(r + 1) * P], xpatch[:, 2 * r:2 * r + 2, :].rearrange("p q n -> p (q n)"),
                                  pers["ident"][:])
            mm.then_inc(S["xt_ready"], 1)

        def pe_scores(pe, i, u):
            r, s = u // 2, u % 2
            if u == 0:
                pe.wait_ge(S["q_copied"], 2 * (i + 1))
                pe.wait_ge(S["v_copied"], 4 * (i + 1))
            else:
                pe.wait_ge(S["scores_read"], 8 * i + u)
            for q in range(2):
                col = PQ * (2 * r + q)
                for j in range(4):
                    mm = pe.matmul(psS[j][64 * q:64 * q + 64, 0:KEYS],
                                   Q[s][32 * j:32 * j + 32, 2 * r + q, :], K[s][32 * j:32 * j + 32, :, col:col + PK],
                                   start=True, stop=True)
            mm.then_inc(S["scores_ready"], 1)

        def pe_turn(pe, i, u):
            pe.wait_ge(S["probs_ready"], 8 * i + u + 1)
            if u:
                pe.wait_ge(S["pt_act"], 8 * i + u)
                pe.wait_ge(S["pt_dve"], 8 * i + u)
            for j in range(4):
                for hf in range(2):
                    mm = pe.transpose(psT[j // 2][0:HALF, (2 * (j % 2) + hf) * P:(2 * (j % 2) + hf + 1) * P],
                                      Pr[u % 2][:, j, HALF * hf:HALF * hf + HALF], pers["ident"][:])
            mm.then_inc(S["pt_ready"], 1)

        def pe_values(pe, i, u):
            r, s = u // 2, u % 2
            pe.wait_ge(S["pt_act"], 8 * i + u + 1)
            pe.wait_ge(S["pt_dve"], 8 * i + u + 1)
            if s == 0:
                wait(pe, "out_read", 4 * i + r)
                if r == 0:
                    wait(pe, "ffn_read", i - 1)
            for j in range(4):
                g = 4 * s + j
                for q in range(2):
                    for hf in range(2):
                        mm = pe.matmul(psO[64 * q:64 * q + 64, HC * g:HC * g + HC],
                                       PT[s][:, 2 * j + hf, 64 * q:64 * q + 64],
                                       V[:, 2 * (2 * r + q) + hf, HC * g:HC * g + HC],
                                       start=(hf == 0), stop=(hf == 1))
            mm.then_inc(S["pv_done"], 1)

        def pe_back(pe, i, k):
            pe.wait_ge(S["t_ready"], k + 1)
            wait(pe, "xt_copied", i + 1)
            pe.wait_ge(S["qt_copied"], k + 1)
            for r in range(NPAIR):
                mm = pe.transpose(psM[:, r * P:(r + 1) * P], tfin[:, r, :], pers["ident"][:])
            mm.then_inc(S["tt_ready"], 1)

        def pe_ffn(pe, i, k):
            pe.wait_ge(S["qf_ready"], k + 1)
            wait(pe, "xt_copied", i + 1)
            wait(pe, "tt_copied", k)
            for r in range(NPAIR):
                mm = pe.transpose(psM[0:NQB, r * P:(r + 1) * P], fq[:, 3, r, :], pers["ident"][:])
            mm.then_inc(S["qt_ready"], 1)
            pe.wait_ge(S["qt_copied"], k + 1)

            def hidden(f):
                if f < 4:
                    wait(pe, "scores_read", 8 * (i + 1))
                elif f < 6:
                    wait(pe, "pt_act", 8 * (i + 1))
                    wait(pe, "pt_dve", 8 * (i + 1))
                else:
                    pe.wait_ge(S["relu_dve" if f % 2 else "relu_act"], 8 * k + (f - 6) // 2 + 1)
                pe.matmul(hbank[f % 6][:], tok["w1b"][:, P * f:P * f + P], tok["qT"][:], start=True, stop=True)\
                    .then_inc(S["h_ready"], 1)

            def output(f):
                if f == 0:
                    wait(pe, "out_read", 4 * (i + 1))
                    wait(pe, "ffn_read", k)
                pe.wait_ge(S["relu_dve" if f % 2 else "relu_act"], 8 * k + f // 2 + 1)
                for r in range(NPAIR):
                    mm = pe.matmul(psO[:, r * P:(r + 1) * P], h[:, f, r * P:(r + 1) * P], tok["w2T"][:, f, :],
                                   start=(f == 0 and r == 0), stop=(f == FT - 1), skip_group_check=True)
                return mm

            for f in range(FT + 4):
                if f < FT:
                    hidden(f)
                if f >= 4:
                    mm = output(f - 4)
            mm.then_inc(S["ffn_done"], 1)

        def pe_step(pe, i, att=True, mid=True, fin=True):
            if att:
                pe_project(pe, i)
            for u in range(10):
                if att and u < 8:
                    pe_scores(pe, i, u)
                if att and 1 <= u <= 8:
                    pe_turn(pe, i, u - 1)
                if att and u >= 2:
                    pe_values(pe, i, u - 2)
                if fin and u == 2:
                    pe_back(pe, i if att else NSTRIP - 1, i - 2)
            if mid:
                pe_ffn(pe, i if att else NSTRIP - 1, i - 1)

        def act_copies(act, i):
            for n in range(2):
                act.wait_ge(S["q_ready"], 2 * i + n + 1)
                wait(act, "scores_ready", 8 * i)
                act.copy(Q[n][:].rearrange("p r (y x) -> p r y x", x=PQ),
                         psT[n][:].rearrange("p (y r x) -> p r y x", y=ROWS, x=PQ)).then_inc(S["q_copied"], 1)
            wait(act, "pv_done", 8 * i)
            for n in range(4):
                act.wait_ge(S["v_ready"], 4 * i + n + 1)
                act.copy(V[:, 4 * n:4 * n + 4, :].rearrange("p w c -> p (w c)"), psS[n][0:HALF, :])\
                    .then_inc(S["v_copied"], 1)
            act.wait_ge(S["xt_ready"], i + 1)
            wait(act, "t0_ready", 4 * i)
            act.copy(xt[:].rearrange("p r c -> p (r c)"), psM[:]).then_inc(S["xt_copied"], 1)

        def act_exp(act, i, u):
            r, s = u // 2, u % 2
            act.wait_ge(S["scores_read"], 8 * i + u + 1)
            wait(act, "pt_ready", 8 * i + u - 1)
            if s == 0:
                wait(act, "out_read", 4 * i + r - 1)
            for j in range(4):
                ins = act.activation(Pr[s][:, j, :], Sm[s][:, j, :], ACT.Exp, scale=-1.0, bias=nmax[s][:, j:j + 1],
                                     accum_out=den[r % 2][:, 4 * s + j:4 * s + j + 1])
            ins.then_inc(S["probs_ready"], 1)

        def act_pt(act, i, u):
            act.wait_ge(S["pt_ready"], 8 * i + u + 1)
            wait(act, "pv_done", 8 * i + u - 1)
            act.copy(PT[u % 2][:, 0:4, :].rearrange("p w c -> p (w c)"), psT[0][0:HALF, :]).then_inc(S["pt_act"], 1)

        def act_sin(act, k, n):
            act.wait_ge(S["sin_in"], 2 * k + n + 1)
            if n == 0:
                act.activation(c[:], arg[:], ACT.Sin, bias=pers["halfpi"][:, 0:1]).then_inc(S["sin_out"], 1)
            else:
                act.activation(fq[:, 2], fq[:, 1], ACT.Sin, bias=pers["halfpi"][:, 0:1]).then_inc(S["sin_out"], 1)

        def act_tt(act, k):
            act.wait_ge(S["tt_ready"], k + 1)
            wait(act, "tt_stored", 16 * k)
            act.copy(tt_sb[:].rearrange("p (y r x) -> p r y x", y=ROWS, x=PQ),
                     psM[:].rearrange("p (r y x) -> p r y x", y=PQ, x=PQ)).then_inc(S["tt_copied"], 1)

        def act_step(act, i, att=True, mid=True, fin=True):
            if att:
                act_copies(act, i)
            for u in range(9):
                if att and u < 8:
                    act_exp(act, i, u)
                if att and u >= 1:
                    act_pt(act, i, u - 1)
                if mid and u == 2:
                    act_sin(act, i - 1, 0)
                if mid and u == 5:
                    act_sin(act, i - 1, 1)
                if fin and u == 3:
                    act_tt(act, i - 2)
            if mid:
                k = i - 1
                for f in range(0, FT, 2):
                    act.wait_ge(S["h_ready"], FT * k + f + 1)
                    if f == 0:
                        wait(act, "ffn_done", k)
                    act.activation(h[:, f, :], hbank[f % 6][:], ACT.Relu).then_inc(S["relu_act"], 1)

        def layer_norm(v, ch, src, dst, st, mv, vv):
            for r in range(NPAIR):
                ch.then(v.bn_stats(st[:, r, :], src[:, r, :]))
            gate(v, ch.sem, ch.base + ch.n)
            for r in range(NPAIR):
                ch.then(v.bn_aggr(mv[:, r, :], st[:, r, :].rearrange("p (a s) -> p a s", a=1)))
            ch.wait()
            ch.link(v.tensor_scalar(vv[:, 0, :], mv[:, :, 1], 1e-5, None, ALU.add))
            rsqrt(v, ch, vv[:, 1, :], vv[:, 0, :], vv[:, 2, :])
            for r in range(NPAIR):
                ch.then(v.tensor_scalar(dst[:, r, :], src[:, r, :], mv[:, r, 0:1], vv[:, 1, r:r + 1],
                                        ALU.subtract, ALU.mult))
            ch.wait()

        def whole_turns(v, ch, src, turns_, dst):
            ch.link(v.tensor_scalar(turns_, src, 1.0 / TWO_PI, 0.25, ALU.mult, ALU.add))
            ch.link(v.tensor_scalar(turns_, turns_, MAGIC, MAGIC, ALU.add, ALU.subtract))
            ch.link(v.scalar_tensor_tensor(out=src, in0=turns_, scalar=-TP1, in1=src, op0=ALU.mult, op1=ALU.add))
            ch.link(v.scalar_tensor_tensor(out=src, in0=turns_, scalar=-TP2, in1=src, op0=ALU.mult, op1=ALU.add))
            return v.tensor_scalar(dst, src, SIN_LO, SIN_HI, ALU.max, ALU.min)

        def rows(name):
            return tok[name][:].unsqueeze(1).to_broadcast([P, NPAIR, P])

        def flat(t):
            return t[:].rearrange("p r c -> p (r c)")

        def dve_keys(v, i):
            wait(v, "scores_ready", 8 * i)
            for s in range(2):
                v.wait_ge(S["k_ready"], 2 * i + s + 1)
                kf, hot = K[s][:].rearrange("p h w -> p (h w)"), pers["hot" + "AB"[s]][:].rearrange("p h w -> p (h w)")
                for n in range(2):
                    a, b = n * NX // 2, (n + 1) * NX // 2
                    ins = v.tensor_tensor(kf[:, a:b], psS[2 * s + n][:, 0:NX // 2], hot[:, a:b], ALU.add)
                ins.then_inc(S["k_copied"], 1)

        def dve_max(v, i, u):
            s = u % 2
            wait(v, "probs_ready", 8 * i + u - 1)
            gate(v, S["scores_ready"], 8 * i + u + 1)
            for j in range(4):
                ins = v.tensor_tensor_reduce(Sm[s][:, j, :], psS[j][:, 0:KEYS],
                                             pers["mask"][:], -1.0, 3.0e38, ALU.add, ALU.min, nmax[s][:, j:j + 1])
            ins.then_inc(S["scores_read"], 1)

        def dve_pt(v, i, u):
            v.wait_ge(S["pt_ready"], 8 * i + u + 1)
            wait(v, "pv_done", 8 * i + u - 1)
            v.tensor_copy(PT[u % 2][:, 4:8, :].rearrange("p w c -> p (w c)"), psT[1][0:HALF, :]).then_inc(S["pt_dve"], 1)

        def dve_out(v, ch, i, r):
            ch.link(v.reciprocal(rden[:], den[r % 2][:]))
            v.wait_ge(S["pv_done"], 8 * i + 2 * r + 2)
            v.tensor_tensor(at[:].rearrange("p (g c) -> p g c", c=HC), psO[:, 0:P].rearrange("p (g c) -> p g c", c=HC),
                            rden[:].unsqueeze(2).to_broadcast([P, HEADS, HC]), ALU.mult).then_inc(S["out_read"], 1)
            v.wait_ge(S["out_read"], 4 * i + r + 1)
            if r == 0:
                v.wait_ge(S["xt_copied"], i + 1)
                wait(v, "t0_kept", i)
            v.tensor_tensor(t0[:, r, :], at[:], xt[:, r, :], ALU.add).then_inc(S["t0_ready"], 1)

        def dve_mid1(v, ch, k):
            v.wait_ge(S["t0_kept"], k + 1)
            layer_norm(v, ch, t0m, n0, stm, mvm, vm)
            ch.link(v.tensor_tensor(turns[:], n0[:], rows("theta"), ALU.add))
            whole_turns(v, ch, turns[:], c[:], arg[:]).then_inc(S["sin_in"], 1)

        def dve_mid2(v, ch, k):
            v.wait_ge(S["sin_out"], 2 * k + 1)
            c8, n8 = c[:].rearrange("p r (g j) -> p (r g) j", j=NQB), n0[:].rearrange("p r (g j) -> p (r g) j", j=NQB)
            s8 = arg[:].rearrange("p r (g j) -> p (r g) j", j=NQB)
            for j in range(1, NQB):
                ch.link(v.tensor_tensor(c8[:, :, j], c8[:, :, j - 1], c8[:, :, j], ALU.mult))
            ch.then(v.tensor_tensor(s8[:, :, 1:], n8[:, :, 1:], c8[:, :, 1:], ALU.add))
            ch.link(v.tensor_tensor(s8[:, :, 0], n8[:, :, 0], c8[:, :, NQB - 1], ALU.add))
            layer_norm(v, ch, arg, x1, stm, mvm, vm)
            ch.link(v.tensor_tensor(x1[:], x1[:], rows("g1"), ALU.mult))
            ch.link(v.tensor_tensor(x1[:], x1[:], rows("be1"), ALU.add))
            ch.link(v.tensor_copy(fq[:, 0], x1[:, :, 0:NQB]))
            whole_turns(v, ch, fq[:, 0], fq[:, 2], fq[:, 1]).then_inc(S["sin_in"], 1)

        def dve_mid3(v, ch, k):
            ch.link(v.tensor_tensor(x1b[:], x1[:], rows("b2"), ALU.add))
            v.wait_ge(S["sin_out"], 2 * k + 2)
            wait(v, "qt_ready", k)
            v.tensor_tensor(fq[:, 3], fq[:, 2], pers["cosphi"][:].unsqueeze(1).to_broadcast([P, NPAIR, NQB]),
                            ALU.mult).then_inc(S["qf_ready"], 1)

        def dve_ffn(v, k):
            v.wait_ge(S["qt_ready"], k + 1)
            wait(v, "ffn_done", k)
            v.tensor_copy(tok["qT"][0:NQB, :], psM[0:NQB, :]).then_inc(S["qt_copied"], 1)
            for f in range(1, FT, 2):
                v.wait_ge(S["h_ready"], FT * k + f + 1)
                v.tensor_scalar(h[:, f, :], hbank[f % 6][:], 0.0, None, ALU.max).then_inc(S["relu_dve"], 1)

        def dve_fin1(v, ch, k):
            v.wait_ge(S["ffn_done"], k + 1)
            v.tensor_tensor(flat(y), psO[:], flat(x1b), ALU.add).then_inc(S["ffn_read"], 1)
            v.wait_ge(S["ffn_read"], k + 1)
            layer_norm(v, ch, y, y, stf, mvf, vf)
            ch.link(v.tensor_tensor(y[:], y[:], rows("g2"), ALU.mult))
            ch.link(v.tensor_tensor(y[:], y[:], rows("be2"), ALU.add))
            v.wait_ge(S["t0f_kept"], k + 1)
            wait(v, "tt_ready", k)
            v.tensor_tensor(tfin[:], y[:], t0f[:], ALU.add).then_inc(S["t_ready"], 1)

        def dve_fin2(v, ch, k):
            v.wait_ge(S["t_ready"], k + 1)
            layer_norm(v, ch, tfin, y, stf, mvf, vf)
            wait(v, "u_stored", 16 * 2 * NPAIR * k)
            ch.link(v.tensor_scalar(uhl[:, :, 0, :], y[:], U_SCALE, None, ALU.mult))
            v.scalar_tensor_tensor(out=uhl[:, :, 1, :], in0=y[:], scalar=U_SCALE, in1=uhl[:, :, 0, :],
                                   op0=ALU.mult, op1=ALU.subtract).then_inc(S["u_ready"], 1)

        def dve_step(v, i, att=True, mid=True, fin=True):
            ach = Chain(v, S["ach"], ATT_LINKS * i)
            mch = Chain(v, S["mch"], MID_LINKS * (i - 1))
            fch = Chain(v, S["fch"], FIN_LINKS * (i - 2))
            if att:
                dve_keys(v, i)
            if fin:
                dve_fin1(v, fch, i - 2)
            for u in range(10):
                if att and u < 8:
                    dve_max(v, i, u)
                if att and 1 <= u <= 8:
                    dve_pt(v, i, u - 1)
                if att and u >= 3 and u % 2 == 1:
                    dve_out(v, ach, i, (u - 3) // 2)
                if fin and u == 0:
                    dve_fin2(v, fch, i - 2)
                if mid and u == 1:
                    dve_mid1(v, mch, i - 1)
                if mid and u == 3:
                    dve_mid2(v, mch, i - 1)
                if mid and u == 5:
                    dve_mid3(v, mch, i - 1)
            if mid:
                dve_ffn(v, i - 1)
            assert (not att or ach.n == ATT_LINKS) and (not mid or mch.n == MID_LINKS) and \
                (not fin or fch.n == FIN_LINKS), (ach.n, mch.n, fch.n)

        def pool_windows(pool, i):
            wait(pool, "v_ready", 4 * i)
            wait(pool, "xt_ready", 1 * i)
            pool.wait_ge(S["strip_in"], 16 * (i + 1))
            for p in range(2 * NPAIR):
                copy = pool.tensor_copy if p else lambda out, in_: pool_copy(pool, out, in_)
                copy(xwin[:, p, :].rearrange("p (a b) -> p a b", a=PK), xn3[:, :, PQ * p:PQ * p + PK])
            pool.tensor_copy(xpatch[:].rearrange("p r (y x) -> p r y x", x=PQ), xw).then_inc(S["win_ready"], 1)

        def pool_step(pool, i, att=True, mid=True, fin=True):
            if att:
                pool_windows(pool, i)
            if fin:
                wait(pool, "t_ready", i - 2)
                pool.wait_ge(S["t0_kept"], i - 1)
                pool_copy(pool, t0f[:], t0m[:]).then_inc(S["t0f_kept"], 1)
                pool.wait_ge(S["t0f_kept"], i - 1)
            if mid:
                wait(pool, "sin_in", 2 * (i - 1))
                pool.wait_ge(S["t0_ready"], 4 * i)
                pool_copy(pool, t0m[:], t0[:]).then_inc(S["t0_kept"], 1)

        block = ctx.enter_context(nc.Block())

        @block.sync
        def _(sp):
            sp_load(sp, 0)
            sp_load(sp, 1)
            sp_load(sp, 2)
            with sp.Fori(2, NSTRIP - 1) as i:
                sp_load(sp, i + 1)
                sp_store(sp, i - 2)
            for k in range(NSTRIP - 3, NSTRIP):
                sp_store(sp, k)
            sp.wait_ge(S["u_stored"], 16 * 2 * NPAIR * NSTRIP)
            sp.wait_ge(S["tt_stored"], 16 * NSTRIP)

        @block.tensor
        def _(pe):
            pe_step(pe, 0, mid=False, fin=False)
            pe_step(pe, 1, fin=False)
            with pe.Fori(2, NSTRIP) as i:
                pe_step(pe, i)
            pe_step(pe, NSTRIP, att=False)
            pe_step(pe, NSTRIP + 1, att=False, mid=False)

        @block.scalar
        def _(act):
            act_step(act, 0, mid=False, fin=False)
            act_step(act, 1, fin=False)
            with act.Fori(2, NSTRIP) as i:
                act_step(act, i)
            act_step(act, NSTRIP, att=False)
            act_step(act, NSTRIP + 1, att=False, mid=False)

        @block.vector
        def _(v):
            dve_step(v, 0, mid=False, fin=False)
            dve_step(v, 1, fin=False)
            with v.Fori(2, NSTRIP) as i:
                dve_step(v, i)
            dve_step(v, NSTRIP, att=False)
            dve_step(v, NSTRIP + 1, att=False, mid=False)

        @block.gpsimd
        def _(pool):
            pool.memset(one_cell[:], 1.0).then_inc(S["one"], 1)
            pool.wait_ge(S["one"], 1)
            pool_step(pool, 0, mid=False, fin=False)
            pool_step(pool, 1, fin=False)
            with pool.Fori(2, NSTRIP) as i:
                pool_step(pool, i)
            pool_step(pool, NSTRIP, att=False)
            pool_step(pool, NSTRIP + 1, att=False, mid=False)


KF = 16
LAGS = 3
NMAT = LAGS + 2 * KF
PH = T // 2
BLK = PH // P
CH = 512
NCH = PH // CH
FRONT = 130
FLEN = FRONT + PH
F_SCALE = 1024.0
M_SCALE = 1024.0
TINY = 1.0e-30
NV = 4


def spectral_prepare(nc, ident, phi, sigma, m_u, m_plus, m_minus, log_weights, gumbel, filt, mats, mgain):
    with ExitStack() as ctx:
        def sb(name, shape, dt=F32):
            return ctx.enter_context(nc.sbuf_tensor("sp_" + name, shape, dt))

        phi_in = sb("phi", [P, T // P, KF])
        phiT = sb("phiT", [KF, T])
        fhl = sb("fhl", [KF, 2, 2, FLEN], F16)
        sig, pmax, inv, al, tm = (sb(n, [KF, 1]) for n in ("sig", "pmax", "inv", "al", "tm"))
        diag = sb("diag", [KF, KF])
        ones = sb("ones", [P, P])
        alpha = sb("alpha", [P, KF])
        zz = sb("zz", [P, 2, NV])
        z, e, ysoft, eq, cum, hard, wts = (sb(n, [P, NV]) for n in ("z", "e", "ysoft", "eq", "cum", "hard", "wts"))
        zs = sb("zs", [P, 4])
        pp = [sb(f"pp{n}", [P, 2, KF, P]) for n in range(2)]
        mu = [sb(f"mu{n}", [P, LAGS, P]) for n in range(2)]
        acc = sb("acc", [P, 2, KF, P])
        accu = sb("accu", [P, LAGS, P])
        mix = sb("mix", [P, NMAT, P])
        mhl = sb("mhl", [P, NMAT, 2, P], F16)
        mx = sb("mx", [P, 4])
        mrow = sb("mrow", [1, 2])
        ps = [ctx.enter_context(nc.psum_tensor(f"sp_ps{n}", [P, 512], F32)) for n in range(8)]
        names = "phi_in row_in phit filt_ready diag_ready alpha_ps z_ready e_ready mx_ready mxt mrow_ready gmax mhl_ready stored vch".split()
        S = {n: ctx.enter_context(nc.semaphore("sp_" + n)) for n in names}
        m_in = [ctx.enter_context(nc.semaphore(f"sp_m_in{n}")) for n in range(2)]
        block = ctx.enter_context(nc.Block())

        @block.sync
        def _(sp):
            sp.dma_start(phi_in[:], phi.rearrange("(n p) k -> p n k", p=P)).then_inc(S["phi_in"], 16)
            sp.dma_start(sig[:], sigma.rearrange("(k a) -> k a", a=1)).then_inc(S["row_in"], 16)
            sp.dma_start(zz[:, 0, :], log_weights.partition_broadcast(P)).then_inc(S["row_in"], 16)
            sp.dma_start(zz[:, 1, :], gumbel.partition_broadcast(P)).then_inc(S["row_in"], 16)

            def load(n):
                sp.dma_start(pp[n % 2][:, 0], m_plus[n].rearrange("k d e -> d k e")).then_inc(m_in[n % 2], 16)
                sp.dma_start(pp[n % 2][:, 1], m_minus[n].rearrange("k d e -> d k e")).then_inc(m_in[n % 2], 16)
                sp.dma_start(mu[n % 2][:], m_u[n].rearrange("k d e -> d k e")).then_inc(m_in[n % 2], 16)

            load(0)
            load(1)
            sp.wait_ge(S["filt_ready"], 1)
            sp.dma_start(filt.rearrange("k h r n -> k (h r n)"), fhl[:].rearrange("k h r n -> k (h r n)"))\
                .then_inc(S["stored"], 16)
            for n in range(NV):
                sp.wait_ge(S["mhl_ready"], n + 1)
                sp.dma_start(mats[n], mhl[:].rearrange("d m h e -> d (m h e)")).then_inc(S["stored"], 16)
                if n + 2 < NV:
                    load(n + 2)
            sp.wait_ge(S["stored"], 16 * (NV + 1))

        @block.tensor
        def _(pe):
            pe.wait_ge(S["phi_in"], 16)
            for n in range(T // P):
                mm = pe.transpose(ps[n // 4][0:KF, (n % 4) * P:(n % 4 + 1) * P], phi_in[:, n, :], ident[:])
            mm.then_inc(S["phit"], 1)
            pe.wait_ge(S["diag_ready"], 1)
            pe.matmul(ps[0][:, 0:KF], ones[0:KF, :], diag[:], start=True, stop=True).then_inc(S["alpha_ps"], 1)
            for n in range(NV):
                pe.wait_ge(S["mx_ready"], n + 1)
                pe.transpose(ps[1][0:1, 0:P], mx[:, 0:1], ident[:]).then_inc(S["mxt"], 1)
                pe.wait_ge(S["mrow_ready"], n + 1)
                pe.matmul(ps[2][:, 0:1], ones[0:1, :], mrow[0:1, 0:1], start=True, stop=True).then_inc(S["gmax"], 1)

        @block.scalar
        def _(act):
            act.wait_ge(S["z_ready"], 1)
            act.activation(e[:], z[:], ACT.Exp, bias=zs[:, 1:2], accum_out=zs[:, 2:3]).then_inc(S["e_ready"], 1)

        @block.vector
        def _(v):
            ch = Chain(v, S["vch"])
            ch.then(v.memset(ones[:], 1.0))
            ch.link(v.memset(fhl[:], 0.0))
            v.wait_ge(S["row_in"], 48)
            ch.link(v.tensor_tensor(z[:], zz[:, 0, :], zz[:, 1, :], ALU.add))
            ch.link(v.tensor_reduce(zs[:, 0:1], z[:], AX.X, ALU.max))
            v.tensor_scalar(zs[:, 1:2], zs[:, 0:1], -1.0, None, ALU.mult).then_inc(S["z_ready"], 1)
            v.wait_ge(S["e_ready"], 1)
            ch.link(v.reciprocal(zs[:, 3:4], zs[:, 2:3]))
            ch.link(v.tensor_scalar(ysoft[:], e[:], zs[:, 3:4], None, ALU.mult))
            ch.link(v.tensor_reduce(zs[:, 0:1], ysoft[:], AX.X, ALU.max))
            ch.link(v.tensor_scalar(eq[:], ysoft[:], zs[:, 0:1], None, ALU.is_equal))
            ch.link(v.tensor_copy(cum[:], eq[:]))
            for n in range(1, NV):
                ch.link(v.tensor_tensor(cum[:, n:n + 1], cum[:, n - 1:n], eq[:, n:n + 1], ALU.max))
            ch.then(v.tensor_copy(hard[:, 0:1], cum[:, 0:1]))
            ch.link(v.tensor_tensor(hard[:, 1:NV], cum[:, 1:NV], cum[:, 0:NV - 1], ALU.subtract))
            ch.link(v.tensor_tensor(hard[:], hard[:], ysoft[:], ALU.subtract))
            ch.link(v.tensor_tensor(wts[:], hard[:], ysoft[:], ALU.add))
            v.wait_ge(S["phit"], 1)
            for n in range(8):
                ch.then(v.tensor_copy(phiT[:, 512 * n:512 * n + 512], ps[n][0:KF, :]))
            ch.wait()
            ch.link(v.tensor_reduce(pmax[:], phiT[:], AX.X, ALU.max, apply_absolute_value=True))
            ch.link(v.tensor_scalar(pmax[:], pmax[:], TINY, None, ALU.max))
            ch.link(v.reciprocal(inv[:], pmax[:]))
            ch.link(v.tensor_scalar(phiT[:], phiT[:], inv[:, 0:1], F_SCALE, ALU.mult, ALU.mult))
            src = phiT[:].rearrange("k (n r) -> k r n", r=2)
            ch.link(v.tensor_copy(fhl[:, 0, :, FRONT:], src))
            v.tensor_tensor(fhl[:, 1, :, FRONT:], src, fhl[:, 0, :, FRONT:], ALU.subtract).then_inc(S["filt_ready"], 1)
            ch.link(v.tensor_copy(al[:], sig[:]))
            rsqrt(v, ch, inv[:], al[:], tm[:])
            rsqrt(v, ch, al[:], inv[:], tm[:])
            ch.link(v.tensor_tensor(al[:], al[:], pmax[:], ALU.mult))
            v.tensor_scalar(diag[:], ident[0:KF, 0:KF], al[:, 0:1], None, ALU.mult).then_inc(S["diag_ready"], 1)
            v.wait_ge(S["alpha_ps"], 1)
            ch.link(v.tensor_copy(alpha[:], ps[0][:, 0:KF]))
            albc = alpha[:].unsqueeze(2).to_broadcast([P, KF, P])
            even = mix[:, LAGS:].rearrange("d (k r) e -> d r k e", r=2)
            for n in range(NV):
                v.wait_ge(m_in[n % 2], 48 * (n // 2 + 1))
                w = wts[:, n:n + 1]
                a2, p2 = acc[:].rearrange("d s k e -> d (s k e)"), pp[n % 2][:].rearrange("d s k e -> d (s k e)")
                u2, m2 = accu[:].rearrange("d k e -> d (k e)"), mu[n % 2][:].rearrange("d k e -> d (k e)")
                if n == 0:
                    ch.then(v.tensor_scalar(a2, p2, w, None, ALU.mult))
                    ch.link(v.tensor_scalar(u2, m2, w, None, ALU.mult))
                else:
                    ch.then(v.scalar_tensor_tensor(out=a2, in0=p2, scalar=w, in1=a2, op0=ALU.mult, op1=ALU.add))
                    ch.link(v.scalar_tensor_tensor(out=u2, in0=m2, scalar=w, in1=u2, op0=ALU.mult, op1=ALU.add))
                ch.then(v.tensor_copy(mix[:, 0:LAGS, :], accu[:]))
                ch.then(v.tensor_tensor(even[:, 0], acc[:, 0], acc[:, 1], ALU.add))
                ch.link(v.tensor_tensor(even[:, 1], acc[:, 0], acc[:, 1], ALU.subtract))
                for r in range(2):
                    ch.link(v.tensor_tensor(even[:, r], even[:, r], albc, ALU.mult))
                v.tensor_reduce(mx[:, 0:1], mix[:].rearrange("d m e -> d (m e)"), AX.X, ALU.max,
                                apply_absolute_value=True).then_inc(S["mx_ready"], 1)
                v.wait_ge(S["mxt"], n + 1)
                v.tensor_reduce(mrow[0:1, 0:1], ps[1][0:1, 0:P], AX.X, ALU.max).then_inc(S["mrow_ready"], 1)
                v.wait_ge(S["gmax"], n + 1)
                ch.link(v.tensor_scalar(mx[:, 1:2], ps[2][:, 0:1], TINY, None, ALU.max))
                ch.link(v.reciprocal(mx[:, 2:3], mx[:, 1:2]))
                ch.then(v.tensor_scalar(mgain[:, n:n + 1], mx[:, 1:2], 1.0 / M_SCALE, None, ALU.mult))
                ch.link(v.tensor_scalar(mix[:], mix[:], mx[:, 2:3], M_SCALE, ALU.mult, ALU.mult))
                if n:
                    v.wait_ge(S["stored"], 16 * (n + 1))
                ch.link(v.tensor_copy(mhl[:, :, 0, :], mix[:]))
                v.tensor_tensor(mhl[:, :, 1, :], mix[:], mhl[:, :, 0, :], ALU.subtract).then_inc(S["mhl_ready"], 1)


def spectral(nc, u_dram, t_dram, filt, mats, mgain, out):
    with ExitStack() as ctx:
        def sb(name, shape, dt=F32):
            return ctx.enter_context(nc.sbuf_tensor("sc_" + name, shape, dt))

        u = sb("u", [P, 2, BLK, B, 2, P], F16)
        H = [sb(f"H{r}", [P, 2, PH], F16) for r in range(2)]
        Mx = [sb(f"M{n}", [P, NMAT, 2, P], F16) for n in range(2)]
        us = sb("us", [P, B, 2, CH], F16)
        tT = [sb(f"tT{n}", [P, B, 2 * CH]) for n in range(2)]
        shift = [sb(f"shift{n}", [P, 2 * P], F16) for n in range(2)]
        flip = sb("flip", [P, P], F16)
        psU = [ctx.enter_context(nc.psum_tensor(f"sc_psU{b}", [P, CH], F32)) for b in range(B)]
        psY = [ctx.enter_context(nc.psum_tensor(f"sc_psY{b}", [P, CH], F32)) for b in range(B)]
        names = "turned_ps turned_act turned_dve shifts conv_done hi_ready us_ready y_done y_read".split()
        S = {n: ctx.enter_context(nc.semaphore("sc_" + n)) for n in names}
        h_in = [ctx.enter_context(nc.semaphore(f"sc_h_in{r}")) for r in range(2)]
        u_in = [ctx.enter_context(nc.semaphore(f"sc_u_in{b}")) for b in range(B)]
        m_in = [ctx.enter_context(nc.semaphore(f"sc_m_in{r}")) for r in range(2)]
        banks = psU + psY
        t_in = [ctx.enter_context(nc.semaphore(f"sc_t_in{r}")) for r in range(2)]
        o_st = [ctx.enter_context(nc.semaphore(f"sc_o_st{r}")) for r in range(2)]
        jobs = [(c, p) for c in range(NCH) for p in range(2)]
        UNITS = B * NMAT
        spans = {0: [(3, 0, CH // 2), (2, CH // 2, CH)], 1: [(1, 0, CH)], 2: [(0, 0, CH)], 3: [(0, 0, CH)]}
        buf = {3: 0, 2: 1, 1: 0, 0: 1}
        mload = {3: 16, 2: 16, 1: 32, 0: 32}
        block = ctx.enter_context(nc.Block())

        NTURN = B * BLK // 2

        def turn(n):
            return n // BLK, n // (BLK // 2) % 2, 2 * (n % (BLK // 2))

        def half(p, r):
            return (p, 0) if r == 0 else (1 - p, 1 - p)

        @block.sync
        def _(sp):
            ub = u_dram.rearrange("(b r) n c -> b (r n) c", b=B)
            for b in range(B):
                for ph in range(2):
                    sp.dma_start(u[:, ph, :, b].rearrange("s k h d -> s k (h d)"),
                                 ub[b].rearrange("(k s q) c -> q s k c", q=2, s=P)[ph]).then_inc(u_in[b], 16)

            def load_m(mx_):
                sp.dma_start(Mx[buf[mx_]][:].rearrange("d m h e -> d (m h e)"), mats[mx_]).then_inc(m_in[buf[mx_]], 16)

            def load_t(c):
                for b in range(B):
                    for a in range(2):
                        sp.dma_start(tT[c % 2][:, b, CH * a:CH * a + CH],
                                     t_dram[b * STRIPS + 2 * c + a]).then_inc(t_in[c % 2], 16)

            def store(c):
                sp.wait_ge(S["y_read"], B * 2 * (c + 1))
                for b in range(B):
                    sp.dma_start(out[b].rearrange("e h w -> e (h w)")[:, 2 * CH * c:2 * CH * (c + 1)],
                                 tT[c % 2][:, b, :]).then_inc(o_st[c % 2], 16)

            load_m(3)
            load_m(2)
            for n, (c, p) in enumerate(jobs):
                L = CH * (c + 1)
                if p == 0:
                    if c >= 2:
                        sp.wait_ge(o_st[c % 2], 16 * B * (c // 2))
                    load_t(c)
                    if c in (1, 2):
                        sp.wait_ge(S["y_done"], 2 * B * c)
                        load_m(2 - c)

                def load_h(k, r):
                    _, sh = half(p, r)
                    a = filt[bass.ds(k, 1), 0, r, :]
                    src = bass.AP(tensor=a.tensor, offset=a.offset + (FRONT - sh - (P - 1)), ap=[[1, P], [2 * FLEN, 2], [1, L]])
                    sp.dma_start(H[r][:, :, 0:L], src).then_inc(h_in[r], 16)

                with sp.Fori(0, KF) as k:
                    for r in range(2):
                        sp.wait_ge(S["conv_done"], k * (2 * B) + (UNITS * n + LAGS * B - B * (1 - r)))
                        load_h(k, r)
                if p == 1:
                    store(c)
            for n in range(2):
                sp.wait_ge(o_st[n], 16 * B * NCH // 2)

        @block.gpsimd
        def _(pool):
            pool.memset(shift[0][:], 0.0).then_inc(S["shifts"], 1)
            pool.memset(shift[1][:], 0.0).then_inc(S["shifts"], 1)
            pool.memset(flip[:], 0.0).then_inc(S["shifts"], 1)
            pool.wait_ge(S["shifts"], 3)
            pool.affine_select(out=flip[:], in_=flip[:], compare_op=ALU.not_equal, fill=1.0,
                               base=-(P - 1), pattern=[[1, P]], channel_multiplier=1).then_inc(S["shifts"], 1)
            for n in range(2):
                pool.affine_select(out=shift[n][:], in_=shift[n][:], compare_op=ALU.not_equal, fill=F_SCALE,
                                   base=-(P - 1) - n, pattern=[[1, 2 * P]], channel_multiplier=1).then_inc(S["shifts"], 1)

        @block.tensor
        def _(pe):
            pe.wait_ge(S["shifts"], 6)
            for n in range(2 * NTURN):
                b, ph, k = turn(n)
                if k == 0 and ph == 0:
                    pe.wait_ge(u_in[b], 32)
                if n >= 8:
                    pe.wait_ge(S["turned_dve" if n % 2 else "turned_act"], (n - 8) // 2 + 1)
                pe.matmul(banks[n % 8][:], flip[:], u[:, ph, k:k + 2, b], start=True, stop=True)\
                    .then_inc(S["turned_ps"], 1)
            pe.wait_ge(S["turned_act"], NTURN)
            pe.wait_ge(S["turned_dve"], NTURN)

            def conv_free(unit):
                if not (isinstance(unit, int) and unit < 4):
                    pe.wait_ge(S["us_ready"], unit - 3)

            def conv_lag(c, p, lag, b, unit):
                conv_free(unit)
                ph, sh = (p, lag // 2) if lag != 1 else (1 - p, 1 - p)
                first = True
                for i in range(-1 if (sh and c) else 0, 4):
                    for hl in range(2):
                        lo = max(0, P * i)
                        hi = min(CH, P * i + P + (P if sh else 0))
                        mm = pe.matmul(psU[b][:, lo:hi], u[:, ph, 4 * c + i, b, hl, :],
                                       shift[sh][:, lo - P * i:hi - P * i], start=first, stop=False,
                                       skip_group_check=True)
                        first = False
                mm.then_inc(S["conv_done"], 1)

            def conv(c, p, r, b, unit):
                conv_free(unit)
                ph, _ = half(p, r)
                for s in range(4 * c + 4):
                    lo = max(0, P * (s - 4 * c))
                    x = CH * c - P * s + lo
                    for hu, hh in ((0, 0), (0, 1), (1, 0)):
                        mm = pe.matmul(psU[b][:, lo:CH], u[:, ph, s, b, hu, :], H[r][:, hh, x:x + CH - lo],
                                       start=(s == 0 and hu == 0 and hh == 0), stop=False, skip_group_check=True)
                mm.then_inc(S["conv_done"], 1)

            def project(c, slot, b, unit, first=False):
                pe.wait_ge(S["us_ready"], unit + 1)
                for mx_, lo, hi in spans[c]:
                    for hm, hu in ((0, 0), (1, 0), (0, 1)):
                        m = Mx[buf[mx_]][:, slot, hm, :] if isinstance(slot, int) else \
                            Mx[buf[mx_]][:, bass.ds(slot, 1), hm, :].rearrange("d a e -> d (a e)")
                        mm = pe.matmul(psY[b][:, lo:hi], m, us[:, b, hu, lo:hi],
                                       start=(first and lo == 0 and hm == 0 and hu == 0), stop=False,
                                       skip_group_check=True)
                return mm

            for n, (c, p) in enumerate(jobs):
                base = UNITS * n
                for mx_, _, _ in spans[c]:
                    pe.wait_ge(m_in[buf[mx_]], mload[mx_])
                queue = [(lag, b) for lag in range(LAGS) for b in range(B)]
                for q, (lag, b) in enumerate(queue):
                    conv_lag(c, p, lag, b, base + q)
                    if q >= 2:
                        if q == 2 and n:
                            pe.wait_ge(S["y_read"], B * n)
                        lg, bb = queue[q - 2]
                        project(c, lg, bb, base + q - 2, first=(lg == 0))
                with pe.Fori(0, KF) as k:
                    unit0 = k * (2 * B) + (base + LAGS * B)
                    for r in range(2):
                        pe.wait_ge(h_in[r], k * 16 + 16 * (KF * n + 1))
                        for b in range(B):
                            q = r * B + b
                            conv(c, p, r, b, unit0 + q)
                            if q < 2:
                                project(c, k * 2 + (LAGS - 1), B - 2 + q, unit0 + q - 2)
                            else:
                                project(c, k * 2 + (LAGS + (q - 2) // B), (q - 2) % B, unit0 + q - 2)
                for b in range(B - 2, B):
                    mm = project(c, NMAT - 1, b, base + UNITS - B + b)
                mm.then_inc(S["y_done"], B)

        @block.scalar
        def _(act):
            def hi(b, unit):
                act.wait_ge(S["conv_done"], unit + 1)
                act.activation(us[:, b, 0, :], psU[b][:], ACT.Copy, scale=1.0 / (U_SCALE * F_SCALE))\
                    .then_inc(S["hi_ready"], 1)

            for n in range(0, 2 * NTURN, 2):
                b, ph, k = turn(n)
                act.wait_ge(S["turned_ps"], n + 1)
                act.copy(u[:, ph, k:k + 2, b], banks[n % 8][:].rearrange("p (k h d) -> p k h d", k=2, h=2))\
                    .then_inc(S["turned_act"], 1)
            with act.Fori(0, len(jobs) * NMAT) as j:
                for b in range(B):
                    hi(b, j * B + b)

        @block.vector
        def _(v):
            def lo(b, unit):
                v.wait_ge(S["hi_ready"], unit + 1)
                v.scalar_tensor_tensor(out=us[:, b, 1, :], in0=psU[b][:], scalar=1.0 / (U_SCALE * F_SCALE),
                                       in1=us[:, b, 0, :], op0=ALU.mult, op1=ALU.subtract).then_inc(S["us_ready"], 1)

            for n in range(1, 2 * NTURN, 2):
                b, ph, k = turn(n)
                v.wait_ge(S["turned_ps"], n + 1)
                v.tensor_copy(u[:, ph, k:k + 2, b], banks[n % 8][:].rearrange("p (k h d) -> p k h d", k=2, h=2))\
                    .then_inc(S["turned_dve"], 1)
            for n, (c, p) in enumerate(jobs):
                with v.Fori(0, NMAT) as j:
                    for b in range(B):
                        lo(b, j * B + (b + UNITS * n))
                v.wait_ge(S["y_done"], B * (n + 1))
                v.wait_ge(t_in[c % 2], 16 * 2 * B * (c // 2 + 1))
                for b in range(B):
                    for mx_, a, z in spans[c]:
                        t2 = tT[c % 2][:, b, :].rearrange("e (m q) -> e q m", q=2)[:, p, a:z]
                        ins = v.scalar_tensor_tensor(out=t2, in0=psY[b][:, a:z], scalar=mgain[:, mx_:mx_ + 1], in1=t2,
                                                     op0=ALU.mult, op1=ALU.add)
                    ins.then_inc(S["y_read"], 1)


def program(nc, x, wq, wk, wv, rel_h, rel_w, theta, phi_ffn, w1, b1, w2, b2, g1, be1, g2, be2,
            sigma, phi, m_u, m_plus, m_minus, log_weights, gumbel, out):
    xn_strips = nc.dram_tensor("xn_strips", [NSTRIP, P, KROWS * KCOLS + STOK], F32, kind="Internal").ap()
    u_dram = nc.dram_tensor("u_dram", [NSTRIP, STOK, 2 * P], F16, kind="Internal").ap()
    t_dram = nc.dram_tensor("t_dram", [NSTRIP, P, STOK], F32, kind="Internal").ap()
    filt = nc.dram_tensor("filt", [KF, 2, 2, FLEN], F16, kind="Internal").ap()
    mats = nc.dram_tensor("mats", [NV, P, NMAT * 2 * P], F16, kind="Internal").ap()
    with ExitStack() as ctx:
        def sb(name, shape):
            return ctx.enter_context(nc.sbuf_tensor("k_" + name, shape, F32))

        ident, mgain = sb("ident", [P, P]), sb("mgain", [P, NV])
        with ExitStack() as inner:
            def si(name, shape):
                return inner.enter_context(nc.sbuf_tensor("k_" + name, shape, F32))

            pers = {"ident": ident, "halfpi": si("halfpi", [P, 1]), "wk": si("wk", [P, 2, P]),
                    "LA": si("LA", [P, PQ, P]), "LB": si("LB", [P, 16, P]), "wv": si("wv", [P, P]),
                    "hotA": si("hotA", [P, KROWS, KCOLS]), "hotB": si("hotB", [P, KROWS, KCOLS]),
                    "mask": si("mask", [P, KEYS]), "cosphi": si("cosphi", [P, NQB])}
            prepare(nc, pers, x, wq, wk, wv, rel_h, rel_w, phi_ffn, xn_strips)
            with ExitStack() as tctx:
                tok = {name: tctx.enter_context(nc.sbuf_tensor("k_" + name, shape, F32)) for name, shape in (
                    ("theta", [P, P]), ("w1b", [NQB + 1, FF]), ("w2T", [P, FT, P]), ("qT", [NQB + 1, STOK]),
                    ("g1", [P, P]), ("be1", [P, P]), ("g2", [P, P]), ("be2", [P, P]), ("b2", [P, P]))}
                load_token_weights(nc, tok, theta, w1, b1, w2, b2, g1, be1, g2, be2, ident)
                strips(nc, pers, tok, xn_strips, u_dram, t_dram)
        spectral_prepare(nc, ident, phi, sigma, m_u, m_plus, m_minus, log_weights, gumbel, filt, mats, mgain)
        spectral(nc, u_dram, t_dram, filt, mats, mgain, out)


_INS = ['x', 'L0_conv_Wq', 'L0_conv_Wk', 'L0_conv_Wv', 'L0_conv_rel_h', 'L0_conv_rel_w',
        'L1_attn_theta_attn', 'L1_attn_phi_ffn', 'L1_attn_w1', 'L1_attn_b1', 'L1_attn_w2', 'L1_attn_b2',
        'L1_attn_gamma1', 'L1_attn_beta1', 'L1_attn_gamma2', 'L1_attn_beta2',
        'L1_ffn_sigma', 'L1_ffn_phi', 'L1_ffn_M_u', 'L1_ffn_M_phi_plus', 'L1_ffn_M_phi_minus',
        'L1_ffn_log_weights', 'L1_ffn_gumbel']
_OUTS = [((4, 128, 64, 64), 'float32')]


def kernel(**inputs):
    import numpy as _np
    import concourse.bacc as _bacc
    from concourse import mybir as _mybir
    from concourse.bass_utils import run_bass_kernel_spmd as _run

    nc = _bacc.Bacc("TRN2", target_bir_lowering=False, num_devices=1)
    arrays, args = {}, []
    for name in _INS:
        a = _np.ascontiguousarray(inputs[name])
        arrays[f"in_{name}_dram"] = a
        args.append(nc.dram_tensor(f"in_{name}_dram", a.shape, _mybir.dt.from_np(a.dtype), kind="ExternalInput").ap())
    for i, (shape, dtype) in enumerate(_OUTS):
        dt = _mybir.dt.from_np(_np.dtype(dtype))
        args.append(nc.dram_tensor(f"out_{i}_dram", shape, dt, kind="ExternalOutput").ap())
    program(nc, *args)
    r = _run(nc, [arrays], core_ids=[0])
    return r.results[0]["out_0_dram"]
```

```python
import concourse.bass as bass
from concourse import mybir
from contextlib import ExitStack
import math

F32 = mybir.dt.float32
F16 = mybir.dt.float16
BF16 = mybir.dt.bfloat16
I32 = mybir.dt.int32
ALU = mybir.AluOpType
ACT = mybir.ActivationFunctionType
AX = mybir.AxisListType

B, C, HH, WW = 4, 128, 64, 64
T = HH * WW
P = 128
WIN, PAD = 7, 3
HEADS, HC = 8, C // 8
ROWS = 8
STRIPS = HH // ROWS
NSTRIP = B * STRIPS
KROWS, KCOLS = ROWS + WIN - 1, WW + 2 * PAD
PQ = 8
PK = PQ + WIN - 1
KEYS = PK * PK
HALF = KEYS // 2
NPAIR = WW // (2 * PQ)
STOK = ROWS * WW
QH, NQB = 16, 8
FF = 2048
FT = FF // P
Q_PARTS, W_PARTS = (0, 0, 0, 1, 1, 2), (0, 1, 2, 0, 1, 0)
NST = len(Q_PARTS)
KST = NST * (NQB + 1)
NEG = -1.0e30
U_SCALE = 1024.0
TWO_PI = 2.0 * math.pi
TP1 = 6.28125
TP2 = TWO_PI - TP1
MAGIC = 1.5 * 2.0 ** 23
SIN_LO, SIN_HI = -1.5 * math.pi + 1e-6, 0.5 * math.pi - 1e-6


class Chain:

    def __init__(self, eng, sem, base=0):
        self.eng, self.sem, self.base, self.n = eng, sem, base, 0

    def then(self, ins):
        ins.then_inc(self.sem, 1)
        self.n += 1
        return self.n

    def link(self, ins):
        self.then(ins)
        self.eng.wait_ge(self.sem, self.base + self.n)

    def wait(self, n=None):
        self.eng.wait_ge(self.sem, self.base + (self.n if n is None else n))


def raw(ap, offset, dims):
    return bass.AP(tensor=ap.tensor, offset=ap.offset + offset, ap=dims)


def prepare(nc, pers, x, wq, wk, wv, rel_h, rel_w, phi_ffn, xn_strips):
    with ExitStack() as ctx:
        def sb(name, shape, dt=F32):
            return ctx.enter_context(nc.sbuf_tensor(name, shape, dt))

        def sem(name):
            return ctx.enter_context(nc.semaphore(name))

        xs = sb("pr_x", [P, B, T])
        xpad = [sb(f"pr_xpad{n}", [P, HH + 2 * PAD, KCOLS]) for n in range(2)]
        w_in = sb("pr_w", [P, 3, P])
        rel = sb("pr_rel", [P, WIN])
        gmask = sb("pr_gmask", [P, HEADS])
        relbd = sb("pr_relbd", [P, HEADS, WIN])
        gsum = sb("pr_gsum", [P, P])
        gsum_t = sb("pr_gsumt", [P, P])
        G = sb("pr_G", [P, HEADS, WIN])
        st = sb("pr_st", [P, B, 8, 6])
        mv = sb("pr_mv", [P, B, 2])
        gm = sb("pr_gm", [P, B])
        dd = sb("pr_dd", [P, B])
        var = sb("pr_var", [P, B])
        rs = sb("pr_rs", [P, B])
        ra = sb("pr_ra", [P, B])
        pidx = sb("pr_pidx", [P, 1], I32)
        pint = sb("pr_pint", [P, 4], I32)
        pf = sb("pr_pf", [P, 4])
        grid = sb("pr_grid", [P, KROWS, KCOLS])
        gridB = sb("pr_gridb", [P, KROWS, 5, 16])
        wgrid = sb("pr_wgrid", [P, 2, KEYS])
        wtmp = sb("pr_wtmp", [P, 3, KEYS])
        ph = sb("pr_ph", [P, 3, NQB])
        psT = ctx.enter_context(nc.psum_tensor("pr_psT", [P, 4, P], F32))
        psG = ctx.enter_context(nc.psum_tensor("pr_psG", [P, 512], F32))
        x_in = [sem(f"pr_x_in{b}") for b in range(B)]
        w_in_s, rel_in = sem("pr_w_in"), sem("pr_rel_in")
        consts, weights_t, g_done = sem("pr_consts"), sem("pr_weights_t"), sem("pr_g_done")
        relbd_ready, mean_ready, sq_ready = sem("pr_relbd"), sem("pr_mean"), sem("pr_sq")
        gstat, pad_ready, stored = sem("pr_gstat"), sem("pr_pad_ready"), [sem("pr_st0"), sem("pr_st1")]
        phi_in, dch, pch, cosd = sem("pr_phi_in"), sem("pr_dch"), sem("pr_pch"), sem("pr_cosd")
        phi_red = sem("pr_phi_red")
        block = ctx.enter_context(nc.Block())

        @block.sync
        def _(sp):
            sp.dma_start(w_in[:, 0, :], wq).then_inc(w_in_s, 16)
            sp.dma_start(w_in[:, 1, :], wk).then_inc(w_in_s, 16)
            sp.dma_start(w_in[:, 2, :], wv).then_inc(w_in_s, 16)
            half = C // 2
            sp.dma_start(rel[0:half, :], rel_h.rearrange("o a b k c -> o (a b k c)")).then_inc(rel_in, 16)
            sp.dma_start(rel[half:C, :], rel_w.rearrange("o a b c k -> o (a b c k)")).then_inc(rel_in, 16)
            for b in range(B):
                sp.dma_start(xs[:, b, :], x[b].rearrange("c h w -> c (h w)")).then_inc(x_in[b], 16)
            for b in range(B):
                sp.wait_ge(pad_ready, b + 1)
                flat = xpad[b % 2][:].rearrange("p h w -> p (h w)")
                for s in range(STRIPS):
                    a = s * ROWS * KCOLS
                    sp.dma_start(xn_strips[b * STRIPS + s, :, 0:KROWS * KCOLS],
                                 flat[:, a:a + KROWS * KCOLS]).then_inc(stored[b % 2], 16)
                sp.dma_start(xn_strips[b * STRIPS:(b + 1) * STRIPS, :, KROWS * KCOLS:].rearrange("s c n -> c s n"),
                             xs[:, b, :].rearrange("c (s n) -> c s n", n=STOK)).then_inc(stored[b % 2], 16)
            for n in range(2):
                sp.wait_ge(stored[n], 16 * (STRIPS + 1) * B // 2)

        @block.gpsimd
        def _(pool):
            ch = Chain(pool, pch)
            ident = pers["ident"]
            pool.dma_start(ph[:, 0, :], phi_ffn.partition_broadcast(P)).then_inc(phi_in, 16)
            ch.then(pool.memset(ident[:], 0.0))
            ch.then(pool.memset(gmask[:], 1.0))
            ch.then(pool.memset(gsum[:], 1.0 / 4))
            ch.then(pool.iota(pidx[:], pattern=[[0, 1]], base=0, channel_multiplier=1))
            ch.then(pool.iota(grid[:], pattern=[[1, KROWS], [0, KCOLS]], base=0, channel_multiplier=0,
                              allow_small_or_imprecise_dtypes=True))
            ch.then(pool.iota(gridB[:], pattern=[[0, KROWS], [0, 5], [1, 16]], base=0, channel_multiplier=0,
                              allow_small_or_imprecise_dtypes=True))
            ch.then(pool.iota(wgrid[:, 0, :], pattern=[[1, PK], [0, PK]], base=0, channel_multiplier=0,
                              allow_small_or_imprecise_dtypes=True))
            ch.link(pool.iota(wgrid[:, 1, :], pattern=[[0, PK], [1, PK]], base=0, channel_multiplier=0,
                              allow_small_or_imprecise_dtypes=True))
            ch.link(pool.affine_select(out=ident[:], in_=ident[:], compare_op=ALU.not_equal, fill=1.0,
                                       base=0, pattern=[[-1, P]], channel_multiplier=1))
            ch.link(pool.affine_select(out=gmask[:], in_=gmask[:], compare_op=ALU.is_ge, fill=0.0,
                                       base=0, pattern=[[-HC, HEADS]], channel_multiplier=1))
            ch.link(pool.affine_select(out=gmask[:], in_=gmask[:], compare_op=ALU.is_ge, fill=0.0,
                                       base=HC - 1, pattern=[[HC, HEADS]], channel_multiplier=-1))
            g4 = gsum[:].rearrange("p (g f) -> p g f", f=4)
            ch.link(pool.affine_select(out=g4, in_=g4, compare_op=ALU.is_ge, fill=0.0,
                                       base=0, pattern=[[-4, P // 4], [0, 4]], channel_multiplier=1))
            ch.link(pool.affine_select(out=g4, in_=g4, compare_op=ALU.is_ge, fill=0.0,
                                       base=3, pattern=[[4, P // 4], [0, 4]], channel_multiplier=-1))
            pool.memset(xpad[0][:], 0.0).then_inc(consts, 1)
            pool.memset(xpad[1][:], 0.0).then_inc(consts, 1)

        @block.tensor
        def _(pe):
            pe.wait_ge(pch, 13)
            pe.wait_ge(w_in_s, 48)
            for n in range(3):
                mm = pe.transpose(psT[:, n, :], w_in[:, n, :], pers["ident"][:])
            mm.then_inc(weights_t, 1)
            pe.wait_ge(relbd_ready, 1)
            pe.matmul(psG[:, 0:HEADS * WIN], w_in[:, 0, :], relbd[:].rearrange("p g k -> p (g k)"),
                      start=True, stop=True).then_inc(g_done, 1)
            pe.wait_ge(mean_ready, 1)
            pe.matmul(psT[:, 3, 0:B], gsum[:], gm[:], start=True, stop=True).then_inc(gstat, 1)
            pe.wait_ge(sq_ready, 1)
            pe.matmul(psT[:, 3, 8:8 + B], gsum[:], dd[:], start=True, stop=True).then_inc(gstat, 1)

        @block.scalar
        def _(act):
            act.wait_ge(phi_red, 1)
            act.activation(pers["cosphi"][:], ph[:, 2, :], ACT.Sin, bias=pers["halfpi"][:, 0:1]).then_inc(cosd, 1)

        @block.vector
        def _(v):
            ch = Chain(v, dch)
            ch.then(v.memset(pers["halfpi"][:], math.pi / 2))
            ch.then(v.memset(pers["wk"][:], 0.0))
            ch.then(v.memset(pers["LA"][:], 0.0))
            ch.link(v.memset(pers["LB"][:], 0.0))
            v.wait_ge(phi_in, 16)
            ch.link(v.tensor_scalar(ph[:, 1, :], ph[:, 0, :], 1.0 / TWO_PI, 0.25, ALU.mult, ALU.add))
            ch.link(v.tensor_scalar(ph[:, 1, :], ph[:, 1, :], MAGIC, MAGIC, ALU.add, ALU.subtract))
            ch.link(v.scalar_tensor_tensor(out=ph[:, 2, :], in0=ph[:, 1, :], scalar=-TP1, in1=ph[:, 0, :],
                                           op0=ALU.mult, op1=ALU.add))
            ch.link(v.scalar_tensor_tensor(out=ph[:, 2, :], in0=ph[:, 1, :], scalar=-TP2, in1=ph[:, 2, :],
                                           op0=ALU.mult, op1=ALU.add))
            v.tensor_scalar(ph[:, 2, :], ph[:, 2, :], SIN_LO, SIN_HI, ALU.max, ALU.min).then_inc(phi_red, 1)
            v.wait_ge(pch, 13)
            ch.then(v.tensor_copy(pers["identb"][:], pers["ident"][:]))
            for n, (sh, mask) in enumerate(((0, 31), (3, 7), (0, 7))):
                ch.then(v.tensor_scalar(pint[:, n:n + 1], pidx[:], sh, mask, ALU.logical_shift_right,
                                        ALU.bitwise_and))
            ch.wait()
            ch.link(v.tensor_copy(pf[:, 0:3], pint[:, 0:3]))
            ch.link(v.tensor_scalar(pf[:, 3:4], pf[:, 0:1], -16.0, None, ALU.add))
            ch.link(v.tensor_scalar(pers["hotA"][:], grid[:], pf[:, 3:4], None, ALU.is_equal))
            ch.link(v.tensor_scalar(pers["hotB"][:], gridB[:].rearrange("p y a c -> p y (a c)")[:, :, 0:KCOLS], pf[:, 3:4], None, ALU.is_equal))
            for n in range(2):
                ch.link(v.tensor_scalar(wtmp[:, 2, :], wgrid[:, n, :], pf[:, 1 + n:2 + n], None, ALU.subtract))
                ch.link(v.tensor_scalar(wtmp[:, n, :], wtmp[:, 2, :], 0.0, None, ALU.is_ge))
                ch.link(v.tensor_scalar(wtmp[:, 2, :], wtmp[:, 2, :], float(WIN - 1), None, ALU.is_le))
                ch.link(v.tensor_tensor(wtmp[:, n, :], wtmp[:, n, :], wtmp[:, 2, :], ALU.mult))
            ch.link(v.tensor_tensor(wtmp[:, 2, :], wtmp[:, 0, :], wtmp[:, 1, :], ALU.mult))
            ch.link(v.tensor_scalar(pers["mask"][:], wtmp[:, 2, :], -NEG, NEG, ALU.mult, ALU.add))
            v.wait_ge(rel_in, 32)
            for g in range(HEADS):
                ins = v.tensor_scalar(relbd[:, g, :], rel[:], gmask[:, g:g + 1], None, ALU.mult)
            ins.then_inc(relbd_ready, 1)
            v.wait_ge(weights_t, 1)
            for s in range(2):
                src = psT[:, :, s * 64:s * 64 + 64].rearrange("p n (j i) -> p n j i", i=HC)
                v.tensor_copy(pers["wk"][:, s, :].rearrange("p (j i) -> p j i", i=32)[:, :, 0:HC], src[:, 1])
                for y in range(PQ):
                    if s == 0:
                        v.tensor_copy(pers["LA"][:, y, :].rearrange("p (j i) -> p j i", i=32)[:, :, 0:HC], src[:, 0])
                for y in range(16):
                    if s == 1:
                        v.tensor_copy(pers["LB"][:, y, :].rearrange("p (j i) -> p j i", i=32)[:, :, 0:HC], src[:, 0])
            v.tensor_copy(pers["wv"][:], psT[:, 2, :])
            v.wait_ge(g_done, 1)
            ch.link(v.tensor_copy(G[:].rearrange("p g k -> p (g k)"), psG[:, 0:HEADS * WIN]))
            for y in range(PQ):
                v.tensor_copy(pers["LA"][:, y, :].rearrange("p (j i) -> p j i", i=32)[:, :, HC + y:HC + y + WIN],
                              G[:, 0:4, :])
            for c in range(16):
                dst = pers["LB"][:, c, :].rearrange("p (j i) -> p j i", i=32)
                n = min(WIN, 16 - c)
                v.tensor_copy(dst[:, :, HC + c:HC + c + n], G[:, 4:8, 0:n])
                if n < WIN:
                    v.tensor_copy(dst[:, :, HC:HC + WIN - n], G[:, 4:8, n:WIN])
            for b in range(B):
                v.wait_ge(x_in[b], 16)
                for k in range(8):
                    ch.then(v.bn_stats(st[:, b, k, :], xs[:, b, 512 * k:512 * k + 512]))
                ch.wait()
                ch.then(v.bn_aggr(mv[:, b, :], st[:, b, :, :]))
            ch.wait()
            v.tensor_copy(gm[:], mv[:, :, 0]).then_inc(mean_ready, 1)
            v.wait_ge(gstat, 1)
            ch.link(v.tensor_copy(gm[:], psT[:, 3, 0:B]))
            ch.link(v.tensor_tensor(ra[:], mv[:, :, 0], gm[:], ALU.subtract))
            ch.link(v.tensor_tensor(rs[:], ra[:], ra[:], ALU.mult))
            v.tensor_tensor(dd[:], rs[:], mv[:, :, 1], ALU.add).then_inc(sq_ready, 1)
            v.wait_ge(gstat, 2)
            ch.link(v.tensor_scalar(var[:], psT[:, 3, 8:8 + B], 1e-5, None, ALU.add))
            rsqrt(v, ch, rs[:], var[:], ra[:])
            for b in range(B):
                if b < 2:
                    v.wait_ge(consts, 2)
                else:
                    v.wait_ge(stored[b % 2], 16 * (STRIPS + 1) * (b // 2))
                v.tensor_scalar(xpad[b % 2][:, PAD:PAD + HH, PAD:PAD + WW],
                                xs[:, b, :].rearrange("p (h w) -> p h w", w=WW), gm[:, b:b + 1], rs[:, b:b + 1],
                                ALU.subtract, ALU.mult).then_inc(pad_ready, 1)


def rsqrt(v, ch, y, x, tmp, src=None, eps=0.0):
    if src is None:
        ch.link(v.tensor_scalar(tmp.bitcast(I32), x.bitcast(I32), 1, None, ALU.arith_shift_right))
        ch.then(v.tensor_scalar(x, x, -0.5, None, ALU.mult))
    else:
        ch.link(v.tensor_scalar(y, src, eps, None, ALU.add))
        ch.then(v.tensor_scalar(x, src, -0.5, -0.5 * eps, ALU.mult, ALU.add))
        ch.link(v.tensor_scalar(tmp.bitcast(I32), y.bitcast(I32), 1, None, ALU.arith_shift_right))
    ch.link(v.tensor_scalar(y.bitcast(I32), tmp.bitcast(I32), -1, 0x5F3759DF, ALU.mult, ALU.add))
    for _ in range(3):
        ch.link(v.tensor_tensor(tmp, y, y, ALU.mult))
        ch.link(v.tensor_tensor(tmp, tmp, x, ALU.mult))
        ch.link(v.scalar_tensor_tensor(out=y, in0=tmp, scalar=1.5, in1=y, op0=ALU.add, op1=ALU.mult))


def load_token_weights(nc, tok, theta, w1, b1, w2, b2, g1, be1, g2, be2, ident, identb):
    with ExitStack() as ctx:
        w1_in = ctx.enter_context(nc.sbuf_tensor("tw_w1", [P, FT, NQB + 1], F32))
        b1_in = ctx.enter_context(nc.sbuf_tensor("tw_b1", [FT, P], F32))
        rest = [ctx.enter_context(nc.sbuf_tensor(f"tw_rest{n}", [P, FT, NQB + 1], F32)) for n in range(2)]
        part = [ctx.enter_context(nc.sbuf_tensor(f"tw_part{n}", [P, FT, NQB + 1], BF16)) for n in range(3)]
        stack = ctx.enter_context(nc.sbuf_tensor("tw_stack", [P, FT, NST, NQB + 1], BF16))
        w2_in = ctx.enter_context(nc.sbuf_tensor("tw_w2", [P, FT, P], F32))
        th = ctx.enter_context(nc.sbuf_tensor("tw_th", [P, NQB], F32))
        ps = [ctx.enter_context(nc.psum_tensor(f"tw_ps{n}", [P, 4, P], F32)) for n in range(8)]
        rows_in, w1_s, w2_s, b1_s, b1t, split, stacked, w1t, w2t, done = (
            ctx.enter_context(nc.semaphore("tw_" + n))
            for n in ("rows_in", "w1_in", "w2_in", "b1_in", "b1t", "split", "stacked", "w1t", "w2t", "done"))
        block = ctx.enter_context(nc.Block())

        @block.sync
        def _(sp):
            sp.dma_start(w1_in[:, :, 0:NQB], w1.rearrange("(k p) q -> p k q", p=P)).then_inc(w1_s, 16)
            sp.dma_start(b1_in[:], b1.rearrange("(k p) -> k p", p=P)).then_inc(b1_s, 16)
            sp.dma_start(w2_in[:], w2.rearrange("e (k f) -> e k f", f=P)).then_inc(w2_s, 16)
            sp.dma_start(th[:], theta.partition_broadcast(P)).then_inc(rows_in, 16)
            for name, row in (("b2", b2), ("g1", g1), ("be1", be1), ("g2", g2), ("be2", be2)):
                sp.dma_start(tok[name][:], row.partition_broadcast(P)).then_inc(rows_in, 16)
            sp.wait_ge(rows_in, 16 * 6)

        @block.tensor
        def _(pe):
            pe.wait_ge(b1_s, 16)
            pe.transpose(ps[0][:, 0, 0:FT], b1_in[:], ident[0:FT, 0:FT]).then_inc(b1t, 1)
            pe.wait_ge(w2_s, 16)
            for k in range(FT):
                mm = pe.transpose(ps[4 + k // 4][:, k % 4, :], w2_in[:, k, :], ident[:])
            mm.then_inc(w2t, 1)
            pe.wait_ge(stacked, 1)
            for k in range(FT):
                mm = pe.matmul(ps[k // 4][0:KST, k % 4, :], stack[:, k].rearrange("p n q -> p (n q)"), identb[:],
                               start=True, stop=True)
            mm.then_inc(w1t, 1)

        @block.vector
        def _(v):
            ch = Chain(v, split)
            v.wait_ge(w1_s, 16)
            v.wait_ge(b1t, 1)
            ch.link(v.tensor_copy(w1_in[:, :, NQB], ps[0][:, 0, 0:FT]))
            three_parts(v, ch, w1_in[:], [t[:] for t in rest], [t[:] for t in part])
            for n, w in enumerate(W_PARTS):
                ins = v.tensor_copy(stack[:, :, n, :], part[w][:])
            ins.then_inc(stacked, 1)
            v.wait_ge(w2t, 1)
            for n in range(4):
                v.tensor_copy(tok["w2T"][:, 4 * n:4 * n + 4, :], ps[4 + n][:]).then_inc(done, 1)
            v.wait_ge(w1t, 1)
            for n in range(4):
                v.tensor_copy(tok["w1s"][:, 512 * n:512 * n + 512].rearrange("p (k f) -> p k f", f=P),
                              ps[n][0:KST, :, :]).then_inc(done, 1)
            v.wait_ge(rows_in, 16 * 6)
            v.tensor_copy(tok["theta"][:].rearrange("p (g j) -> p g j", j=NQB),
                          th[:].unsqueeze(1).to_broadcast([P, QH, NQB])).then_inc(done, 1)
            v.wait_ge(done, 9)


def three_parts(v, ch, src, rest, part):
    ch.link(v.tensor_copy(part[0], src))
    ch.link(v.tensor_tensor(rest[0], src, part[0], ALU.subtract))
    ch.link(v.tensor_copy(part[1], rest[0]))
    ch.link(v.tensor_tensor(rest[1], rest[0], part[1], ALU.subtract))
    ch.link(v.tensor_copy(part[2], rest[1]))


ATT_LINKS, MID_LINKS, FIN_LINKS = 4, 77, 53


def strips(nc, pers, tok, xn_strips, u_dram, t_dram):
    with ExitStack() as ctx:
        def sb(name, shape, dt=F32):
            return ctx.enter_context(nc.sbuf_tensor(name, shape, dt))

        def sem(name):
            return ctx.enter_context(nc.semaphore(name))

        NX = KROWS * KCOLS
        strip = sb("st_strip", [P, NX + STOK])
        xn3 = strip[:, 0:NX].rearrange("p (h w) -> p h w", w=KCOLS)
        xw = strip[:, NX:].rearrange("p (y r x) -> p r y x", y=ROWS, r=2 * NPAIR)
        xwin = sb("st_xwin", [P, 2 * NPAIR, KEYS])
        xpatch = sb("st_xpatch", [P, 2 * NPAIR, PQ * PQ])
        K = [sb(f"st_K{s}", [P, KROWS, KCOLS]) for s in range(2)]
        Q = [sb(f"st_Q{s}", [P, 2 * NPAIR, PQ * PQ]) for s in range(2)]
        V = sb("st_V", [HALF, 2 * 2 * NPAIR, P])
        Sm = [sb(f"st_Sm{s}", [P, 4, KEYS]) for s in range(2)]
        Pr = [sb(f"st_Pr{s}", [P, 4, KEYS]) for s in range(2)]
        nmax = [sb(f"st_nmax{s}", [P, 4]) for s in range(2)]
        den = [sb(f"st_den{s}", [P, HEADS]) for s in range(2)]
        rden = sb("st_rden", [P, HEADS])
        PT = [sb(f"st_PT{s}", [HALF, 8, P]) for s in range(2)]
        xt = sb("st_xt", [P, NPAIR, P])
        at = sb("st_at", [P, P])
        t0, t0m, t0g, t0f = (sb("st_" + n, [P, NPAIR, P]) for n in ("t0", "t0m", "t0g", "t0f"))
        n0, arg, turns, c, x1, x1b = (sb("st_" + n, [P, NPAIR, P]) for n in ("n0", "arg", "turns", "c", "x1", "x1b"))
        y, tt_sb = sb("st_y", [P, NPAIR, P]), sb("st_tt", [P, STOK])
        tfin = sb("st_tfin", [P, NPAIR, P])
        uhl = sb("st_uhl", [P, NPAIR, 2, P], F16)
        stm, stf = sb("st_stm", [P, NPAIR, 6]), sb("st_stf", [P, NPAIR, 6])
        mvm, mvf = sb("st_mvm", [P, NPAIR, 2]), sb("st_mvf", [P, NPAIR, 2])
        vm, vf = sb("st_vm", [P, 3, NPAIR]), sb("st_vf", [P, 3, NPAIR])
        fq = sb("st_fq", [P, 4, NPAIR, NQB])
        qrest = [sb(f"st_qrest{n}", [P, NPAIR, NQB]) for n in range(2)]
        qpart = [sb(f"st_qpart{n}", [P, NPAIR, NQB], BF16) for n in range(3)]
        qstack = sb("st_qstack", [P, NPAIR, NST, NQB + 1], BF16)
        cell, one_cell = sb("st_cell", [P, 1]), sb("st_one", [P, 1])
        h = sb("st_h", [P, FT, STOK])
        psS = [ctx.enter_context(nc.psum_tensor(f"st_psS{n}", [P, 512], F32)) for n in range(4)]
        psT = [ctx.enter_context(nc.psum_tensor(f"st_psT{n}", [P, 512], F32)) for n in range(2)]
        psO = ctx.enter_context(nc.psum_tensor("st_psO", [P, 512], F32))
        psF = ctx.enter_context(nc.psum_tensor("st_psF", [P, 512], F32))

        names = ("one win_ready strip_in k_ready q_ready v_ready xt_ready k_copied q_copied v_copied xt_copied "
                 "scores_ready scores_read probs_ready pt_ready pt_act pt_dve pv_done out_read t0_ready "
                 "t0_kept sin_in sin_out qf_ready qt_ready qt_copied h_ready relu_act relu_dve "
                 "ffn_done ffn_read x1b_kept t0g_kept stack_const t_ready tt_ready tt_copied tt_stored u_ready u_stored t0f_kept "
                 "ach mch fch").split()
        S = {n: sem("st_" + n) for n in names}

        def wait(eng, name, value):
            if not (isinstance(value, int) and value <= 0):
                eng.wait_ge(S[name], value)

        def gate(v, sem_, value):
            if not (isinstance(value, int) and value <= 0):
                v.wait_ge(sem_, value)
            if not isinstance(value, int):
                v.memset(cell[:], 0.0)

        def pool_copy(pool, out, in_):
            one = one_cell[:] if len(in_.shape) == 2 else one_cell[:].unsqueeze(1)
            return pool.tensor_tensor(out, in_, one.to_broadcast(list(in_.shape)), ALU.mult)

        def sp_load(sp, i):
            wait(sp, "q_ready", 2 * i)
            wait(sp, "win_ready", 1 * i)
            sp.dma_start(strip[:], xn_strips[bass.ds(i, 1)].rearrange("a c n -> (a c) n")).then_inc(S["strip_in"], 16)

        def sp_store(sp, i):
            sp.wait_ge(S["u_ready"], i + 1)
            for r in range(NPAIR):
                for q in range(2):
                    dst = u_dram[bass.ds(i, 1)].rearrange("a (y r q x) n -> (a r) q y x n", y=ROWS, r=NPAIR, q=2)
                    sp.dma_start(dst[r, q], uhl[64 * q:64 * q + 64, r].rearrange("p a b -> p (a b)"))\
                        .then_inc(S["u_stored"], 16)
            sp.wait_ge(S["tt_copied"], i + 1)
            sp.dma_start(t_dram[bass.ds(i, 1)].rearrange("a c n -> (a c) n"),
                         tt_sb[:]).then_inc(S["tt_stored"], 16)

        def pe_project(pe, i):
            pe.wait_ge(S["strip_in"], 16 * (i + 1))
            wait(pe, "scores_read", 8 * i)
            flat = strip[:, 0:NX]
            for s in range(2):
                for n in range(2):
                    mm = pe.matmul(psS[2 * s + n][:, 0:NX // 2], pers["wk"][:, s, :],
                                   flat[:, n * NX // 2:(n + 1) * NX // 2], start=True, stop=True)
                mm.then_inc(S["k_ready"], 1)
            wait(pe, "pt_act", 8 * i)
            for y_ in range(ROWS):
                mm = pe.matmul(psT[0][:, 64 * y_:64 * y_ + 64], pers["LA"][:, y_, :],
                               xn3[:, PAD + y_, PAD:PAD + WW], start=True, stop=True)
            mm.then_inc(S["q_ready"], 1)
            wait(pe, "pt_dve", 8 * i)
            qb = psT[1][:].rearrange("p (y a m) -> p m y a", y=ROWS, m=16)
            for m in range(16):
                mm = pe.matmul(qb[:, m], pers["LB"][:, m, :], xn3[:, PAD:PAD + ROWS, PAD + m:PAD + m + 49:16],
                               start=True, stop=True)
            mm.then_inc(S["q_ready"], 1)
            for w in range(2 * 2 * NPAIR):
                p, hf = w // 2, w % 2
                if w == 0:
                    pe.wait_ge(S["win_ready"], i + 1)
                if w % 4 == 0:
                    pe.wait_ge(S["k_copied"], 2 * i + 1 + (w >= 8))
                mm = pe.matmul(psS[w // 4][0:HALF, (w % 4) * P:(w % 4 + 1) * P],
                               xwin[:, p, HALF * hf:HALF * hf + HALF], pers["wv"][:], start=True, stop=True)
                if w % 4 == 3:
                    mm.then_inc(S["v_ready"], 1)
            pe.wait_ge(S["q_copied"], 2 * i + 1)
            for r in range(NPAIR):
                mm = pe.transpose(psT[0][:, r * P:(r + 1) * P], xpatch[:, 2 * r:2 * r + 2, :].rearrange("p q n -> p (q n)"),
                                  pers["ident"][:])
            mm.then_inc(S["xt_ready"], 1)

        def pe_scores(pe, i, u):
            r, s = u // 2, u % 2
            if u == 0:
                pe.wait_ge(S["q_copied"], 2 * (i + 1))
                pe.wait_ge(S["v_copied"], 4 * (i + 1))
            else:
                pe.wait_ge(S["scores_read"], 8 * i + u)
            for q in range(2):
                col = PQ * (2 * r + q)
                for j in range(4):
                    mm = pe.matmul(psS[j][64 * q:64 * q + 64, 0:KEYS],
                                   Q[s][32 * j:32 * j + 32, 2 * r + q, :], K[s][32 * j:32 * j + 32, :, col:col + PK],
                                   start=True, stop=True)
            mm.then_inc(S["scores_ready"], 1)

        def pe_turn(pe, i, u, ffn):
            pe.wait_ge(S["probs_ready"], 8 * i + u + 1)
            if ffn:
                pe.wait_ge(S["relu_act"], 8 * (i - 2) + u + 1)
                pe.wait_ge(S["relu_dve"], 8 * (i - 2) + u + 1)
            elif u:
                pe.wait_ge(S["pt_act"], 8 * i + u)
                pe.wait_ge(S["pt_dve"], 8 * i + u)
            else:
                pe.wait_ge(S["xt_copied"], i + 1)
            for j in range(4):
                for hf in range(2):
                    mm = pe.transpose(psT[j // 2][0:HALF, (2 * (j % 2) + hf) * P:(2 * (j % 2) + hf + 1) * P],
                                      Pr[u % 2][:, j, HALF * hf:HALF * hf + HALF], pers["ident"][:])
            mm.then_inc(S["pt_ready"], 1)

        def pe_values(pe, i, u):
            r, s = u // 2, u % 2
            pe.wait_ge(S["pt_act"], 8 * i + u + 1)
            pe.wait_ge(S["pt_dve"], 8 * i + u + 1)
            if s == 0:
                wait(pe, "out_read", 4 * i + r)
            for j in range(4):
                g = 4 * s + j
                for q in range(2):
                    for hf in range(2):
                        mm = pe.matmul(psO[64 * q:64 * q + 64, HC * g:HC * g + HC],
                                       PT[s][:, 2 * j + hf, 64 * q:64 * q + 64],
                                       V[:, 2 * (2 * r + q) + hf, HC * g:HC * g + HC],
                                       start=(hf == 0), stop=(hf == 1))
            mm.then_inc(S["pv_done"], 1)

        def pe_back(pe, k):
            pe.wait_ge(S["t_ready"], k + 1)
            for r in range(NPAIR):
                mm = pe.transpose(psF[:, r * P:(r + 1) * P], tfin[:, r, :], pers["ident"][:])
            mm.then_inc(S["tt_ready"], 1)

        def pe_qt(pe, i, k, att):
            pe.wait_ge(S["qf_ready"], k + 1)
            if att:
                pe.wait_ge(S["q_copied"], 2 * (i + 1))
            else:
                pe.wait_ge(S["pt_dve"], 8 * NSTRIP)
                pe.wait_ge(S["relu_dve"], 8 * k)
            for r in range(NPAIR):
                mm = pe.matmul(psT[1][0:KST, r * P:(r + 1) * P], qstack[:, r].rearrange("p n q -> p (n q)"),
                               pers["identb"][:], start=True, stop=True)
            mm.then_inc(S["qt_ready"], 1)

        def pe_hidden(pe, i, k, u, att):
            if u == 0:
                pe.wait_ge(S["qt_copied"], k + 1)
                if att:
                    pe.wait_ge(S["xt_copied"], i + 1)
                else:
                    pe.wait_ge(S["pt_act"], 8 * NSTRIP)
                    pe.wait_ge(S["relu_act"], 8 * k)
            for n in range(2):
                if u:
                    if att:
                        pe.wait_ge(S[("pt_act", "pt_dve")[n]], 8 * i + u)
                    else:
                        pe.wait_ge(S[("relu_act", "relu_dve")[n]], 8 * k + u)
                f = 2 * u + n
                pe.matmul(psT[n][:], tok["w1s"][:, P * f:P * f + P], tok["qT"][:], start=True, stop=True)\
                    .then_inc(S["h_ready"], 1)

        def pe_output(pe, k, w):
            if w == 0:
                wait(pe, "tt_copied", k)
            for n in range(2):
                f = 2 * w + n
                pe.wait_ge(S[("relu_act", "relu_dve")[n]], 8 * k + w + 1)
                for r in range(NPAIR):
                    mm = pe.matmul(psF[:, r * P:(r + 1) * P], h[:, f, r * P:(r + 1) * P], tok["w2T"][:, f, :],
                                   start=(f == 0 and r == 0), stop=(f == FT - 1), skip_group_check=True)
            if w == 7:
                mm.then_inc(S["ffn_done"], 1)

        def pe_step(pe, i, att=True, mid=True, ffn=True, fin=True):
            if att:
                pe_project(pe, i)
            if ffn:
                pe_qt(pe, i, i - 2, att)
            for u in range(10):
                if att and u < 8:
                    pe_scores(pe, i, u)
                if att and 1 <= u <= 8:
                    pe_turn(pe, i, u - 1, ffn)
                if fin and u == 2:
                    pe_back(pe, i - 3)
                if ffn and u >= 3:
                    if u == 3:
                        pe_output(pe, i - 2, 0)
                    pe_output(pe, i - 2, u - 2)
                if att and u >= 2:
                    pe_values(pe, i, u - 2)
                if ffn and u < 8:
                    pe_hidden(pe, i, i - 2, u, att)

        def act_copies(act, i):
            for n in range(2):
                act.wait_ge(S["q_ready"], 2 * i + n + 1)
                wait(act, "scores_ready", 8 * i)
                act.copy(Q[n][:].rearrange("p r (y x) -> p r y x", x=PQ),
                         psT[n][:].rearrange("p (y r x) -> p r y x", y=ROWS, x=PQ)).then_inc(S["q_copied"], 1)
            wait(act, "pv_done", 8 * i)
            for n in range(4):
                act.wait_ge(S["v_ready"], 4 * i + n + 1)
                act.copy(V[:, 4 * n:4 * n + 4, :].rearrange("p w c -> p (w c)"), psS[n][0:HALF, :])\
                    .then_inc(S["v_copied"], 1)
            act.wait_ge(S["xt_ready"], i + 1)
            wait(act, "t0_ready", 4 * i)
            act.copy(xt[:].rearrange("p r c -> p (r c)"), psT[0][:]).then_inc(S["xt_copied"], 1)

        def act_exp(act, i, u):
            r, s = u // 2, u % 2
            act.wait_ge(S["scores_read"], 8 * i + u + 1)
            wait(act, "pt_ready", 8 * i + u - 1)
            if s == 0:
                wait(act, "out_read", 4 * i + r - 1)
            for j in range(4):
                ins = act.activation(Pr[s][:, j, :], Sm[s][:, j, :], ACT.Exp, scale=-1.0, bias=nmax[s][:, j:j + 1],
                                     accum_out=den[r % 2][:, 4 * s + j:4 * s + j + 1])
            ins.then_inc(S["probs_ready"], 1)

        def act_pt(act, i, u):
            act.wait_ge(S["pt_ready"], 8 * i + u + 1)
            wait(act, "pv_done", 8 * i + u - 1)
            act.copy(PT[u % 2][:, 0:4, :].rearrange("p w c -> p (w c)"), psT[0][0:HALF, :]).then_inc(S["pt_act"], 1)

        def act_sin(act, k, n):
            act.wait_ge(S["sin_in"], 2 * k + n + 1)
            if n == 0:
                act.activation(c[:], arg[:], ACT.Sin, bias=pers["halfpi"][:, 0:1]).then_inc(S["sin_out"], 1)
            else:
                act.activation(fq[:, 2], fq[:, 1], ACT.Sin, bias=pers["halfpi"][:, 0:1]).then_inc(S["sin_out"], 1)

        def act_tt(act, k):
            act.wait_ge(S["tt_ready"], k + 1)
            wait(act, "tt_stored", 16 * k)
            act.copy(tt_sb[:].rearrange("p (y r x) -> p r y x", y=ROWS, x=PQ),
                     psF[:].rearrange("p (r y x) -> p r y x", y=PQ, x=PQ)).then_inc(S["tt_copied"], 1)

        def act_relu(act, k, u):
            act.wait_ge(S["h_ready"], FT * k + 2 * u + 1)
            if u == 0:
                wait(act, "ffn_done", k)
            act.activation(h[:, 2 * u, :], psT[0][:], ACT.Relu).then_inc(S["relu_act"], 1)

        def act_step(act, i, att=True, mid=True, ffn=True, fin=True):
            if att:
                act_copies(act, i)
            for u in range(9):
                if att and u < 8:
                    act_exp(act, i, u)
                if att and u >= 1:
                    act_pt(act, i, u - 1)
                if fin and u == 2:
                    act_tt(act, i - 3)
                if ffn and u < 8:
                    act_relu(act, i - 2, u)
                if mid and u == 4:
                    act_sin(act, i - 1, 0)
                if mid and u == 7:
                    act_sin(act, i - 1, 1)

        def norm_stats(v, ch, src, st, mv):
            for r in range(NPAIR):
                ch.then(v.bn_stats(st[:, r, :], src[:, r, :]))
            gate(v, ch.sem, ch.base + ch.n)
            for r in range(NPAIR):
                ch.then(v.bn_aggr(mv[:, r, :], st[:, r, :].rearrange("p (a s) -> p a s", a=1)))
            ch.wait()

        def norm_apply(v, ch, src, dst, mv, vv):
            rsqrt(v, ch, vv[:, 1, :], vv[:, 0, :], vv[:, 2, :], src=mv[:, :, 1], eps=1e-5)
            for r in range(NPAIR):
                ch.then(v.tensor_scalar(dst[:, r, :], src[:, r, :], mv[:, r, 0:1], vv[:, 1, r:r + 1],
                                        ALU.subtract, ALU.mult))
            ch.wait()

        def whole_turns(v, ch, src, turns_, dst):
            ch.link(v.tensor_scalar(turns_, src, 1.0 / TWO_PI, 0.25, ALU.mult, ALU.add))
            ch.link(v.tensor_scalar(turns_, turns_, MAGIC, MAGIC, ALU.add, ALU.subtract))
            ch.link(v.scalar_tensor_tensor(out=src, in0=turns_, scalar=-TP1, in1=src, op0=ALU.mult, op1=ALU.add))
            ch.link(v.scalar_tensor_tensor(out=src, in0=turns_, scalar=-TP2, in1=src, op0=ALU.mult, op1=ALU.add))
            return v.tensor_scalar(dst, src, SIN_LO, SIN_HI, ALU.max, ALU.min)

        def rows(name):
            return tok[name][:].unsqueeze(1).to_broadcast([P, NPAIR, P])

        def flat(t):
            return t[:].rearrange("p r c -> p (r c)")

        def dve_keys(v, i):
            wait(v, "scores_ready", 8 * i)
            for s in range(2):
                v.wait_ge(S["k_ready"], 2 * i + s + 1)
                kf, hot = K[s][:].rearrange("p h w -> p (h w)"), pers["hot" + "AB"[s]][:].rearrange("p h w -> p (h w)")
                for n in range(2):
                    a, b = n * NX // 2, (n + 1) * NX // 2
                    ins = v.tensor_tensor(kf[:, a:b], psS[2 * s + n][:, 0:NX // 2], hot[:, a:b], ALU.add)
                ins.then_inc(S["k_copied"], 1)

        def dve_max(v, i, u):
            s = u % 2
            wait(v, "probs_ready", 8 * i + u - 1)
            gate(v, S["scores_ready"], 8 * i + u + 1)
            for j in range(4):
                ins = v.tensor_tensor_reduce(Sm[s][:, j, :], psS[j][:, 0:KEYS],
                                             pers["mask"][:], -1.0, 3.0e38, ALU.add, ALU.min, nmax[s][:, j:j + 1])
            ins.then_inc(S["scores_read"], 1)

        def dve_pt(v, i, u):
            v.wait_ge(S["pt_ready"], 8 * i + u + 1)
            wait(v, "pv_done", 8 * i + u - 1)
            v.tensor_copy(PT[u % 2][:, 4:8, :].rearrange("p w c -> p (w c)"), psT[1][0:HALF, :]).then_inc(S["pt_dve"], 1)

        def dve_out(v, ch, i, r):
            ch.link(v.reciprocal(rden[:], den[r % 2][:]))
            v.wait_ge(S["pv_done"], 8 * i + 2 * r + 2)
            v.tensor_tensor(at[:].rearrange("p (g c) -> p g c", c=HC), psO[:, 0:P].rearrange("p (g c) -> p g c", c=HC),
                            rden[:].unsqueeze(2).to_broadcast([P, HEADS, HC]), ALU.mult).then_inc(S["out_read"], 1)
            v.wait_ge(S["out_read"], 4 * i + r + 1)
            if r == 0:
                v.wait_ge(S["xt_copied"], i + 1)
                wait(v, "t0_kept", i)
            v.tensor_tensor(t0[:, r, :], at[:], xt[:, r, :], ALU.add).then_inc(S["t0_ready"], 1)

        def dve_mid1(v, ch, k):
            v.wait_ge(S["t0_kept"], k + 1)
            norm_stats(v, ch, t0m, stm, mvm)

        def dve_mid1b(v, ch, k):
            norm_apply(v, ch, t0m, n0, mvm, vm)

        def dve_mid2(v, ch, k):
            ch.link(v.tensor_tensor(turns[:], n0[:], rows("theta"), ALU.add))
            whole_turns(v, ch, turns[:], c[:], arg[:]).then_inc(S["sin_in"], 1)

        def dve_mid3(v, ch, k):
            v.wait_ge(S["sin_out"], 2 * k + 1)
            c8, n8 = c[:].rearrange("p r (g j) -> p (r g) j", j=NQB), n0[:].rearrange("p r (g j) -> p (r g) j", j=NQB)
            s8 = arg[:].rearrange("p r (g j) -> p (r g) j", j=NQB)
            for j in range(1, NQB):
                ch.link(v.tensor_tensor(c8[:, :, j], c8[:, :, j - 1], c8[:, :, j], ALU.mult))
            ch.then(v.tensor_tensor(s8[:, :, 1:], n8[:, :, 1:], c8[:, :, 1:], ALU.add))
            ch.link(v.tensor_tensor(s8[:, :, 0], n8[:, :, 0], c8[:, :, NQB - 1], ALU.add))

        def dve_mid4(v, ch, k):
            norm_stats(v, ch, arg, stm, mvm)

        def dve_mid4b(v, ch, k):
            norm_apply(v, ch, arg, x1, mvm, vm)

        def dve_mid5(v, ch, k):
            ch.link(v.tensor_tensor(x1[:], x1[:], rows("g1"), ALU.mult))
            ch.link(v.tensor_tensor(x1[:], x1[:], rows("be1"), ALU.add))
            ch.link(v.tensor_copy(fq[:, 0], x1[:, :, 0:NQB]))
            whole_turns(v, ch, fq[:, 0], fq[:, 2], fq[:, 1]).then_inc(S["sin_in"], 1)

        def dve_mid6(v, ch, k):
            v.wait_ge(S["sin_out"], 2 * k + 2)
            ch.link(v.tensor_tensor(fq[:, 3], fq[:, 2], pers["cosphi"][:].unsqueeze(1).to_broadcast([P, NPAIR, NQB]),
                                    ALU.mult))
            three_parts(v, ch, fq[:, 3], [t[:] for t in qrest], [t[:] for t in qpart])
            wait(v, "qt_ready", k)
            for n in range(NST):
                ins = v.tensor_copy(qstack[:, :, n, 0:NQB], qpart[Q_PARTS[n]][:])
            ins.then_inc(S["qf_ready"], 1)

        def dve_qt(v, k):
            v.wait_ge(S["qt_ready"], k + 1)
            v.tensor_copy(tok["qT"][:], psT[1][0:KST, :]).then_inc(S["qt_copied"], 1)

        def dve_relu(v, k, u):
            v.wait_ge(S["h_ready"], FT * k + 2 * u + 2)
            if u == 0:
                wait(v, "ffn_done", k)
            v.tensor_scalar(h[:, 2 * u + 1, :], psT[1][:], 0.0, None, ALU.max).then_inc(S["relu_dve"], 1)

        def dve_fin1(v, k):
            v.wait_ge(S["ffn_done"], k + 1)
            v.tensor_tensor(flat(y), psF[:], flat(x1b), ALU.add).then_inc(S["ffn_read"], 1)
            v.wait_ge(S["ffn_read"], k + 1)

        def dve_keep_x1b(v, k):
            v.tensor_tensor(x1b[:], x1[:], rows("b2"), ALU.add).then_inc(S["x1b_kept"], 1)
            v.wait_ge(S["x1b_kept"], k + 1)

        def dve_fin2(v, ch, k):
            norm_stats(v, ch, y, stf, mvf)

        def dve_fin2b(v, ch, k):
            norm_apply(v, ch, y, y, mvf, vf)

        def dve_fin3(v, ch, k):
            ch.link(v.tensor_tensor(y[:], y[:], rows("g2"), ALU.mult))
            ch.link(v.tensor_tensor(y[:], y[:], rows("be2"), ALU.add))
            v.wait_ge(S["t0f_kept"], k + 1)
            wait(v, "tt_ready", k)
            v.tensor_tensor(tfin[:], y[:], t0f[:], ALU.add).then_inc(S["t_ready"], 1)
            v.wait_ge(S["t_ready"], k + 1)

        def dve_fin4(v, ch, k):
            norm_stats(v, ch, tfin, stf, mvf)

        def dve_fin4b(v, ch, k):
            norm_apply(v, ch, tfin, y, mvf, vf)

        def dve_fin5(v, ch, k):
            wait(v, "u_stored", 16 * 2 * NPAIR * k)
            ch.link(v.tensor_scalar(uhl[:, :, 0, :], y[:], U_SCALE, None, ALU.mult))
            v.scalar_tensor_tensor(out=uhl[:, :, 1, :], in0=y[:], scalar=U_SCALE, in1=uhl[:, :, 0, :],
                                   op0=ALU.mult, op1=ALU.subtract).then_inc(S["u_ready"], 1)

        def dve_step(v, i, att=True, mid=True, ffn=True, fin=True):
            ach = Chain(v, S["ach"], ATT_LINKS * i)
            mch = Chain(v, S["mch"], MID_LINKS * (i - 1))
            fch = Chain(v, S["fch"], FIN_LINKS * (i - 3))
            if att:
                dve_keys(v, i)
            if ffn:
                dve_qt(v, i - 2)
            if fin:
                dve_fin1(v, i - 3)
            if ffn:
                dve_keep_x1b(v, i - 2)
            for u in range(10):
                if att and u < 8:
                    dve_max(v, i, u)
                if att and 1 <= u <= 8:
                    dve_pt(v, i, u - 1)
                if fin and u == 1:
                    dve_fin2b(v, fch, i - 3)
                if mid and u == 2:
                    dve_mid1(v, mch, i - 1)
                if mid and u == 3:
                    dve_mid2(v, mch, i - 1)
                if fin and u == 4:
                    dve_fin4b(v, fch, i - 3)
                if mid and u == 5:
                    dve_mid3(v, mch, i - 1)
                if mid and u == 6:
                    dve_mid4b(v, mch, i - 1)
                if ffn and u < 8:
                    dve_relu(v, i - 2, u)
                if att and u >= 3 and u % 2 == 1:
                    dve_out(v, ach, i, (u - 3) // 2)
                if fin and u == 0:
                    dve_fin2(v, fch, i - 3)
                if fin and u == 1:
                    dve_fin3(v, fch, i - 3)
                if mid and u == 2:
                    dve_mid1b(v, mch, i - 1)
                if fin and u == 3:
                    dve_fin4(v, fch, i - 3)
                if fin and u == 4:
                    dve_fin5(v, fch, i - 3)
                if mid and u == 5:
                    dve_mid4(v, mch, i - 1)
                if mid and u == 6:
                    dve_mid5(v, mch, i - 1)
                if mid and u == 8:
                    dve_mid6(v, mch, i - 1)
            assert (not att or ach.n == ATT_LINKS) and (not mid or mch.n == MID_LINKS) and \
                (not fin or fch.n == FIN_LINKS), (ach.n, mch.n, fch.n)

        def pool_windows(pool, i):
            wait(pool, "v_ready", 4 * i)
            wait(pool, "xt_ready", 1 * i)
            pool.wait_ge(S["strip_in"], 16 * (i + 1))
            for p in range(2 * NPAIR):
                copy = pool.tensor_copy if p else lambda out, in_: pool_copy(pool, out, in_)
                copy(xwin[:, p, :].rearrange("p (a b) -> p a b", a=PK), xn3[:, :, PQ * p:PQ * p + PK])
            pool.tensor_copy(xpatch[:].rearrange("p r (y x) -> p r y x", x=PQ), xw).then_inc(S["win_ready"], 1)

        def pool_step(pool, i, att=True, mid=True, ffn=True, fin=True):
            if att:
                pool_windows(pool, i)
            if fin:
                wait(pool, "t_ready", i - 3)
                pool.wait_ge(S["t0g_kept"], i - 2)
                pool_copy(pool, t0f[:], t0g[:]).then_inc(S["t0f_kept"], 1)
            if ffn:
                wait(pool, "t0f_kept", i - 2)
                pool.wait_ge(S["t0_kept"], i - 1)
                pool_copy(pool, t0g[:], t0m[:]).then_inc(S["t0g_kept"], 1)
                pool.wait_ge(S["t0g_kept"], i - 1)
            if mid:
                wait(pool, "sin_in", 2 * (i - 1))
                pool.wait_ge(S["t0_ready"], 4 * i)
                pool_copy(pool, t0m[:], t0[:]).then_inc(S["t0_kept"], 1)

        def run(eng, step):
            step(eng, 0, mid=False, ffn=False, fin=False)
            step(eng, 1, ffn=False, fin=False)
            step(eng, 2, fin=False)
            with eng.Fori(3, NSTRIP) as i:
                step(eng, i)
            step(eng, NSTRIP, att=False)
            step(eng, NSTRIP + 1, att=False, mid=False)
            step(eng, NSTRIP + 2, att=False, mid=False, ffn=False)

        block = ctx.enter_context(nc.Block())

        @block.sync
        def _(sp):
            for i in range(4):
                sp_load(sp, i)
            with sp.Fori(3, NSTRIP - 1) as i:
                sp_load(sp, i + 1)
                sp_store(sp, i - 3)
            for k in range(NSTRIP - 4, NSTRIP):
                sp_store(sp, k)
            sp.wait_ge(S["u_stored"], 16 * 2 * NPAIR * NSTRIP)
            sp.wait_ge(S["tt_stored"], 16 * NSTRIP)

        @block.tensor
        def _(pe):
            run(pe, pe_step)

        @block.scalar
        def _(act):
            run(act, act_step)

        @block.vector
        def _(v):
            v.memset(qstack[:], 0.0).then_inc(S["stack_const"], 1)
            v.wait_ge(S["stack_const"], 1)
            v.memset(qstack[:, :, 0:Q_PARTS.count(0), NQB:], 1.0).then_inc(S["stack_const"], 1)
            v.wait_ge(S["stack_const"], 2)
            run(v, dve_step)

        @block.gpsimd
        def _(pool):
            pool.memset(one_cell[:], 1.0).then_inc(S["one"], 1)
            pool.wait_ge(S["one"], 1)
            run(pool, pool_step)


KF = 16
LAGS = 3
NMAT = LAGS + 2 * KF
PH = T // 2
BLK = PH // P
CH = 512
NCH = PH // CH
FRONT = 130
FLEN = FRONT + PH
F_SCALE = 1024.0
M_SCALE = 1024.0
TINY = 1.0e-30
NV = 4


def spectral_prepare(nc, ident, phi, sigma, m_u, m_plus, m_minus, log_weights, gumbel, filt, mats, mgain):
    with ExitStack() as ctx:
        def sb(name, shape, dt=F32):
            return ctx.enter_context(nc.sbuf_tensor("sp_" + name, shape, dt))

        phi_in = sb("phi", [P, T // P, KF])
        phiT = sb("phiT", [KF, T])
        fhl = sb("fhl", [KF, 2, 2, FLEN], F16)
        sig, pmax, inv, al, tm = (sb(n, [KF, 1]) for n in ("sig", "pmax", "inv", "al", "tm"))
        diag = sb("diag", [KF, KF])
        ones = sb("ones", [P, P])
        alpha = sb("alpha", [P, KF])
        zz = sb("zz", [P, 2, NV])
        z, e, ysoft, eq, cum, hard, wts = (sb(n, [P, NV]) for n in ("z", "e", "ysoft", "eq", "cum", "hard", "wts"))
        zs = sb("zs", [P, 4])
        pp = [sb(f"pp{n}", [P, 2, KF, P]) for n in range(2)]
        mu = [sb(f"mu{n}", [P, LAGS, P]) for n in range(2)]
        acc = sb("acc", [P, 2, KF, P])
        accu = sb("accu", [P, LAGS, P])
        mix = sb("mix", [P, NMAT, P])
        mhl = sb("mhl", [P, NMAT, 2, P], F16)
        mx = sb("mx", [P, 4])
        mrow = sb("mrow", [1, 2])
        ps = [ctx.enter_context(nc.psum_tensor(f"sp_ps{n}", [P, 512], F32)) for n in range(8)]
        names = "phi_in row_in phit filt_ready diag_ready alpha_ps z_ready e_ready mx_ready mxt mrow_ready gmax mhl_ready stored vch".split()
        S = {n: ctx.enter_context(nc.semaphore("sp_" + n)) for n in names}
        m_in = [ctx.enter_context(nc.semaphore(f"sp_m_in{n}")) for n in range(2)]
        block = ctx.enter_context(nc.Block())

        @block.sync
        def _(sp):
            sp.dma_start(phi_in[:], phi.rearrange("(n p) k -> p n k", p=P)).then_inc(S["phi_in"], 16)
            sp.dma_start(sig[:], sigma.rearrange("(k a) -> k a", a=1)).then_inc(S["row_in"], 16)
            sp.dma_start(zz[:, 0, :], log_weights.partition_broadcast(P)).then_inc(S["row_in"], 16)
            sp.dma_start(zz[:, 1, :], gumbel.partition_broadcast(P)).then_inc(S["row_in"], 16)

            def load(n):
                sp.dma_start(pp[n % 2][:, 0], m_plus[n].rearrange("k d e -> d k e")).then_inc(m_in[n % 2], 16)
                sp.dma_start(pp[n % 2][:, 1], m_minus[n].rearrange("k d e -> d k e")).then_inc(m_in[n % 2], 16)
                sp.dma_start(mu[n % 2][:], m_u[n].rearrange("k d e -> d k e")).then_inc(m_in[n % 2], 16)

            load(0)
            load(1)
            sp.wait_ge(S["filt_ready"], 1)
            sp.dma_start(filt.rearrange("k h r n -> k (h r n)"), fhl[:].rearrange("k h r n -> k (h r n)"))\
                .then_inc(S["stored"], 16)
            for n in range(NV):
                sp.wait_ge(S["mhl_ready"], n + 1)
                sp.dma_start(mats[n], mhl[:].rearrange("d m h e -> d (m h e)")).then_inc(S["stored"], 16)
                if n + 2 < NV:
                    load(n + 2)
            sp.wait_ge(S["stored"], 16 * (NV + 1))

        @block.tensor
        def _(pe):
            pe.wait_ge(S["phi_in"], 16)
            for n in range(T // P):
                mm = pe.transpose(ps[n // 4][0:KF, (n % 4) * P:(n % 4 + 1) * P], phi_in[:, n, :], ident[:])
            mm.then_inc(S["phit"], 1)
            pe.wait_ge(S["diag_ready"], 1)
            pe.matmul(ps[0][:, 0:KF], ones[0:KF, :], diag[:], start=True, stop=True).then_inc(S["alpha_ps"], 1)
            for n in range(NV):
                pe.wait_ge(S["mx_ready"], n + 1)
                pe.transpose(ps[1][0:1, 0:P], mx[:, 0:1], ident[:]).then_inc(S["mxt"], 1)
                pe.wait_ge(S["mrow_ready"], n + 1)
                pe.matmul(ps[2][:, 0:1], ones[0:1, :], mrow[0:1, 0:1], start=True, stop=True).then_inc(S["gmax"], 1)

        @block.scalar
        def _(act):
            act.wait_ge(S["z_ready"], 1)
            act.activation(e[:], z[:], ACT.Exp, bias=zs[:, 1:2], accum_out=zs[:, 2:3]).then_inc(S["e_ready"], 1)

        @block.vector
        def _(v):
            ch = Chain(v, S["vch"])
            ch.then(v.memset(ones[:], 1.0))
            ch.link(v.memset(fhl[:], 0.0))
            v.wait_ge(S["row_in"], 48)
            ch.link(v.tensor_tensor(z[:], zz[:, 0, :], zz[:, 1, :], ALU.add))
            ch.link(v.tensor_reduce(zs[:, 0:1], z[:], AX.X, ALU.max))
            v.tensor_scalar(zs[:, 1:2], zs[:, 0:1], -1.0, None, ALU.mult).then_inc(S["z_ready"], 1)
            v.wait_ge(S["e_ready"], 1)
            ch.link(v.reciprocal(zs[:, 3:4], zs[:, 2:3]))
            ch.link(v.tensor_scalar(ysoft[:], e[:], zs[:, 3:4], None, ALU.mult))
            ch.link(v.tensor_reduce(zs[:, 0:1], ysoft[:], AX.X, ALU.max))
            ch.link(v.tensor_scalar(eq[:], ysoft[:], zs[:, 0:1], None, ALU.is_equal))
            ch.link(v.tensor_copy(cum[:], eq[:]))
            for n in range(1, NV):
                ch.link(v.tensor_tensor(cum[:, n:n + 1], cum[:, n - 1:n], eq[:, n:n + 1], ALU.max))
            ch.then(v.tensor_copy(hard[:, 0:1], cum[:, 0:1]))
            ch.link(v.tensor_tensor(hard[:, 1:NV], cum[:, 1:NV], cum[:, 0:NV - 1], ALU.subtract))
            ch.link(v.tensor_tensor(hard[:], hard[:], ysoft[:], ALU.subtract))
            ch.link(v.tensor_tensor(wts[:], hard[:], ysoft[:], ALU.add))
            v.wait_ge(S["phit"], 1)
            for n in range(8):
                ch.then(v.tensor_copy(phiT[:, 512 * n:512 * n + 512], ps[n][0:KF, :]))
            ch.wait()
            ch.link(v.tensor_reduce(pmax[:], phiT[:], AX.X, ALU.max, apply_absolute_value=True))
            ch.link(v.tensor_scalar(pmax[:], pmax[:], TINY, None, ALU.max))
            ch.link(v.reciprocal(inv[:], pmax[:]))
            ch.link(v.tensor_scalar(phiT[:], phiT[:], inv[:, 0:1], F_SCALE, ALU.mult, ALU.mult))
            src = phiT[:].rearrange("k (n r) -> k r n", r=2)
            ch.link(v.tensor_copy(fhl[:, 0, :, FRONT:], src))
            v.tensor_tensor(fhl[:, 1, :, FRONT:], src, fhl[:, 0, :, FRONT:], ALU.subtract).then_inc(S["filt_ready"], 1)
            ch.link(v.tensor_copy(al[:], sig[:]))
            rsqrt(v, ch, inv[:], al[:], tm[:])
            rsqrt(v, ch, al[:], inv[:], tm[:])
            ch.link(v.tensor_tensor(al[:], al[:], pmax[:], ALU.mult))
            v.tensor_scalar(diag[:], ident[0:KF, 0:KF], al[:, 0:1], None, ALU.mult).then_inc(S["diag_ready"], 1)
            v.wait_ge(S["alpha_ps"], 1)
            ch.link(v.tensor_copy(alpha[:], ps[0][:, 0:KF]))
            albc = alpha[:].unsqueeze(2).to_broadcast([P, KF, P])
            even = mix[:, LAGS:].rearrange("d (k r) e -> d r k e", r=2)
            for n in range(NV):
                v.wait_ge(m_in[n % 2], 48 * (n // 2 + 1))
                w = wts[:, n:n + 1]
                a2, p2 = acc[:].rearrange("d s k e -> d (s k e)"), pp[n % 2][:].rearrange("d s k e -> d (s k e)")
                u2, m2 = accu[:].rearrange("d k e -> d (k e)"), mu[n % 2][:].rearrange("d k e -> d (k e)")
                if n == 0:
                    ch.then(v.tensor_scalar(a2, p2, w, None, ALU.mult))
                    ch.link(v.tensor_scalar(u2, m2, w, None, ALU.mult))
                else:
                    ch.then(v.scalar_tensor_tensor(out=a2, in0=p2, scalar=w, in1=a2, op0=ALU.mult, op1=ALU.add))
                    ch.link(v.scalar_tensor_tensor(out=u2, in0=m2, scalar=w, in1=u2, op0=ALU.mult, op1=ALU.add))
                ch.then(v.tensor_copy(mix[:, 0:LAGS, :], accu[:]))
                ch.then(v.tensor_tensor(even[:, 0], acc[:, 0], acc[:, 1], ALU.add))
                ch.link(v.tensor_tensor(even[:, 1], acc[:, 0], acc[:, 1], ALU.subtract))
                for r in range(2):
                    ch.link(v.tensor_tensor(even[:, r], even[:, r], albc, ALU.mult))
                v.tensor_reduce(mx[:, 0:1], mix[:].rearrange("d m e -> d (m e)"), AX.X, ALU.max,
                                apply_absolute_value=True).then_inc(S["mx_ready"], 1)
                v.wait_ge(S["mxt"], n + 1)
                v.tensor_reduce(mrow[0:1, 0:1], ps[1][0:1, 0:P], AX.X, ALU.max).then_inc(S["mrow_ready"], 1)
                v.wait_ge(S["gmax"], n + 1)
                ch.link(v.tensor_scalar(mx[:, 1:2], ps[2][:, 0:1], TINY, None, ALU.max))
                ch.link(v.reciprocal(mx[:, 2:3], mx[:, 1:2]))
                ch.then(v.tensor_scalar(mgain[:, n:n + 1], mx[:, 1:2], 1.0 / M_SCALE, None, ALU.mult))
                ch.link(v.tensor_scalar(mix[:], mix[:], mx[:, 2:3], M_SCALE, ALU.mult, ALU.mult))
                if n:
                    v.wait_ge(S["stored"], 16 * (n + 1))
                ch.link(v.tensor_copy(mhl[:, :, 0, :], mix[:]))
                v.tensor_tensor(mhl[:, :, 1, :], mix[:], mhl[:, :, 0, :], ALU.subtract).then_inc(S["mhl_ready"], 1)


def spectral(nc, u_dram, t_dram, filt, mats, mgain, out):
    with ExitStack() as ctx:
        def sb(name, shape, dt=F32):
            return ctx.enter_context(nc.sbuf_tensor("sc_" + name, shape, dt))

        u = sb("u", [P, 2, BLK, B, 2, P], F16)
        H = [sb(f"H{r}", [P, 2, PH], F16) for r in range(2)]
        Mx = [sb(f"M{n}", [P, NMAT, 2, P], F16) for n in range(2)]
        us = sb("us", [P, B, 2, CH], F16)
        tT = [sb(f"tT{n}", [P, B, 2 * CH]) for n in range(2)]
        shift = [sb(f"shift{n}", [P, 2 * P], F16) for n in range(2)]
        flip = sb("flip", [P, P], F16)
        psU = [ctx.enter_context(nc.psum_tensor(f"sc_psU{b}", [P, CH], F32)) for b in range(B)]
        psY = [ctx.enter_context(nc.psum_tensor(f"sc_psY{b}", [P, CH], F32)) for b in range(B)]
        names = "turned_ps turned_act turned_dve shifts conv_done hi_ready us_ready y_done y_read".split()
        S = {n: ctx.enter_context(nc.semaphore("sc_" + n)) for n in names}
        h_in = [ctx.enter_context(nc.semaphore(f"sc_h_in{r}")) for r in range(2)]
        u_in = [ctx.enter_context(nc.semaphore(f"sc_u_in{b}")) for b in range(B)]
        m_in = [ctx.enter_context(nc.semaphore(f"sc_m_in{r}")) for r in range(2)]
        banks = psU + psY
        t_in = [ctx.enter_context(nc.semaphore(f"sc_t_in{r}")) for r in range(2)]
        o_st = [ctx.enter_context(nc.semaphore(f"sc_o_st{r}")) for r in range(2)]
        jobs = [(c, p) for c in range(NCH) for p in range(2)]
        UNITS = B * NMAT
        spans = {0: [(3, 0, CH // 2), (2, CH // 2, CH)], 1: [(1, 0, CH)], 2: [(0, 0, CH)], 3: [(0, 0, CH)]}
        buf = {3: 0, 2: 1, 1: 0, 0: 1}
        mload = {3: 16, 2: 16, 1: 32, 0: 32}
        block = ctx.enter_context(nc.Block())

        NTURN = B * BLK // 2

        def turn(n):
            return n // BLK, n // (BLK // 2) % 2, 2 * (n % (BLK // 2))

        def half(p, r):
            return (p, 0) if r == 0 else (1 - p, 1 - p)

        @block.sync
        def _(sp):
            ub = u_dram.rearrange("(b r) n c -> b (r n) c", b=B)
            for b in range(B):
                for ph in range(2):
                    sp.dma_start(u[:, ph, :, b].rearrange("s k h d -> s k (h d)"),
                                 ub[b].rearrange("(k s q) c -> q s k c", q=2, s=P)[ph]).then_inc(u_in[b], 16)

            def load_m(mx_):
                sp.dma_start(Mx[buf[mx_]][:].rearrange("d m h e -> d (m h e)"), mats[mx_]).then_inc(m_in[buf[mx_]], 16)

            def load_t(c):
                for b in range(B):
                    for a in range(2):
                        sp.dma_start(tT[c % 2][:, b, CH * a:CH * a + CH],
                                     t_dram[b * STRIPS + 2 * c + a]).then_inc(t_in[c % 2], 16)

            def store(c):
                sp.wait_ge(S["y_read"], B * 2 * (c + 1))
                for b in range(B):
                    sp.dma_start(out[b].rearrange("e h w -> e (h w)")[:, 2 * CH * c:2 * CH * (c + 1)],
                                 tT[c % 2][:, b, :]).then_inc(o_st[c % 2], 16)

            load_m(3)
            load_m(2)
            for n, (c, p) in enumerate(jobs):
                L = CH * (c + 1)
                if p == 0:
                    if c >= 2:
                        sp.wait_ge(o_st[c % 2], 16 * B * (c // 2))
                    load_t(c)
                    if c in (1, 2):
                        sp.wait_ge(S["y_done"], 2 * B * c)
                        load_m(2 - c)

                def load_h(k, r):
                    _, sh = half(p, r)
                    a = filt[bass.ds(k, 1), 0, r, :]
                    src = bass.AP(tensor=a.tensor, offset=a.offset + (FRONT - sh - (P - 1)), ap=[[1, P], [2 * FLEN, 2], [1, L]])
                    sp.dma_start(H[r][:, :, 0:L], src).then_inc(h_in[r], 16)

                with sp.Fori(0, KF) as k:
                    for r in range(2):
                        sp.wait_ge(S["conv_done"], k * (2 * B) + (UNITS * n + LAGS * B - B * (1 - r)))
                        load_h(k, r)
                if p == 1:
                    store(c)
            for n in range(2):
                sp.wait_ge(o_st[n], 16 * B * NCH // 2)

        @block.gpsimd
        def _(pool):
            pool.memset(shift[0][:], 0.0).then_inc(S["shifts"], 1)
            pool.memset(shift[1][:], 0.0).then_inc(S["shifts"], 1)
            pool.memset(flip[:], 0.0).then_inc(S["shifts"], 1)
            pool.wait_ge(S["shifts"], 3)
            pool.affine_select(out=flip[:], in_=flip[:], compare_op=ALU.not_equal, fill=1.0,
                               base=-(P - 1), pattern=[[1, P]], channel_multiplier=1).then_inc(S["shifts"], 1)
            for n in range(2):
                pool.affine_select(out=shift[n][:], in_=shift[n][:], compare_op=ALU.not_equal, fill=F_SCALE,
                                   base=-(P - 1) - n, pattern=[[1, 2 * P]], channel_multiplier=1).then_inc(S["shifts"], 1)

        @block.tensor
        def _(pe):
            pe.wait_ge(S["shifts"], 6)
            for n in range(2 * NTURN):
                b, ph, k = turn(n)
                if k == 0 and ph == 0:
                    pe.wait_ge(u_in[b], 32)
                if n >= 8:
                    pe.wait_ge(S["turned_dve" if n % 2 else "turned_act"], (n - 8) // 2 + 1)
                pe.matmul(banks[n % 8][:], flip[:], u[:, ph, k:k + 2, b], start=True, stop=True)\
                    .then_inc(S["turned_ps"], 1)
            pe.wait_ge(S["turned_act"], NTURN)
            pe.wait_ge(S["turned_dve"], NTURN)

            def conv_free(unit):
                if not (isinstance(unit, int) and unit < 4):
                    pe.wait_ge(S["us_ready"], unit - 3)

            def conv_lag(c, p, lag, b, unit):
                conv_free(unit)
                ph, sh = (p, lag // 2) if lag != 1 else (1 - p, 1 - p)
                first = True
                for i in range(-1 if (sh and c) else 0, 4):
                    for hl in range(2):
                        lo = max(0, P * i)
                        hi = min(CH, P * i + P + (P if sh else 0))
                        mm = pe.matmul(psU[b][:, lo:hi], u[:, ph, 4 * c + i, b, hl, :],
                                       shift[sh][:, lo - P * i:hi - P * i], start=first, stop=False,
                                       skip_group_check=True)
                        first = False
                mm.then_inc(S["conv_done"], 1)

            def conv(c, p, r, b, unit):
                conv_free(unit)
                ph, _ = half(p, r)
                for s in range(4 * c + 4):
                    lo = max(0, P * (s - 4 * c))
                    x = CH * c - P * s + lo
                    for hu, hh in ((0, 0), (0, 1), (1, 0)):
                        mm = pe.matmul(psU[b][:, lo:CH], u[:, ph, s, b, hu, :], H[r][:, hh, x:x + CH - lo],
                                       start=(s == 0 and hu == 0 and hh == 0), stop=False, skip_group_check=True)
                mm.then_inc(S["conv_done"], 1)

            def project(c, slot, b, unit, first=False):
                pe.wait_ge(S["us_ready"], unit + 1)
                for mx_, lo, hi in spans[c]:
                    for hm, hu in ((0, 0), (1, 0), (0, 1)):
                        m = Mx[buf[mx_]][:, slot, hm, :] if isinstance(slot, int) else \
                            Mx[buf[mx_]][:, bass.ds(slot, 1), hm, :].rearrange("d a e -> d (a e)")
                        mm = pe.matmul(psY[b][:, lo:hi], m, us[:, b, hu, lo:hi],
                                       start=(first and lo == 0 and hm == 0 and hu == 0), stop=False,
                                       skip_group_check=True)
                return mm

            for n, (c, p) in enumerate(jobs):
                base = UNITS * n
                for mx_, _, _ in spans[c]:
                    pe.wait_ge(m_in[buf[mx_]], mload[mx_])
                queue = [(lag, b) for lag in range(LAGS) for b in range(B)]
                for q, (lag, b) in enumerate(queue):
                    conv_lag(c, p, lag, b, base + q)
                    if q >= 2:
                        if q == 2 and n:
                            pe.wait_ge(S["y_read"], B * n)
                        lg, bb = queue[q - 2]
                        project(c, lg, bb, base + q - 2, first=(lg == 0))
                with pe.Fori(0, KF) as k:
                    unit0 = k * (2 * B) + (base + LAGS * B)
                    for r in range(2):
                        pe.wait_ge(h_in[r], k * 16 + 16 * (KF * n + 1))
                        for b in range(B):
                            q = r * B + b
                            conv(c, p, r, b, unit0 + q)
                            if q < 2:
                                project(c, k * 2 + (LAGS - 1), B - 2 + q, unit0 + q - 2)
                            else:
                                project(c, k * 2 + (LAGS + (q - 2) // B), (q - 2) % B, unit0 + q - 2)
                for b in range(B - 2, B):
                    mm = project(c, NMAT - 1, b, base + UNITS - B + b)
                mm.then_inc(S["y_done"], B)

        @block.scalar
        def _(act):
            def hi(b, unit):
                act.wait_ge(S["conv_done"], unit + 1)
                act.activation(us[:, b, 0, :], psU[b][:], ACT.Copy, scale=1.0 / (U_SCALE * F_SCALE))\
                    .then_inc(S["hi_ready"], 1)

            for n in range(0, 2 * NTURN, 2):
                b, ph, k = turn(n)
                act.wait_ge(S["turned_ps"], n + 1)
                act.copy(u[:, ph, k:k + 2, b], banks[n % 8][:].rearrange("p (k h d) -> p k h d", k=2, h=2))\
                    .then_inc(S["turned_act"], 1)
            with act.Fori(0, len(jobs) * NMAT) as j:
                for b in range(B):
                    hi(b, j * B + b)

        @block.vector
        def _(v):
            def lo(b, unit):
                v.wait_ge(S["hi_ready"], unit + 1)
                v.scalar_tensor_tensor(out=us[:, b, 1, :], in0=psU[b][:], scalar=1.0 / (U_SCALE * F_SCALE),
                                       in1=us[:, b, 0, :], op0=ALU.mult, op1=ALU.subtract).then_inc(S["us_ready"], 1)

            for n in range(1, 2 * NTURN, 2):
                b, ph, k = turn(n)
                v.wait_ge(S["turned_ps"], n + 1)
                v.tensor_copy(u[:, ph, k:k + 2, b], banks[n % 8][:].rearrange("p (k h d) -> p k h d", k=2, h=2))\
                    .then_inc(S["turned_dve"], 1)
            for n, (c, p) in enumerate(jobs):
                with v.Fori(0, NMAT) as j:
                    for b in range(B):
                        lo(b, j * B + (b + UNITS * n))
                v.wait_ge(S["y_done"], B * (n + 1))
                v.wait_ge(t_in[c % 2], 16 * 2 * B * (c // 2 + 1))
                for b in range(B):
                    for mx_, a, z in spans[c]:
                        t2 = tT[c % 2][:, b, :].rearrange("e (m q) -> e q m", q=2)[:, p, a:z]
                        ins = v.scalar_tensor_tensor(out=t2, in0=psY[b][:, a:z], scalar=mgain[:, mx_:mx_ + 1], in1=t2,
                                                     op0=ALU.mult, op1=ALU.add)
                    ins.then_inc(S["y_read"], 1)


def program(nc, x, wq, wk, wv, rel_h, rel_w, theta, phi_ffn, w1, b1, w2, b2, g1, be1, g2, be2,
            sigma, phi, m_u, m_plus, m_minus, log_weights, gumbel, out):
    xn_strips = nc.dram_tensor("xn_strips", [NSTRIP, P, KROWS * KCOLS + STOK], F32, kind="Internal").ap()
    u_dram = nc.dram_tensor("u_dram", [NSTRIP, STOK, 2 * P], F16, kind="Internal").ap()
    t_dram = nc.dram_tensor("t_dram", [NSTRIP, P, STOK], F32, kind="Internal").ap()
    filt = nc.dram_tensor("filt", [KF, 2, 2, FLEN], F16, kind="Internal").ap()
    mats = nc.dram_tensor("mats", [NV, P, NMAT * 2 * P], F16, kind="Internal").ap()
    with ExitStack() as ctx:
        def sb(name, shape):
            return ctx.enter_context(nc.sbuf_tensor("k_" + name, shape, F32))

        ident, mgain = sb("ident", [P, P]), sb("mgain", [P, NV])
        with ExitStack() as inner:
            def si(name, shape, dt=F32):
                return inner.enter_context(nc.sbuf_tensor("k_" + name, shape, dt))

            pers = {"ident": ident, "halfpi": si("halfpi", [P, 1]), "wk": si("wk", [P, 2, P]),
                    "LA": si("LA", [P, PQ, P]), "LB": si("LB", [P, 16, P]), "wv": si("wv", [P, P]),
                    "hotA": si("hotA", [P, KROWS, KCOLS]), "hotB": si("hotB", [P, KROWS, KCOLS]),
                    "mask": si("mask", [P, KEYS]), "cosphi": si("cosphi", [P, NQB]),
                    "identb": si("identb", [P, P], BF16)}
            prepare(nc, pers, x, wq, wk, wv, rel_h, rel_w, phi_ffn, xn_strips)
            with ExitStack() as tctx:
                tok = {name: tctx.enter_context(nc.sbuf_tensor("k_" + name, shape, dt)) for name, shape, dt in (
                    ("theta", [P, P], F32), ("w1s", [KST, FF], BF16), ("w2T", [P, FT, P], F32),
                    ("qT", [KST, STOK], BF16), ("g1", [P, P], F32), ("be1", [P, P], F32), ("g2", [P, P], F32),
                    ("be2", [P, P], F32), ("b2", [P, P], F32))}
                load_token_weights(nc, tok, theta, w1, b1, w2, b2, g1, be1, g2, be2, ident, pers["identb"])
                strips(nc, pers, tok, xn_strips, u_dram, t_dram)
        spectral_prepare(nc, ident, phi, sigma, m_u, m_plus, m_minus, log_weights, gumbel, filt, mats, mgain)
        spectral(nc, u_dram, t_dram, filt, mats, mgain, out)


_INS = ['x', 'L0_conv_Wq', 'L0_conv_Wk', 'L0_conv_Wv', 'L0_conv_rel_h', 'L0_conv_rel_w',
        'L1_attn_theta_attn', 'L1_attn_phi_ffn', 'L1_attn_w1', 'L1_attn_b1', 'L1_attn_w2', 'L1_attn_b2',
        'L1_attn_gamma1', 'L1_attn_beta1', 'L1_attn_gamma2', 'L1_attn_beta2',
        'L1_ffn_sigma', 'L1_ffn_phi', 'L1_ffn_M_u', 'L1_ffn_M_phi_plus', 'L1_ffn_M_phi_minus',
        'L1_ffn_log_weights', 'L1_ffn_gumbel']
_OUTS = [((4, 128, 64, 64), 'float32')]


def kernel(**inputs):
    import numpy as _np
    import concourse.bacc as _bacc
    from concourse import mybir as _mybir
    from concourse.bass_utils import run_bass_kernel_spmd as _run

    nc = _bacc.Bacc("TRN2", target_bir_lowering=False, num_devices=1)
    arrays, args = {}, []
    for name in _INS:
        a = _np.ascontiguousarray(inputs[name])
        arrays[f"in_{name}_dram"] = a
        args.append(nc.dram_tensor(f"in_{name}_dram", a.shape, _mybir.dt.from_np(a.dtype), kind="ExternalInput").ap())
    for i, (shape, dtype) in enumerate(_OUTS):
        dt = _mybir.dt.from_np(_np.dtype(dtype))
        args.append(nc.dram_tensor(f"out_{i}_dram", shape, dt, kind="ExternalOutput").ap())
    program(nc, *args)
    r = _run(nc, [arrays], core_ids=[0])
    return r.results[0]["out_0_dram"]
```

```python
import concourse.bass as bass
from concourse import mybir
from contextlib import ExitStack
import math

F32 = mybir.dt.float32
F16 = mybir.dt.float16
BF16 = mybir.dt.bfloat16
I32 = mybir.dt.int32
ALU = mybir.AluOpType
ACT = mybir.ActivationFunctionType
AX = mybir.AxisListType

B, C, HH, WW = 4, 128, 64, 64
T = HH * WW
P = 128
WIN, PAD = 7, 3
HEADS, HC = 8, C // 8
ROWS = 8
STRIPS = HH // ROWS
NSTRIP = B * STRIPS
KROWS, KCOLS = ROWS + WIN - 1, WW + 2 * PAD
PQ = 8
PK = PQ + WIN - 1
KEYS = PK * PK
HALF = KEYS // 2
NPAIR = WW // (2 * PQ)
STOK = ROWS * WW
QH, NQB = 16, 8
FF = 2048
FT = FF // P
Q_PARTS, W_PARTS = (0, 0, 0, 1, 1, 2), (0, 1, 2, 0, 1, 0)
NST = len(Q_PARTS)
KST = NST * (NQB + 1)
NEG = -1.0e30
U_SCALE = 1024.0
TWO_PI = 2.0 * math.pi
TP1 = 6.28125
TP2 = TWO_PI - TP1
MAGIC = 1.5 * 2.0 ** 23
SIN_LO, SIN_HI = -1.5 * math.pi + 1e-6, 0.5 * math.pi - 1e-6


class Chain:

    def __init__(self, eng, sem, base=0):
        self.eng, self.sem, self.base, self.n = eng, sem, base, 0

    def then(self, ins):
        ins.then_inc(self.sem, 1)
        self.n += 1
        return self.n

    def link(self, ins):
        self.then(ins)
        self.eng.wait_ge(self.sem, self.base + self.n)

    def wait(self, n=None):
        self.eng.wait_ge(self.sem, self.base + (self.n if n is None else n))


def raw(ap, offset, dims):
    return bass.AP(tensor=ap.tensor, offset=ap.offset + offset, ap=dims)


def prepare(nc, pers, x, wq, wk, wv, rel_h, rel_w, phi_ffn, xn_strips):
    with ExitStack() as ctx:
        def sb(name, shape, dt=F32):
            return ctx.enter_context(nc.sbuf_tensor(name, shape, dt))

        def sem(name):
            return ctx.enter_context(nc.semaphore(name))

        xs = sb("pr_x", [P, B, T])
        xpad = [sb(f"pr_xpad{n}", [P, HH + 2 * PAD, KCOLS]) for n in range(2)]
        w_in = sb("pr_w", [P, 3, P])
        rel = sb("pr_rel", [P, WIN])
        gmask = sb("pr_gmask", [P, HEADS])
        relbd = sb("pr_relbd", [P, HEADS, WIN])
        gsum = sb("pr_gsum", [P, P])
        gsum_t = sb("pr_gsumt", [P, P])
        G = sb("pr_G", [P, HEADS, WIN])
        st = sb("pr_st", [P, B, 8, 6])
        mv = sb("pr_mv", [P, B, 2])
        gm = sb("pr_gm", [P, B])
        dd = sb("pr_dd", [P, B])
        var = sb("pr_var", [P, B])
        rs = sb("pr_rs", [P, B])
        ra = sb("pr_ra", [P, B])
        pidx = sb("pr_pidx", [P, 1], I32)
        pint = sb("pr_pint", [P, 4], I32)
        pf = sb("pr_pf", [P, 4])
        grid = sb("pr_grid", [P, KROWS, KCOLS])
        gridB = sb("pr_gridb", [P, KROWS, 5, 16])
        wgrid = sb("pr_wgrid", [P, 2, KEYS])
        wtmp = sb("pr_wtmp", [P, 3, KEYS])
        ph = sb("pr_ph", [P, 3, NQB])
        psT = ctx.enter_context(nc.psum_tensor("pr_psT", [P, 4, P], F32))
        psG = ctx.enter_context(nc.psum_tensor("pr_psG", [P, 512], F32))
        x_in = [sem(f"pr_x_in{b}") for b in range(B)]
        w_in_s, rel_in = sem("pr_w_in"), sem("pr_rel_in")
        consts, weights_t, g_done = sem("pr_consts"), sem("pr_weights_t"), sem("pr_g_done")
        relbd_ready, mean_ready, sq_ready = sem("pr_relbd"), sem("pr_mean"), sem("pr_sq")
        gstat, pad_ready, stored = sem("pr_gstat"), sem("pr_pad_ready"), [sem("pr_st0"), sem("pr_st1")]
        phi_in, dch, pch, cosd = sem("pr_phi_in"), sem("pr_dch"), sem("pr_pch"), sem("pr_cosd")
        phi_red = sem("pr_phi_red")
        block = ctx.enter_context(nc.Block())

        @block.sync
        def _(sp):
            sp.dma_start(w_in[:, 0, :], wq).then_inc(w_in_s, 16)
            sp.dma_start(w_in[:, 1, :], wk).then_inc(w_in_s, 16)
            sp.dma_start(w_in[:, 2, :], wv).then_inc(w_in_s, 16)
            half = C // 2
            sp.dma_start(rel[0:half, :], rel_h.rearrange("o a b k c -> o (a b k c)")).then_inc(rel_in, 16)
            sp.dma_start(rel[half:C, :], rel_w.rearrange("o a b c k -> o (a b c k)")).then_inc(rel_in, 16)
            for b in range(B):
                sp.dma_start(xs[:, b, :], x[b].rearrange("c h w -> c (h w)")).then_inc(x_in[b], 16)
            for b in range(B):
                sp.wait_ge(pad_ready, b + 1)
                flat = xpad[b % 2][:].rearrange("p h w -> p (h w)")
                for s in range(STRIPS):
                    a = s * ROWS * KCOLS
                    sp.dma_start(xn_strips[b * STRIPS + s, :, 0:KROWS * KCOLS],
                                 flat[:, a:a + KROWS * KCOLS]).then_inc(stored[b % 2], 16)
                sp.dma_start(xn_strips[b * STRIPS:(b + 1) * STRIPS, :, KROWS * KCOLS:].rearrange("s c n -> c s n"),
                             xs[:, b, :].rearrange("c (s n) -> c s n", n=STOK)).then_inc(stored[b % 2], 16)
            for n in range(2):
                sp.wait_ge(stored[n], 16 * (STRIPS + 1) * B // 2)

        @block.gpsimd
        def _(pool):
            ch = Chain(pool, pch)
            ident = pers["ident"]
            pool.dma_start(ph[:, 0, :], phi_ffn.partition_broadcast(P)).then_inc(phi_in, 16)
            ch.then(pool.memset(ident[:], 0.0))
            ch.then(pool.memset(gmask[:], 1.0))
            ch.then(pool.memset(gsum[:], 1.0 / 4))
            ch.then(pool.iota(pidx[:], pattern=[[0, 1]], base=0, channel_multiplier=1))
            ch.then(pool.iota(grid[:], pattern=[[1, KROWS], [0, KCOLS]], base=0, channel_multiplier=0,
                              allow_small_or_imprecise_dtypes=True))
            ch.then(pool.iota(gridB[:], pattern=[[0, KROWS], [0, 5], [1, 16]], base=0, channel_multiplier=0,
                              allow_small_or_imprecise_dtypes=True))
            ch.then(pool.iota(wgrid[:, 0, :], pattern=[[1, PK], [0, PK]], base=0, channel_multiplier=0,
                              allow_small_or_imprecise_dtypes=True))
            ch.link(pool.iota(wgrid[:, 1, :], pattern=[[0, PK], [1, PK]], base=0, channel_multiplier=0,
                              allow_small_or_imprecise_dtypes=True))
            ch.link(pool.affine_select(out=ident[:], in_=ident[:], compare_op=ALU.not_equal, fill=1.0,
                                       base=0, pattern=[[-1, P]], channel_multiplier=1))
            ch.link(pool.affine_select(out=gmask[:], in_=gmask[:], compare_op=ALU.is_ge, fill=0.0,
                                       base=0, pattern=[[-HC, HEADS]], channel_multiplier=1))
            ch.link(pool.affine_select(out=gmask[:], in_=gmask[:], compare_op=ALU.is_ge, fill=0.0,
                                       base=HC - 1, pattern=[[HC, HEADS]], channel_multiplier=-1))
            g4 = gsum[:].rearrange("p (g f) -> p g f", f=4)
            ch.link(pool.affine_select(out=g4, in_=g4, compare_op=ALU.is_ge, fill=0.0,
                                       base=0, pattern=[[-4, P // 4], [0, 4]], channel_multiplier=1))
            ch.link(pool.affine_select(out=g4, in_=g4, compare_op=ALU.is_ge, fill=0.0,
                                       base=3, pattern=[[4, P // 4], [0, 4]], channel_multiplier=-1))
            pool.memset(xpad[0][:], 0.0).then_inc(consts, 1)
            pool.memset(xpad[1][:], 0.0).then_inc(consts, 1)

        @block.tensor
        def _(pe):
            pe.wait_ge(pch, 13)
            pe.wait_ge(w_in_s, 48)
            for n in range(3):
                mm = pe.transpose(psT[:, n, :], w_in[:, n, :], pers["ident"][:])
            mm.then_inc(weights_t, 1)
            pe.wait_ge(relbd_ready, 1)
            pe.matmul(psG[:, 0:HEADS * WIN], w_in[:, 0, :], relbd[:].rearrange("p g k -> p (g k)"),
                      start=True, stop=True).then_inc(g_done, 1)
            pe.wait_ge(mean_ready, 1)
            pe.matmul(psT[:, 3, 0:B], gsum[:], gm[:], start=True, stop=True).then_inc(gstat, 1)
            pe.wait_ge(sq_ready, 1)
            pe.matmul(psT[:, 3, 8:8 + B], gsum[:], dd[:], start=True, stop=True).then_inc(gstat, 1)

        @block.scalar
        def _(act):
            act.wait_ge(phi_red, 1)
            act.activation(pers["cosphi"][:], ph[:, 2, :], ACT.Sin, bias=pers["halfpi"][:, 0:1]).then_inc(cosd, 1)

        @block.vector
        def _(v):
            ch = Chain(v, dch)
            ch.then(v.memset(pers["halfpi"][:], math.pi / 2))
            ch.then(v.memset(pers["wk"][:], 0.0))
            ch.then(v.memset(pers["LA"][:], 0.0))
            ch.link(v.memset(pers["LB"][:], 0.0))
            v.wait_ge(phi_in, 16)
            ch.link(v.tensor_scalar(ph[:, 1, :], ph[:, 0, :], 1.0 / TWO_PI, 0.25, ALU.mult, ALU.add))
            ch.link(v.tensor_scalar(ph[:, 1, :], ph[:, 1, :], MAGIC, MAGIC, ALU.add, ALU.subtract))
            ch.link(v.scalar_tensor_tensor(out=ph[:, 2, :], in0=ph[:, 1, :], scalar=-TP1, in1=ph[:, 0, :],
                                           op0=ALU.mult, op1=ALU.add))
            ch.link(v.scalar_tensor_tensor(out=ph[:, 2, :], in0=ph[:, 1, :], scalar=-TP2, in1=ph[:, 2, :],
                                           op0=ALU.mult, op1=ALU.add))
            v.tensor_scalar(ph[:, 2, :], ph[:, 2, :], SIN_LO, SIN_HI, ALU.max, ALU.min).then_inc(phi_red, 1)
            v.wait_ge(pch, 13)
            ch.then(v.tensor_copy(pers["identb"][:], pers["ident"][:]))
            for n, (sh, mask) in enumerate(((0, 31), (3, 7), (0, 7))):
                ch.then(v.tensor_scalar(pint[:, n:n + 1], pidx[:], sh, mask, ALU.logical_shift_right,
                                        ALU.bitwise_and))
            ch.wait()
            ch.link(v.tensor_copy(pf[:, 0:3], pint[:, 0:3]))
            ch.link(v.tensor_scalar(pf[:, 3:4], pf[:, 0:1], -16.0, None, ALU.add))
            ch.link(v.tensor_scalar(pers["hotA"][:], grid[:], pf[:, 3:4], None, ALU.is_equal))
            ch.link(v.tensor_scalar(pers["hotB"][:], gridB[:].rearrange("p y a c -> p y (a c)")[:, :, 0:KCOLS], pf[:, 3:4], None, ALU.is_equal))
            for n in range(2):
                ch.link(v.tensor_scalar(wtmp[:, 2, :], wgrid[:, n, :], pf[:, 1 + n:2 + n], None, ALU.subtract))
                ch.link(v.tensor_scalar(wtmp[:, n, :], wtmp[:, 2, :], 0.0, None, ALU.is_ge))
                ch.link(v.tensor_scalar(wtmp[:, 2, :], wtmp[:, 2, :], float(WIN - 1), None, ALU.is_le))
                ch.link(v.tensor_tensor(wtmp[:, n, :], wtmp[:, n, :], wtmp[:, 2, :], ALU.mult))
            ch.link(v.tensor_tensor(wtmp[:, 2, :], wtmp[:, 0, :], wtmp[:, 1, :], ALU.mult))
            ch.link(v.tensor_scalar(pers["mask"][:], wtmp[:, 2, :], -NEG, NEG, ALU.mult, ALU.add))
            v.wait_ge(rel_in, 32)
            for g in range(HEADS):
                ins = v.tensor_scalar(relbd[:, g, :], rel[:], gmask[:, g:g + 1], None, ALU.mult)
            ins.then_inc(relbd_ready, 1)
            v.wait_ge(weights_t, 1)
            for s in range(2):
                src = psT[:, :, s * 64:s * 64 + 64].rearrange("p n (j i) -> p n j i", i=HC)
                v.tensor_copy(pers["wk"][:, s, :].rearrange("p (j i) -> p j i", i=32)[:, :, 0:HC], src[:, 1])
                for y in range(PQ):
                    if s == 0:
                        v.tensor_copy(pers["LA"][:, y, :].rearrange("p (j i) -> p j i", i=32)[:, :, 0:HC], src[:, 0])
                for y in range(16):
                    if s == 1:
                        v.tensor_copy(pers["LB"][:, y, :].rearrange("p (j i) -> p j i", i=32)[:, :, 0:HC], src[:, 0])
            v.tensor_copy(pers["wv"][:], psT[:, 2, :])
            v.wait_ge(g_done, 1)
            ch.link(v.tensor_copy(G[:].rearrange("p g k -> p (g k)"), psG[:, 0:HEADS * WIN]))
            for y in range(PQ):
                v.tensor_copy(pers["LA"][:, y, :].rearrange("p (j i) -> p j i", i=32)[:, :, HC + y:HC + y + WIN],
                              G[:, 0:4, :])
            for c in range(16):
                dst = pers["LB"][:, c, :].rearrange("p (j i) -> p j i", i=32)
                n = min(WIN, 16 - c)
                v.tensor_copy(dst[:, :, HC + c:HC + c + n], G[:, 4:8, 0:n])
                if n < WIN:
                    v.tensor_copy(dst[:, :, HC:HC + WIN - n], G[:, 4:8, n:WIN])
            for b in range(B):
                v.wait_ge(x_in[b], 16)
                for k in range(8):
                    ch.then(v.bn_stats(st[:, b, k, :], xs[:, b, 512 * k:512 * k + 512]))
                ch.wait()
                ch.then(v.bn_aggr(mv[:, b, :], st[:, b, :, :]))
            ch.wait()
            v.tensor_copy(gm[:], mv[:, :, 0]).then_inc(mean_ready, 1)
            v.wait_ge(gstat, 1)
            ch.link(v.tensor_copy(gm[:], psT[:, 3, 0:B]))
            ch.link(v.tensor_tensor(ra[:], mv[:, :, 0], gm[:], ALU.subtract))
            ch.link(v.tensor_tensor(rs[:], ra[:], ra[:], ALU.mult))
            v.tensor_tensor(dd[:], rs[:], mv[:, :, 1], ALU.add).then_inc(sq_ready, 1)
            v.wait_ge(gstat, 2)
            ch.link(v.tensor_scalar(var[:], psT[:, 3, 8:8 + B], 1e-5, None, ALU.add))
            rsqrt(v, ch, rs[:], var[:], ra[:])
            for b in range(B):
                if b < 2:
                    v.wait_ge(consts, 2)
                else:
                    v.wait_ge(stored[b % 2], 16 * (STRIPS + 1) * (b // 2))
                v.tensor_scalar(xpad[b % 2][:, PAD:PAD + HH, PAD:PAD + WW],
                                xs[:, b, :].rearrange("p (h w) -> p h w", w=WW), gm[:, b:b + 1], rs[:, b:b + 1],
                                ALU.subtract, ALU.mult).then_inc(pad_ready, 1)


def rsqrt(v, ch, y, x, tmp, src=None, eps=0.0):
    if src is None:
        ch.link(v.tensor_scalar(tmp.bitcast(I32), x.bitcast(I32), 1, None, ALU.arith_shift_right))
        ch.then(v.tensor_scalar(x, x, -0.5, None, ALU.mult))
    else:
        ch.link(v.tensor_scalar(y, src, eps, None, ALU.add))
        ch.then(v.tensor_scalar(x, src, -0.5, -0.5 * eps, ALU.mult, ALU.add))
        ch.link(v.tensor_scalar(tmp.bitcast(I32), y.bitcast(I32), 1, None, ALU.arith_shift_right))
    ch.link(v.tensor_scalar(y.bitcast(I32), tmp.bitcast(I32), -1, 0x5F3759DF, ALU.mult, ALU.add))
    for _ in range(3):
        ch.link(v.tensor_tensor(tmp, y, y, ALU.mult))
        ch.link(v.tensor_tensor(tmp, tmp, x, ALU.mult))
        ch.link(v.scalar_tensor_tensor(out=y, in0=tmp, scalar=1.5, in1=y, op0=ALU.add, op1=ALU.mult))


def load_token_weights(nc, tok, theta, w1, b1, w2, b2, g1, be1, g2, be2, ident, identb):
    with ExitStack() as ctx:
        w1_in = ctx.enter_context(nc.sbuf_tensor("tw_w1", [P, FT, NQB + 1], F32))
        b1_in = ctx.enter_context(nc.sbuf_tensor("tw_b1", [FT, P], F32))
        rest = [ctx.enter_context(nc.sbuf_tensor(f"tw_rest{n}", [P, FT, NQB + 1], F32)) for n in range(2)]
        part = [ctx.enter_context(nc.sbuf_tensor(f"tw_part{n}", [P, FT, NQB + 1], BF16)) for n in range(3)]
        stack = ctx.enter_context(nc.sbuf_tensor("tw_stack", [P, FT, NST, NQB + 1], BF16))
        w2_in = ctx.enter_context(nc.sbuf_tensor("tw_w2", [P, FT, P], F32))
        th = ctx.enter_context(nc.sbuf_tensor("tw_th", [P, NQB], F32))
        ps = [ctx.enter_context(nc.psum_tensor(f"tw_ps{n}", [P, 4, P], F32)) for n in range(8)]
        rows_in, w1_s, w2_s, b1_s, b1t, split, stacked, w1t, w2t, done = (
            ctx.enter_context(nc.semaphore("tw_" + n))
            for n in ("rows_in", "w1_in", "w2_in", "b1_in", "b1t", "split", "stacked", "w1t", "w2t", "done"))
        block = ctx.enter_context(nc.Block())

        @block.sync
        def _(sp):
            sp.dma_start(w1_in[:, :, 0:NQB], w1.rearrange("(k p) q -> p k q", p=P)).then_inc(w1_s, 16)
            sp.dma_start(b1_in[:], b1.rearrange("(k p) -> k p", p=P)).then_inc(b1_s, 16)
            sp.dma_start(w2_in[:], w2.rearrange("e (k f) -> e k f", f=P)).then_inc(w2_s, 16)
            sp.dma_start(th[:], theta.partition_broadcast(P)).then_inc(rows_in, 16)
            for name, row in (("b2", b2), ("g1", g1), ("be1", be1), ("g2", g2), ("be2", be2)):
                sp.dma_start(tok[name][:], row.partition_broadcast(P)).then_inc(rows_in, 16)
            sp.wait_ge(rows_in, 16 * 6)

        @block.tensor
        def _(pe):
            pe.wait_ge(b1_s, 16)
            pe.transpose(ps[0][:, 0, 0:FT], b1_in[:], ident[0:FT, 0:FT]).then_inc(b1t, 1)
            pe.wait_ge(w2_s, 16)
            for k in range(FT):
                mm = pe.transpose(ps[4 + k // 4][:, k % 4, :], w2_in[:, k, :], ident[:])
            mm.then_inc(w2t, 1)
            pe.wait_ge(stacked, 1)
            for k in range(FT):
                mm = pe.matmul(ps[k // 4][0:KST, k % 4, :], stack[:, k].rearrange("p n q -> p (n q)"), identb[:],
                               start=True, stop=True)
            mm.then_inc(w1t, 1)

        @block.vector
        def _(v):
            ch = Chain(v, split)
            v.wait_ge(w1_s, 16)
            v.wait_ge(b1t, 1)
            ch.link(v.tensor_copy(w1_in[:, :, NQB], ps[0][:, 0, 0:FT]))
            three_parts(v, ch, w1_in[:], [t[:] for t in rest], [t[:] for t in part])
            for n, w in enumerate(W_PARTS):
                ins = v.tensor_copy(stack[:, :, n, :], part[w][:])
            ins.then_inc(stacked, 1)
            v.wait_ge(w2t, 1)
            for n in range(4):
                v.tensor_copy(tok["w2T"][:, 4 * n:4 * n + 4, :], ps[4 + n][:]).then_inc(done, 1)
            v.wait_ge(w1t, 1)
            for n in range(4):
                v.tensor_copy(tok["w1s"][:, 512 * n:512 * n + 512].rearrange("p (k f) -> p k f", f=P),
                              ps[n][0:KST, :, :]).then_inc(done, 1)
            v.wait_ge(rows_in, 16 * 6)
            v.tensor_copy(tok["theta"][:].rearrange("p (g j) -> p g j", j=NQB),
                          th[:].unsqueeze(1).to_broadcast([P, QH, NQB])).then_inc(done, 1)
            v.wait_ge(done, 9)


def three_parts(v, ch, src, rest, part):
    ch.link(v.tensor_copy(part[0], src))
    ch.link(v.tensor_tensor(rest[0], src, part[0], ALU.subtract))
    ch.link(v.tensor_copy(part[1], rest[0]))
    ch.link(v.tensor_tensor(rest[1], rest[0], part[1], ALU.subtract))
    ch.link(v.tensor_copy(part[2], rest[1]))


ATT_LINKS, MID_LINKS, FIN_LINKS = 4, 77, 53


def strips(nc, pers, tok, xn_strips, u_dram, t_dram):
    with ExitStack() as ctx:
        def sb(name, shape, dt=F32):
            return ctx.enter_context(nc.sbuf_tensor(name, shape, dt))

        def sem(name):
            return ctx.enter_context(nc.semaphore(name))

        NX = KROWS * KCOLS
        strip = sb("st_strip", [P, NX + STOK])
        xn3 = strip[:, 0:NX].rearrange("p (h w) -> p h w", w=KCOLS)
        xw = strip[:, NX:].rearrange("p (y r x) -> p r y x", y=ROWS, r=2 * NPAIR)
        xwin = sb("st_xwin", [P, 2 * NPAIR, KEYS])
        xpatch = sb("st_xpatch", [P, 2 * NPAIR, PQ * PQ])
        K = [sb(f"st_K{s}", [P, KROWS, KCOLS]) for s in range(2)]
        Q = [sb(f"st_Q{s}", [P, 2 * NPAIR, PQ * PQ]) for s in range(2)]
        V = sb("st_V", [HALF, 2 * 2 * NPAIR, P])
        Sm = [sb(f"st_Sm{s}", [P, 4, KEYS]) for s in range(2)]
        Pr = [sb(f"st_Pr{s}", [P, 4, KEYS]) for s in range(2)]
        nmax = [sb(f"st_nmax{s}", [P, 4]) for s in range(2)]
        den = [sb(f"st_den{s}", [P, HEADS]) for s in range(2)]
        rden = sb("st_rden", [P, HEADS])
        PT = [sb(f"st_PT{s}", [HALF, 8, P]) for s in range(2)]
        xt = sb("st_xt", [P, NPAIR, P])
        at = sb("st_at", [P, P])
        t0, t0m, t0g, t0f = (sb("st_" + n, [P, NPAIR, P]) for n in ("t0", "t0m", "t0g", "t0f"))
        n0, arg, turns, c, x1, x1b = (sb("st_" + n, [P, NPAIR, P]) for n in ("n0", "arg", "turns", "c", "x1", "x1b"))
        y, tt_sb = sb("st_y", [P, NPAIR, P]), sb("st_tt", [P, STOK])
        tfin = sb("st_tfin", [P, NPAIR, P])
        uhl = sb("st_uhl", [P, NPAIR, 2, P], F16)
        stm, stf = sb("st_stm", [P, NPAIR, 6]), sb("st_stf", [P, NPAIR, 6])
        mvm, mvf = sb("st_mvm", [P, NPAIR, 2]), sb("st_mvf", [P, NPAIR, 2])
        vm, vf = sb("st_vm", [P, 3, NPAIR]), sb("st_vf", [P, 3, NPAIR])
        fq = sb("st_fq", [P, 4, NPAIR, NQB])
        qrest = [sb(f"st_qrest{n}", [P, NPAIR, NQB]) for n in range(2)]
        qpart = [sb(f"st_qpart{n}", [P, NPAIR, NQB], BF16) for n in range(3)]
        qstack = sb("st_qstack", [P, NPAIR, NST, NQB + 1], BF16)
        cell, one_cell = sb("st_cell", [P, 1]), sb("st_one", [P, 1])
        h = sb("st_h", [P, FT, STOK])
        psS = [ctx.enter_context(nc.psum_tensor(f"st_psS{n}", [P, 512], F32)) for n in range(4)]
        psT = [ctx.enter_context(nc.psum_tensor(f"st_psT{n}", [P, 512], F32)) for n in range(2)]
        psO = ctx.enter_context(nc.psum_tensor("st_psO", [P, 512], F32))
        psF = ctx.enter_context(nc.psum_tensor("st_psF", [P, 512], F32))

        names = ("one win_ready strip_in k_ready q_ready v_ready xt_ready k_copied q_copied v_copied xt_copied "
                 "scores_ready scores_read probs_ready pt_ready pt_act pt_dve pv_done out_read t0_ready "
                 "t0_kept sin_in sin_out qf_ready qt_ready qt_copied h_ready relu_even relu_odd "
                 "ffn_done ffn_read x1b_kept t0g_kept stack_const t_ready tt_ready tt_copied tt_stored u_ready u_stored t0f_kept "
                 "ach mch fch").split()
        S = {n: sem("st_" + n) for n in names}

        def wait(eng, name, value):
            if not (isinstance(value, int) and value <= 0):
                eng.wait_ge(S[name], value)

        def gate(v, sem_, value):
            if not (isinstance(value, int) and value <= 0):
                v.wait_ge(sem_, value)
            if not isinstance(value, int):
                v.memset(cell[:], 0.0)

        def pool_copy(pool, out, in_):
            one = one_cell[:] if len(in_.shape) == 2 else one_cell[:].unsqueeze(1)
            return pool.tensor_tensor(out, in_, one.to_broadcast(list(in_.shape)), ALU.mult)

        def sp_load(sp, i):
            wait(sp, "q_ready", 2 * i)
            wait(sp, "win_ready", 1 * i)
            sp.dma_start(strip[:], xn_strips[bass.ds(i, 1)].rearrange("a c n -> (a c) n")).then_inc(S["strip_in"], 16)

        def sp_store(sp, i):
            sp.wait_ge(S["u_ready"], i + 1)
            for r in range(NPAIR):
                for q in range(2):
                    dst = u_dram[bass.ds(i, 1)].rearrange("a (y r q x) n -> (a r) q y x n", y=ROWS, r=NPAIR, q=2)
                    sp.dma_start(dst[r, q], uhl[64 * q:64 * q + 64, r].rearrange("p a b -> p (a b)"))\
                        .then_inc(S["u_stored"], 16)
            sp.wait_ge(S["tt_copied"], i + 1)
            sp.dma_start(t_dram[bass.ds(i, 1)].rearrange("a c n -> (a c) n"),
                         tt_sb[:]).then_inc(S["tt_stored"], 16)

        def pe_keys(pe, i):
            pe.wait_ge(S["strip_in"], 16 * (i + 1))
            wait(pe, "scores_read", 8 * i)
            flat = strip[:, 0:NX]
            for s in range(2):
                for n in range(2):
                    mm = pe.matmul(psS[2 * s + n][:, 0:NX // 2], pers["wk"][:, s, :],
                                   flat[:, n * NX // 2:(n + 1) * NX // 2], start=True, stop=True)
                mm.then_inc(S["k_ready"], 1)

        def pe_project(pe, i, ffn):
            wait(pe, "pt_dve", 8 * i)
            qb = psT[1][:].rearrange("p (y a m) -> p m y a", y=ROWS, m=16)
            for m in range(16):
                mm = pe.matmul(qb[:, m], pers["LB"][:, m, :], xn3[:, PAD:PAD + ROWS, PAD + m:PAD + m + 49:16],
                               start=True, stop=True)
            mm.then_inc(S["q_ready"], 1)
            wait(pe, "pt_act", 8 * i)
            for y_ in range(ROWS):
                mm = pe.matmul(psT[0][:, 64 * y_:64 * y_ + 64], pers["LA"][:, y_, :],
                               xn3[:, PAD + y_, PAD:PAD + WW], start=True, stop=True)
            mm.then_inc(S["q_ready"], 1)
            for w in range(2 * 2 * NPAIR):
                p, hf = w // 2, w % 2
                if w == 0:
                    pe.wait_ge(S["win_ready"], i + 1)
                if w % 4 == 0:
                    pe.wait_ge(S["k_copied"], 2 * i + 1 + (w >= 8))
                mm = pe.matmul(psS[w // 4][0:HALF, (w % 4) * P:(w % 4 + 1) * P],
                               xwin[:, p, HALF * hf:HALF * hf + HALF], pers["wv"][:], start=True, stop=True)
                if w % 4 == 3:
                    mm.then_inc(S["v_ready"], 1)
            if ffn:
                pe_qt(pe, i - 2, True, i)
            pe.wait_ge(S["q_copied"], 2 * (i + 1))
            for r in range(NPAIR):
                mm = pe.transpose(psT[0][:, r * P:(r + 1) * P], xpatch[:, 2 * r:2 * r + 2, :].rearrange("p q n -> p (q n)"),
                                  pers["ident"][:])
            mm.then_inc(S["xt_ready"], 1)

        def pe_scores(pe, i, u):
            r, s = u // 2, u % 2
            if u == 0:
                pe.wait_ge(S["q_copied"], 2 * (i + 1))
                pe.wait_ge(S["v_copied"], 4 * (i + 1))
            else:
                pe.wait_ge(S["scores_read"], 8 * i + u)
            for q in range(2):
                col = PQ * (2 * r + q)
                for j in range(4):
                    mm = pe.matmul(psS[j][64 * q:64 * q + 64, 0:KEYS],
                                   Q[s][32 * j:32 * j + 32, 2 * r + q, :], K[s][32 * j:32 * j + 32, :, col:col + PK],
                                   start=True, stop=True)
            mm.then_inc(S["scores_ready"], 1)

        def pe_turn(pe, i, u, ffn):
            pe.wait_ge(S["probs_ready"], 8 * i + u + 1)
            if ffn:
                pe.wait_ge(S["relu_even"], 8 * (i - 2) + u + 1)
                pe.wait_ge(S["relu_odd"], 8 * (i - 2) + u + 1)
            elif u:
                pe.wait_ge(S["pt_act"], 8 * i + u)
                pe.wait_ge(S["pt_dve"], 8 * i + u)
            else:
                pe.wait_ge(S["xt_copied"], i + 1)
            for j in range(4):
                for hf in range(2):
                    mm = pe.transpose(psT[j // 2][0:HALF, (2 * (j % 2) + hf) * P:(2 * (j % 2) + hf + 1) * P],
                                      Pr[u % 2][:, j, HALF * hf:HALF * hf + HALF], pers["ident"][:])
            mm.then_inc(S["pt_ready"], 1)

        def pe_values(pe, i, u):
            r, s = u // 2, u % 2
            pe.wait_ge(S["pt_act"], 8 * i + u + 1)
            pe.wait_ge(S["pt_dve"], 8 * i + u + 1)
            if s == 0:
                wait(pe, "out_read", 4 * i + r)
            for j in range(4):
                g = 4 * s + j
                for q in range(2):
                    for hf in range(2):
                        mm = pe.matmul(psO[64 * q:64 * q + 64, HC * g:HC * g + HC],
                                       PT[s][:, 2 * j + hf, 64 * q:64 * q + 64],
                                       V[:, 2 * (2 * r + q) + hf, HC * g:HC * g + HC],
                                       start=(hf == 0), stop=(hf == 1))
            mm.then_inc(S["pv_done"], 1)

        def pe_back(pe, k):
            pe.wait_ge(S["t_ready"], k + 1)
            for r in range(NPAIR):
                mm = pe.transpose(psF[:, r * P:(r + 1) * P], tfin[:, r, :], pers["ident"][:])
            mm.then_inc(S["tt_ready"], 1)

        def pe_qt(pe, k, att, i=None):
            pe.wait_ge(S["qf_ready"], k + 1)
            if att:
                pe.wait_ge(S["q_copied"], 2 * i + 1)
            else:
                pe.wait_ge(S["pt_dve"], 8 * NSTRIP)
                pe.wait_ge(S["relu_odd"], 8 * k)
            for r in range(NPAIR):
                mm = pe.matmul(psT[1][0:KST, r * P:(r + 1) * P], qstack[:, r].rearrange("p n q -> p (n q)"),
                               pers["identb"][:], start=True, stop=True)
            mm.then_inc(S["qt_ready"], 1)

        def pe_hidden(pe, i, k, u, att):
            if u == 0:
                pe.wait_ge(S["qt_copied"], k + 1)
                if att:
                    pe.wait_ge(S["xt_copied"], i + 1)
                else:
                    pe.wait_ge(S["pt_act"], 8 * NSTRIP)
                    pe.wait_ge(S["relu_even"], 8 * k)
            for n in range(2):
                if u:
                    if att:
                        pe.wait_ge(S[("pt_act", "pt_dve")[n]], 8 * i + u)
                    else:
                        pe.wait_ge(S[("relu_even", "relu_odd")[n]], 8 * k + u)
                f = 2 * u + n
                pe.matmul(psT[n][:], tok["w1s"][:, P * f:P * f + P], tok["qT"][:], start=True, stop=True)\
                    .then_inc(S["h_ready"], 1)

        def pe_output(pe, k, w):
            if w == 0:
                wait(pe, "tt_copied", k)
            for n in range(2):
                f = 2 * w + n
                pe.wait_ge(S[("relu_even", "relu_odd")[n]], 8 * k + w + 1)
                for r in range(NPAIR):
                    mm = pe.matmul(psF[:, r * P:(r + 1) * P], h[:, f, r * P:(r + 1) * P], tok["w2T"][:, f, :],
                                   start=(f == 0 and r == 0), stop=(f == FT - 1), skip_group_check=True)
            if w == 7:
                mm.then_inc(S["ffn_done"], 1)

        def pe_step(pe, i, att=True, mid=True, ffn=True, fin=True, more=True):
            if att:
                pe_project(pe, i, ffn)
            elif ffn:
                pe_qt(pe, i - 2, False)
            for u in range(10):
                if att and u < 8:
                    pe_scores(pe, i, u)
                if att and 1 <= u <= 8:
                    pe_turn(pe, i, u - 1, ffn)
                if fin and u == 1:
                    pe_back(pe, i - 3)
                if ffn and u >= 3:
                    if u == 3:
                        pe_output(pe, i - 2, 0)
                    pe_output(pe, i - 2, u - 2)
                if more and u == 9:
                    pe_keys(pe, i + 1)
                if att and u >= 2:
                    pe_values(pe, i, u - 2)
                if ffn and u < 8:
                    pe_hidden(pe, i, i - 2, u, att)

        def act_copies(act, i):
            for n in (1, 0):
                act.wait_ge(S["q_ready"], 2 * i + 2 - n)
                wait(act, "scores_ready", 8 * i)
                act.copy(Q[n][:].rearrange("p r (y x) -> p r y x", x=PQ),
                         psT[n][:].rearrange("p (y r x) -> p r y x", y=ROWS, x=PQ)).then_inc(S["q_copied"], 1)
            wait(act, "pv_done", 8 * i)
            for n in range(4):
                act.wait_ge(S["v_ready"], 4 * i + n + 1)
                act.copy(V[:, 4 * n:4 * n + 4, :].rearrange("p w c -> p (w c)"), psS[n][0:HALF, :])\
                    .then_inc(S["v_copied"], 1)
            act.wait_ge(S["xt_ready"], i + 1)
            wait(act, "t0_ready", 4 * i)
            act.copy(xt[:].rearrange("p r c -> p (r c)"), psT[0][:]).then_inc(S["xt_copied"], 1)

        def act_exp(act, i, u):
            r, s = u // 2, u % 2
            act.wait_ge(S["scores_read"], 8 * i + u + 1)
            wait(act, "pt_ready", 8 * i + u - 1)
            if s == 0:
                wait(act, "out_read", 4 * i + r - 1)
            for j in range(4):
                ins = act.activation(Pr[s][:, j, :], Sm[s][:, j, :], ACT.Exp, scale=-1.0, bias=nmax[s][:, j:j + 1],
                                     accum_out=den[r % 2][:, 4 * s + j:4 * s + j + 1])
            ins.then_inc(S["probs_ready"], 1)

        def act_pt(act, i, u):
            act.wait_ge(S["pt_ready"], 8 * i + u + 1)
            wait(act, "pv_done", 8 * i + u - 1)
            act.copy(PT[u % 2][:, 0:4, :].rearrange("p w c -> p (w c)"), psT[0][0:HALF, :]).then_inc(S["pt_act"], 1)

        def act_sin(act, k, n):
            act.wait_ge(S["sin_in"], 2 * k + n + 1)
            if n == 0:
                act.activation(c[:], arg[:], ACT.Sin, bias=pers["halfpi"][:, 0:1]).then_inc(S["sin_out"], 1)
            else:
                act.activation(fq[:, 2], fq[:, 1], ACT.Sin, bias=pers["halfpi"][:, 0:1]).then_inc(S["sin_out"], 1)

        def act_tt(act, k):
            act.wait_ge(S["tt_ready"], k + 1)
            wait(act, "tt_stored", 16 * k)
            act.copy(tt_sb[:].rearrange("p (y r x) -> p r y x", y=ROWS, x=PQ),
                     psF[:].rearrange("p (r y x) -> p r y x", y=PQ, x=PQ)).then_inc(S["tt_copied"], 1)

        def act_relu(act, k, u):
            act.wait_ge(S["h_ready"], FT * k + 2 * u + 1)
            if u == 0:
                wait(act, "ffn_done", k)
            act.activation(h[:, 2 * u, :], psT[0][:], ACT.Relu).then_inc(S["relu_even"], 1)
            act.wait_ge(S["h_ready"], FT * k + 2 * u + 2)
            act.activation(h[:, 2 * u + 1, :], psT[1][:], ACT.Relu).then_inc(S["relu_odd"], 1)

        def act_step(act, i, att=True, mid=True, ffn=True, fin=True, more=True):
            if att:
                act_copies(act, i)
            for u in range(9):
                if att and u < 8:
                    act_exp(act, i, u)
                if att and u >= 1:
                    act_pt(act, i, u - 1)
                if fin and u == 1:
                    act_tt(act, i - 3)
                if ffn and u < 8:
                    act_relu(act, i - 2, u)
                if mid and u == 4:
                    act_sin(act, i - 1, 0)
                if mid and u == 7:
                    act_sin(act, i - 1, 1)

        def norm_stats(v, ch, src, st, mv):
            for r in range(NPAIR):
                ch.then(v.bn_stats(st[:, r, :], src[:, r, :]))
            gate(v, ch.sem, ch.base + ch.n)
            for r in range(NPAIR):
                ch.then(v.bn_aggr(mv[:, r, :], st[:, r, :].rearrange("p (a s) -> p a s", a=1)))
            ch.wait()

        def norm_apply(v, ch, src, dst, mv, vv):
            rsqrt(v, ch, vv[:, 1, :], vv[:, 0, :], vv[:, 2, :], src=mv[:, :, 1], eps=1e-5)
            for r in range(NPAIR):
                ch.then(v.tensor_scalar(dst[:, r, :], src[:, r, :], mv[:, r, 0:1], vv[:, 1, r:r + 1],
                                        ALU.subtract, ALU.mult))
            ch.wait()

        def whole_turns(v, ch, src, turns_, dst):
            ch.link(v.tensor_scalar(turns_, src, 1.0 / TWO_PI, 0.25, ALU.mult, ALU.add))
            ch.link(v.tensor_scalar(turns_, turns_, MAGIC, MAGIC, ALU.add, ALU.subtract))
            ch.link(v.scalar_tensor_tensor(out=src, in0=turns_, scalar=-TP1, in1=src, op0=ALU.mult, op1=ALU.add))
            ch.link(v.scalar_tensor_tensor(out=src, in0=turns_, scalar=-TP2, in1=src, op0=ALU.mult, op1=ALU.add))
            return v.tensor_scalar(dst, src, SIN_LO, SIN_HI, ALU.max, ALU.min)

        def rows(name):
            return tok[name][:].unsqueeze(1).to_broadcast([P, NPAIR, P])

        def flat(t):
            return t[:].rearrange("p r c -> p (r c)")

        def dve_keys(v, i):
            wait(v, "scores_ready", 8 * i)
            for s in range(2):
                v.wait_ge(S["k_ready"], 2 * i + s + 1)
                kf, hot = K[s][:].rearrange("p h w -> p (h w)"), pers["hot" + "AB"[s]][:].rearrange("p h w -> p (h w)")
                for n in range(2):
                    a, b = n * NX // 2, (n + 1) * NX // 2
                    ins = v.tensor_tensor(kf[:, a:b], psS[2 * s + n][:, 0:NX // 2], hot[:, a:b], ALU.add)
                ins.then_inc(S["k_copied"], 1)

        def dve_max(v, i, u):
            s = u % 2
            wait(v, "probs_ready", 8 * i + u - 1)
            gate(v, S["scores_ready"], 8 * i + u + 1)
            for j in range(4):
                ins = v.tensor_tensor_reduce(Sm[s][:, j, :], psS[j][:, 0:KEYS],
                                             pers["mask"][:], -1.0, 3.0e38, ALU.add, ALU.min, nmax[s][:, j:j + 1])
            ins.then_inc(S["scores_read"], 1)

        def dve_pt(v, i, u):
            v.wait_ge(S["pt_ready"], 8 * i + u + 1)
            wait(v, "pv_done", 8 * i + u - 1)
            v.tensor_copy(PT[u % 2][:, 4:8, :].rearrange("p w c -> p (w c)"), psT[1][0:HALF, :]).then_inc(S["pt_dve"], 1)

        def dve_out(v, ch, i, r):
            ch.link(v.reciprocal(rden[:], den[r % 2][:]))
            v.wait_ge(S["pv_done"], 8 * i + 2 * r + 2)
            v.tensor_tensor(at[:].rearrange("p (g c) -> p g c", c=HC), psO[:, 0:P].rearrange("p (g c) -> p g c", c=HC),
                            rden[:].unsqueeze(2).to_broadcast([P, HEADS, HC]), ALU.mult).then_inc(S["out_read"], 1)
            v.wait_ge(S["out_read"], 4 * i + r + 1)
            if r == 0:
                v.wait_ge(S["xt_copied"], i + 1)
                wait(v, "t0_kept", i)
            v.tensor_tensor(t0[:, r, :], at[:], xt[:, r, :], ALU.add).then_inc(S["t0_ready"], 1)

        def dve_mid1(v, ch, k):
            v.wait_ge(S["t0_kept"], k + 1)
            norm_stats(v, ch, t0m, stm, mvm)

        def dve_mid1b(v, ch, k):
            norm_apply(v, ch, t0m, n0, mvm, vm)

        def dve_mid2(v, ch, k):
            ch.link(v.tensor_tensor(turns[:], n0[:], rows("theta"), ALU.add))
            whole_turns(v, ch, turns[:], c[:], arg[:]).then_inc(S["sin_in"], 1)

        def dve_mid3(v, ch, k):
            v.wait_ge(S["sin_out"], 2 * k + 1)
            c8, n8 = c[:].rearrange("p r (g j) -> p (r g) j", j=NQB), n0[:].rearrange("p r (g j) -> p (r g) j", j=NQB)
            s8 = arg[:].rearrange("p r (g j) -> p (r g) j", j=NQB)
            for j in range(1, NQB):
                ch.link(v.tensor_tensor(c8[:, :, j], c8[:, :, j - 1], c8[:, :, j], ALU.mult))
            ch.then(v.tensor_tensor(s8[:, :, 1:], n8[:, :, 1:], c8[:, :, 1:], ALU.add))
            ch.link(v.tensor_tensor(s8[:, :, 0], n8[:, :, 0], c8[:, :, NQB - 1], ALU.add))

        def dve_mid4(v, ch, k):
            norm_stats(v, ch, arg, stm, mvm)

        def dve_mid4b(v, ch, k):
            norm_apply(v, ch, arg, x1, mvm, vm)

        def dve_mid5(v, ch, k):
            ch.link(v.tensor_tensor(x1[:], x1[:], rows("g1"), ALU.mult))
            ch.link(v.tensor_tensor(x1[:], x1[:], rows("be1"), ALU.add))
            ch.link(v.tensor_copy(fq[:, 0], x1[:, :, 0:NQB]))
            whole_turns(v, ch, fq[:, 0], fq[:, 2], fq[:, 1]).then_inc(S["sin_in"], 1)

        def dve_mid6(v, ch, k):
            v.wait_ge(S["sin_out"], 2 * k + 2)
            ch.link(v.tensor_tensor(fq[:, 3], fq[:, 2], pers["cosphi"][:].unsqueeze(1).to_broadcast([P, NPAIR, NQB]),
                                    ALU.mult))
            three_parts(v, ch, fq[:, 3], [t[:] for t in qrest], [t[:] for t in qpart])
            wait(v, "qt_ready", k)
            for n in range(NST):
                ins = v.tensor_copy(qstack[:, :, n, 0:NQB], qpart[Q_PARTS[n]][:])
            ins.then_inc(S["qf_ready"], 1)

        def dve_qt(v, k):
            v.wait_ge(S["qt_ready"], k + 1)
            v.tensor_copy(tok["qT"][:], psT[1][0:KST, :]).then_inc(S["qt_copied"], 1)

        def dve_fin1(v, k):
            v.wait_ge(S["ffn_done"], k + 1)
            wait(v, "u_ready", k)
            v.tensor_tensor(flat(y), psF[:], flat(x1b), ALU.add).then_inc(S["ffn_read"], 1)
            v.wait_ge(S["ffn_read"], k + 1)

        def dve_keep_x1b(v, k):
            v.tensor_tensor(x1b[:], x1[:], rows("b2"), ALU.add).then_inc(S["x1b_kept"], 1)
            v.wait_ge(S["x1b_kept"], k + 1)

        def dve_fin2(v, ch, k):
            norm_stats(v, ch, y, stf, mvf)

        def dve_fin2b(v, ch, k):
            norm_apply(v, ch, y, y, mvf, vf)

        def dve_fin3(v, ch, k):
            ch.link(v.tensor_tensor(y[:], y[:], rows("g2"), ALU.mult))
            ch.link(v.tensor_tensor(y[:], y[:], rows("be2"), ALU.add))
            v.wait_ge(S["t0f_kept"], k + 1)
            wait(v, "tt_ready", k)
            v.tensor_tensor(tfin[:], y[:], t0f[:], ALU.add).then_inc(S["t_ready"], 1)
            v.wait_ge(S["t_ready"], k + 1)

        def dve_fin4(v, ch, k):
            norm_stats(v, ch, tfin, stf, mvf)

        def dve_fin4b(v, ch, k):
            norm_apply(v, ch, tfin, y, mvf, vf)

        def dve_fin5(v, ch, k):
            wait(v, "u_stored", 16 * 2 * NPAIR * k)
            ch.link(v.tensor_scalar(uhl[:, :, 0, :], y[:], U_SCALE, None, ALU.mult))
            v.scalar_tensor_tensor(out=uhl[:, :, 1, :], in0=y[:], scalar=U_SCALE, in1=uhl[:, :, 0, :],
                                   op0=ALU.mult, op1=ALU.subtract).then_inc(S["u_ready"], 1)

        def dve_step(v, i, att=True, mid=True, ffn=True, fin=True, more=True):
            ach = Chain(v, S["ach"], ATT_LINKS * i)
            mch = Chain(v, S["mch"], MID_LINKS * (i - 1))
            fch = Chain(v, S["fch"], FIN_LINKS * (i - 3))
            if fin:
                dve_fin1(v, i - 3)
            if ffn:
                dve_keep_x1b(v, i - 2)
            if fin:
                dve_fin2(v, fch, i - 3)
                dve_fin2b(v, fch, i - 3)
                dve_fin3(v, fch, i - 3)
            if ffn:
                dve_qt(v, i - 2)
            for u in range(10):
                if att and u < 8:
                    dve_max(v, i, u)
                if att and 1 <= u <= 8:
                    dve_pt(v, i, u - 1)
                if mid and u == 0:
                    dve_mid1(v, mch, i - 1)
                if mid and u == 2:
                    dve_mid1b(v, mch, i - 1)
                if fin and u == 3:
                    dve_fin4b(v, fch, i - 3)
                if mid and u == 4:
                    dve_mid2(v, mch, i - 1)
                if mid and u == 5:
                    dve_mid3(v, mch, i - 1)
                if mid and u == 6:
                    dve_mid4(v, mch, i - 1)
                    dve_mid4b(v, mch, i - 1)
                if mid and u == 7:
                    dve_mid5(v, mch, i - 1)
                if mid and u == 8:
                    dve_mid6(v, mch, i - 1)
                if more and u == 9:
                    dve_keys(v, i + 1)
                if att and u >= 3 and u % 2 == 1:
                    dve_out(v, ach, i, (u - 3) // 2)
                if fin and u == 2:
                    dve_fin4(v, fch, i - 3)
                if fin and u == 3:
                    dve_fin5(v, fch, i - 3)
            assert (not att or ach.n == ATT_LINKS) and (not mid or mch.n == MID_LINKS) and \
                (not fin or fch.n == FIN_LINKS), (ach.n, mch.n, fch.n)

        def pool_windows(pool, i):
            wait(pool, "v_ready", 4 * i)
            wait(pool, "xt_ready", 1 * i)
            pool.wait_ge(S["strip_in"], 16 * (i + 1))
            for p in range(2 * NPAIR):
                copy = pool.tensor_copy if p else lambda out, in_: pool_copy(pool, out, in_)
                copy(xwin[:, p, :].rearrange("p (a b) -> p a b", a=PK), xn3[:, :, PQ * p:PQ * p + PK])
            pool.tensor_copy(xpatch[:].rearrange("p r (y x) -> p r y x", x=PQ), xw).then_inc(S["win_ready"], 1)

        def pool_step(pool, i, att=True, mid=True, ffn=True, fin=True, more=True):
            if att:
                pool_windows(pool, i)
            if fin:
                wait(pool, "t_ready", i - 3)
                pool.wait_ge(S["t0g_kept"], i - 2)
                pool_copy(pool, t0f[:], t0g[:]).then_inc(S["t0f_kept"], 1)
            if ffn:
                wait(pool, "t0f_kept", i - 2)
                pool.wait_ge(S["t0_kept"], i - 1)
                pool_copy(pool, t0g[:], t0m[:]).then_inc(S["t0g_kept"], 1)
                pool.wait_ge(S["t0g_kept"], i - 1)
            if mid:
                wait(pool, "sin_in", 2 * (i - 1))
                pool.wait_ge(S["t0_ready"], 4 * i)
                pool_copy(pool, t0m[:], t0[:]).then_inc(S["t0_kept"], 1)

        def run(eng, step):
            step(eng, 0, mid=False, ffn=False, fin=False)
            step(eng, 1, ffn=False, fin=False)
            step(eng, 2, fin=False)
            with eng.Fori(3, NSTRIP - 1) as i:
                step(eng, i)
            step(eng, NSTRIP - 1, more=False)
            step(eng, NSTRIP, att=False, more=False)
            step(eng, NSTRIP + 1, att=False, mid=False, more=False)
            step(eng, NSTRIP + 2, att=False, mid=False, ffn=False, more=False)

        block = ctx.enter_context(nc.Block())

        @block.sync
        def _(sp):
            for i in range(4):
                sp_load(sp, i)
            with sp.Fori(3, NSTRIP - 1) as i:
                sp_load(sp, i + 1)
                sp_store(sp, i - 3)
            for k in range(NSTRIP - 4, NSTRIP):
                sp_store(sp, k)
            sp.wait_ge(S["u_stored"], 16 * 2 * NPAIR * NSTRIP)
            sp.wait_ge(S["tt_stored"], 16 * NSTRIP)

        @block.tensor
        def _(pe):
            pe_keys(pe, 0)
            run(pe, pe_step)

        @block.scalar
        def _(act):
            run(act, act_step)

        @block.vector
        def _(v):
            v.memset(qstack[:], 0.0).then_inc(S["stack_const"], 1)
            v.wait_ge(S["stack_const"], 1)
            v.memset(qstack[:, :, 0:Q_PARTS.count(0), NQB:], 1.0).then_inc(S["stack_const"], 1)
            v.wait_ge(S["stack_const"], 2)
            dve_keys(v, 0)
            run(v, dve_step)

        @block.gpsimd
        def _(pool):
            pool.memset(one_cell[:], 1.0).then_inc(S["one"], 1)
            pool.wait_ge(S["one"], 1)
            run(pool, pool_step)


KF = 16
LAGS = 3
NMAT = LAGS + 2 * KF
PH = T // 2
BLK = PH // P
CH = 512
NCH = PH // CH
P_BLKS = CH // P
FRONT = 130
FLEN = FRONT + PH
F_SCALE = 1024.0
M_SCALE = 1024.0
TINY = 1.0e-30
HC2 = CH // 2
WINDOWS = (("d", 1, 0), ("d", -1, CH), ("e", 1, 0), ("e", -1, HC2), ("e", -1, CH), ("e", 1, CH + HC2),
           ("g", 1, CH), ("g", -1, CH + HC2), ("g", 1, 0), ("g", -1, HC2))
NWIN, WLEN = len(WINDOWS), 512
WSB = WLEN - P
NV = 4


def spectral_prepare(nc, ident, phi, sigma, m_u, m_plus, m_minus, log_weights, gumbel, filt, wins, mats, mgain):
    with ExitStack() as ctx:
        def sb(name, shape, dt=F32):
            return ctx.enter_context(nc.sbuf_tensor("sp_" + name, shape, dt))

        phi_in = sb("phi", [P, T // P, KF])
        phiT = sb("phiT", [KF, T])
        fhl = sb("fhl", [KF, 2, 2, FLEN], F16)
        dif = {n: sb("dif_" + n, [KF, 2, size]) for n, size in (("g", PH - HC2), ("d", 2 * CH), ("e", 5 * HC2))}
        whl = sb("whl", [KF, 2, 2, NWIN, WLEN], F16)
        sig, pmax, inv, al, tm = (sb(n, [KF, 1]) for n in ("sig", "pmax", "inv", "al", "tm"))
        diag = sb("diag", [KF, KF])
        ones = sb("ones", [P, P])
        alpha = sb("alpha", [P, KF])
        zz = sb("zz", [P, 2, NV])
        z, e, ysoft, eq, cum, hard, wts = (sb(n, [P, NV]) for n in ("z", "e", "ysoft", "eq", "cum", "hard", "wts"))
        zs = sb("zs", [P, 4])
        pp = [sb(f"pp{n}", [P, 2, KF, P]) for n in range(2)]
        mu = [sb(f"mu{n}", [P, LAGS, P]) for n in range(2)]
        acc = sb("acc", [P, 2, KF, P])
        accu = sb("accu", [P, LAGS, P])
        mix = sb("mix", [P, NMAT, P])
        mhl = sb("mhl", [P, NMAT, 2, P], F16)
        mx = sb("mx", [P, 4])
        mrow = sb("mrow", [1, 2])
        ps = [ctx.enter_context(nc.psum_tensor(f"sp_ps{n}", [P, 512], F32)) for n in range(8)]
        names = "pp_scaled f_scaled f_hi difs win_hi alpha_ready m_scaled acc_done m_hi phi_in row_in phit filt_ready win_ready diag_ready alpha_ps z_ready e_ready mx_ready mxt mrow_ready gmax mhl_ready stored vch".split()
        S = {n: ctx.enter_context(nc.semaphore("sp_" + n)) for n in names}
        m_in = [ctx.enter_context(nc.semaphore(f"sp_m_in{n}")) for n in range(2)]
        MHALF = ((0, NMAT // 2), (NMAT // 2, NMAT))
        block = ctx.enter_context(nc.Block())

        @block.sync
        def _(sp):
            sp.dma_start(phi_in[:], phi.rearrange("(n p) k -> p n k", p=P)).then_inc(S["phi_in"], 16)
            sp.dma_start(sig[:], sigma.rearrange("(k a) -> k a", a=1)).then_inc(S["row_in"], 16)
            sp.dma_start(zz[:, 0, :], log_weights.partition_broadcast(P)).then_inc(S["row_in"], 16)
            sp.dma_start(zz[:, 1, :], gumbel.partition_broadcast(P)).then_inc(S["row_in"], 16)

            def load(n):
                sp.dma_start(pp[n % 2][:, 0], m_plus[n].rearrange("k d e -> d k e")).then_inc(m_in[n % 2], 16)
                sp.dma_start(pp[n % 2][:, 1], m_minus[n].rearrange("k d e -> d k e")).then_inc(m_in[n % 2], 16)
                sp.dma_start(mu[n % 2][:], m_u[n].rearrange("k d e -> d k e")).then_inc(m_in[n % 2], 16)

            load(0)
            load(1)
            sp.wait_ge(S["filt_ready"], 1)
            sp.dma_start(filt.rearrange("k h r n -> k (h r n)"), fhl[:].rearrange("k h r n -> k (h r n)"))\
                .then_inc(S["stored"], 16)
            sp.wait_ge(S["win_ready"], 1)
            sp.dma_start(wins.rearrange("k r h w n -> k (r h w n)"), whl[:].rearrange("k r h w n -> k (r h w n)"))\
                .then_inc(S["stored"], 16)
            for n in range(NV):
                sp.wait_ge(S["mhl_ready"], n + 1)
                sp.dma_start(mats[n], mhl[:].rearrange("d m h e -> d (m h e)")).then_inc(S["stored"], 16)
                if n + 2 < NV:
                    sp.wait_ge(S["acc_done"], n + 1)
                    load(n + 2)
            sp.wait_ge(S["stored"], 16 * (NV + 2))

        @block.tensor
        def _(pe):
            pe.wait_ge(S["phi_in"], 16)
            for n in range(T // P):
                mm = pe.transpose(ps[n // 4][0:KF, (n % 4) * P:(n % 4 + 1) * P], phi_in[:, n, :], ident[:])
            mm.then_inc(S["phit"], 1)
            pe.wait_ge(S["diag_ready"], 1)
            pe.matmul(ps[0][:, 0:KF], ones[0:KF, :], diag[:], start=True, stop=True).then_inc(S["alpha_ps"], 1)
            for n in range(NV):
                pe.wait_ge(S["mx_ready"], n + 1)
                pe.transpose(ps[1][0:1, 0:P], mx[:, 0:1], ident[:]).then_inc(S["mxt"], 1)
                pe.wait_ge(S["mrow_ready"], n + 1)
                pe.matmul(ps[2][:, 0:1], ones[0:1, :], mrow[0:1, 0:1], start=True, stop=True).then_inc(S["gmax"], 1)

        @block.scalar
        def _(act):
            act.wait_ge(S["z_ready"], 1)
            act.activation(e[:], z[:], ACT.Exp, bias=zs[:, 1:2], accum_out=zs[:, 2:3]).then_inc(S["e_ready"], 1)
            act.wait_ge(S["f_scaled"], 1)
            act.copy(fhl[:, 0, :, FRONT:], phiT[:].rearrange("k (n r) -> k r n", r=2)).then_inc(S["f_hi"], 1)
            act.wait_ge(S["difs"], 3)
            for n, (which, sign, first) in enumerate(WINDOWS):
                act.activation(whl[:, :, 0, n, :], dif[which][:, :, first:first + WLEN], ACT.Copy,
                               scale=float(sign)).then_inc(S["win_hi"], 1)
            for n in range(NV):
                act.wait_ge(S["m_scaled"], n + 1)
                if n:
                    act.wait_ge(S["stored"], 16 * (n + 2))
                for a, z_ in MHALF:
                    act.copy(mhl[:, a:z_, 0, :], mix[:, a:z_, :]).then_inc(S["m_hi"], 1)

        @block.gpsimd
        def _(pool):
            pool.wait_ge(S["alpha_ready"], 1)
            for n in range(NV):
                pool.wait_ge(m_in[n % 2], 48 * (n // 2 + 1))
                for s_ in range(2):
                    pool.tensor_tensor(pp[n % 2][:, s_], pp[n % 2][:, s_], alpha[:].unsqueeze(2).to_broadcast([P, KF, P]),
                                       ALU.mult).then_inc(S["pp_scaled"], 1)

        @block.vector
        def _(v):
            ch = Chain(v, S["vch"])
            ch.then(v.memset(ones[:], 1.0))
            ch.link(v.memset(fhl[:], 0.0))
            v.wait_ge(S["row_in"], 48)
            ch.link(v.tensor_tensor(z[:], zz[:, 0, :], zz[:, 1, :], ALU.add))
            ch.link(v.tensor_reduce(zs[:, 0:1], z[:], AX.X, ALU.max))
            v.tensor_scalar(zs[:, 1:2], zs[:, 0:1], -1.0, None, ALU.mult).then_inc(S["z_ready"], 1)
            v.wait_ge(S["e_ready"], 1)
            ch.link(v.reciprocal(zs[:, 3:4], zs[:, 2:3]))
            ch.link(v.tensor_scalar(ysoft[:], e[:], zs[:, 3:4], None, ALU.mult))
            ch.link(v.tensor_reduce(zs[:, 0:1], ysoft[:], AX.X, ALU.max))
            ch.link(v.tensor_scalar(eq[:], ysoft[:], zs[:, 0:1], None, ALU.is_equal))
            ch.link(v.tensor_copy(cum[:], eq[:]))
            for n in range(1, NV):
                ch.link(v.tensor_tensor(cum[:, n:n + 1], cum[:, n - 1:n], eq[:, n:n + 1], ALU.max))
            ch.then(v.tensor_copy(hard[:, 0:1], cum[:, 0:1]))
            ch.link(v.tensor_tensor(hard[:, 1:NV], cum[:, 1:NV], cum[:, 0:NV - 1], ALU.subtract))
            ch.link(v.tensor_tensor(hard[:], hard[:], ysoft[:], ALU.subtract))
            ch.link(v.tensor_tensor(wts[:], hard[:], ysoft[:], ALU.add))
            v.wait_ge(S["phit"], 1)
            for n in range(8):
                ch.then(v.tensor_copy(phiT[:, 512 * n:512 * n + 512], ps[n][0:KF, :]))
            ch.wait()
            ch.link(v.tensor_reduce(pmax[:], phiT[:], AX.X, ALU.max, apply_absolute_value=True))
            ch.link(v.tensor_scalar(pmax[:], pmax[:], TINY, None, ALU.max))
            ch.link(v.reciprocal(inv[:], pmax[:]))
            ch.link(v.tensor_scalar(phiT[:], phiT[:], inv[:, 0:1], F_SCALE, ALU.mult, ALU.mult))
            v.tensor_copy(al[:], sig[:]).then_inc(S["f_scaled"], 1)
            v.wait_ge(S["f_scaled"], 1)
            rsqrt(v, ch, inv[:], al[:], tm[:])
            rsqrt(v, ch, al[:], inv[:], tm[:])
            ch.link(v.tensor_tensor(al[:], al[:], pmax[:], ALU.mult))
            v.tensor_scalar(diag[:], ident[0:KF, 0:KF], al[:, 0:1], None, ALU.mult).then_inc(S["diag_ready"], 1)
            v.wait_ge(S["alpha_ps"], 1)
            v.tensor_copy(alpha[:], ps[0][:, 0:KF]).then_inc(S["alpha_ready"], 1)
            src = phiT[:].rearrange("k (n r) -> k r n", r=2)
            g, d, e_ = (dif[n][:] for n in "gde")
            v.tensor_tensor(g, src[:, :, 0:PH - HC2], src[:, :, HC2:], ALU.subtract).then_inc(S["difs"], 1)
            v.tensor_tensor(d, src[:, :, HC2:HC2 + 2 * CH], src[:, :, HC2 + CH:HC2 + 3 * CH], ALU.subtract)\
                .then_inc(S["difs"], 1)
            v.wait_ge(S["difs"], 1)
            v.tensor_tensor(e_, g[:, :, 0:5 * HC2], g[:, :, CH:CH + 5 * HC2], ALU.subtract).then_inc(S["difs"], 1)
            v.wait_ge(S["difs"], 3)
            v.wait_ge(S["f_hi"], 1)
            v.tensor_tensor(fhl[:, 1, :, FRONT:], src, fhl[:, 0, :, FRONT:], ALU.subtract).then_inc(S["filt_ready"], 1)
            for n, (which, sign, first) in enumerate(WINDOWS):
                v.wait_ge(S["win_hi"], n + 1)
                ins = v.scalar_tensor_tensor(out=whl[:, :, 1, n, :], in0=dif[which][:, :, first:first + WLEN],
                                             scalar=float(sign), in1=whl[:, :, 0, n, :], op0=ALU.mult,
                                             op1=ALU.subtract)
            ins.then_inc(S["win_ready"], 1)
            even = mix[:, LAGS:].rearrange("d (k r) e -> d r k e", r=2)

            def accumulate(n):
                v.wait_ge(S["pp_scaled"], 2 * n + 2)
                w = wts[:, n:n + 1]
                a2, p2 = acc[:].rearrange("d s k e -> d (s k e)"), pp[n % 2][:].rearrange("d s k e -> d (s k e)")
                u2, m2 = accu[:].rearrange("d k e -> d (k e)"), mu[n % 2][:].rearrange("d k e -> d (k e)")
                if n == 0:
                    ch.then(v.tensor_scalar(a2, p2, w, None, ALU.mult))
                    v.tensor_scalar(u2, m2, w, None, ALU.mult).then_inc(S["acc_done"], 1)
                else:
                    ch.then(v.scalar_tensor_tensor(out=a2, in0=p2, scalar=w, in1=a2, op0=ALU.mult, op1=ALU.add))
                    v.scalar_tensor_tensor(out=u2, in0=m2, scalar=w, in1=u2, op0=ALU.mult, op1=ALU.add)\
                        .then_inc(S["acc_done"], 1)
                ch.wait()
                v.wait_ge(S["acc_done"], n + 1)

            accumulate(0)
            for n in range(NV):
                ch.then(v.tensor_copy(mix[:, 0:LAGS, :], accu[:]))
                ch.then(v.tensor_tensor(even[:, 0], acc[:, 0], acc[:, 1], ALU.add))
                ch.link(v.tensor_tensor(even[:, 1], acc[:, 0], acc[:, 1], ALU.subtract))
                v.tensor_reduce(mx[:, 0:1], mix[:].rearrange("d m e -> d (m e)"), AX.X, ALU.max,
                                apply_absolute_value=True).then_inc(S["mx_ready"], 1)
                if n + 1 < NV:
                    accumulate(n + 1)
                v.wait_ge(S["mxt"], n + 1)
                v.tensor_reduce(mrow[0:1, 0:1], ps[1][0:1, 0:P], AX.X, ALU.max).then_inc(S["mrow_ready"], 1)
                v.wait_ge(S["gmax"], n + 1)
                ch.link(v.tensor_scalar(mx[:, 1:2], ps[2][:, 0:1], TINY, None, ALU.max))
                ch.link(v.reciprocal(mx[:, 2:3], mx[:, 1:2]))
                ch.then(v.tensor_scalar(mgain[:, n:n + 1], mx[:, 1:2], 1.0 / M_SCALE, None, ALU.mult))
                v.tensor_scalar(mix[:], mix[:], mx[:, 2:3], M_SCALE, ALU.mult, ALU.mult).then_inc(S["m_scaled"], 1)
                v.wait_ge(S["m_scaled"], n + 1)
                for h_, (a, z_) in enumerate(MHALF):
                    v.wait_ge(S["m_hi"], 2 * n + h_ + 1)
                    ins = v.tensor_tensor(mhl[:, a:z_, 1, :], mix[:, a:z_, :], mhl[:, a:z_, 0, :], ALU.subtract)
                    ch.then(ins) if h_ == 0 else ins.then_inc(S["mhl_ready"], 1)
                ch.wait()
                v.wait_ge(S["mhl_ready"], n + 1)


def shifts_and_flip(pool, done, shift, flip):
    pool.memset(shift[0][:], 0.0).then_inc(done, 1)
    pool.memset(shift[1][:], 0.0).then_inc(done, 1)
    pool.memset(flip[:], 0.0).then_inc(done, 1)
    pool.wait_ge(done, 3)
    pool.affine_select(out=flip[:], in_=flip[:], compare_op=ALU.not_equal, fill=1.0,
                       base=-(P - 1), pattern=[[1, P]], channel_multiplier=1).then_inc(done, 1)
    for n in range(2):
        pool.affine_select(out=shift[n][:], in_=shift[n][:], compare_op=ALU.not_equal, fill=F_SCALE,
                           base=-(P - 1) - n, pattern=[[1, 2 * P]], channel_multiplier=1).then_inc(done, 1)


def spectral_half(nc, upper, u_dram, t_dram, filt, wins, mats, mgain, out):
    tag = "up_" if upper else "lo_"
    with ExitStack() as ctx:
        def sb(name, shape, dt=F32):
            return ctx.enter_context(nc.sbuf_tensor(tag + name, shape, dt))

        NB2, NC2 = 2, 2
        C0 = NCH // 2 if upper else 0
        NBLK = P_BLKS * (C0 + NC2)
        halves = range(C0 + 1)
        SUMS = ([(j, P_BLKS + j) for j in range(P_BLKS)] if upper else []) + \
            [(P_BLKS * c + j, P_BLKS * c + 2 + j) for c in halves for j in range(2)] + \
            ([(j, 2 + j, P_BLKS + j, P_BLKS + 2 + j) for j in range(2)] if upper else [])
        HSUM = P_BLKS if upper else 0
        W0, NW = (0, NWIN) if upper else (NWIN - 2, 2)
        NF = 3 * CH if upper else 3 * HC2
        spans = [[(0, 0, CH)], [(0, 0, CH)]] if upper else [[(3, 0, HC2), (2, HC2, CH)], [(1, 0, CH)]]
        mixes = sorted({m for sp_ in spans for m, _, _ in sp_})
        u = sb("u", [P, 2, NBLK, NB2, 2, P], F16)
        us_sum = sb("us_sum", [P, 2, len(SUMS), NB2, 2, P], F16)
        Hf = [sb(f"Hf{r}", [P, 2, NF], F16) for r in range(2)]
        Hw = [sb(f"Hw{r}", [P, 2, NW, WSB], F16) for r in range(2)]
        H_DMAS = 2 if upper else 3
        Mx = {m: sb(f"M{m}", [P, NMAT, 2, P], F16) for m in mixes}
        E_sb, C_sb, EC_sb = sb("E", [P, CH]), sb("C", [P, NC2, HC2]), sb("EC", [P, HC2])
        Y_sb = sb("Y", [P, NC2, CH])
        us = sb("us", [P, NB2, NC2, 2, CH], F16)
        tT = sb("tT", [P, NB2, 4 * CH])
        shift = [sb(f"shift{n}", [P, 2 * P], F16) for n in range(2)]
        flip = sb("flip", [P, P], F16)
        psE, psC, psU0, psU1 = (ctx.enter_context(nc.psum_tensor(tag + "ps" + n, [P, CH], F32)) for n in ("E", "C", "U0", "U1"))
        psU = [psU0, psU1]
        psY = [[ctx.enter_context(nc.psum_tensor(f"{tag}psY{b}{c}", [P, CH], F32)) for c in range(NC2)] for b in range(NB2)]
        banks = [psE, psC, psU0, psU1] + psY[0] + psY[1]
        names = ("e_done e_copied c_done c_total shifts sum_ps sum_hi sum_done turned_ps turned_act turned_dve ec_done ec_copied conv_done added "
                 "total_ready hi_ready us_ready y_done y_read m_in t_in o_st u_in").split()
        S = {n: ctx.enter_context(nc.semaphore(tag + n)) for n in names}
        h_in = [ctx.enter_context(nc.semaphore(f"{tag}h_in{r}")) for r in range(2)]
        jobs = [(bh, p) for bh in range(B // NB2) for p in range(2)]
        UNITS = NB2 * NMAT
        FUNITS = NB2 * 2 * KF
        NSUM = 2 * len(SUMS) // 2
        NTURN = NB2 * NBLK
        block = ctx.enter_context(nc.Block())

        def half(p, r):
            return (p, 0) if r == 0 else (1 - p, 1 - p)

        def turn(n):
            return n // NBLK, n // (NBLK // 2) % 2, 2 * (n % (NBLK // 2))

        def summed(n):
            return n // (NSUM // 2), 2 * (n % (NSUM // 2))

        @block.sync
        def _(sp):
            ub = u_dram.rearrange("(b r) n c -> b (r n) c", b=B)
            for n, (bh, p) in enumerate(jobs):
                if p == 0:
                    if n:
                        sp.wait_ge(S["conv_done"], 2 * UNITS * n)
                    for b in range(NB2):
                        for ph in range(2):
                            sp.dma_start(u[:, ph, :, b].rearrange("s k h d -> s k (h d)"),
                                         ub[NB2 * bh + b].rearrange("(k s q) c -> q s k c", q=2, s=P)[ph, :, 0:NBLK])\
                                .then_inc(S["u_in"], 16)
                    if n == 0:
                        for m in mixes:
                            sp.dma_start(Mx[m][:].rearrange("d m h e -> d (m h e)"), mats[m]).then_inc(S["m_in"], 16)

                def load_h(k, r):
                    _, sh = half(p, r)
                    a = filt[bass.ds(k, 1), 0, r, :]
                    sp.dma_start(Hf[r][:], bass.AP(tensor=a.tensor, offset=a.offset + (FRONT - sh - (P - 1)),
                                                   ap=[[1, P], [2 * FLEN, 2], [1, NF]])).then_inc(h_in[r], 16)
                    at = CH - P - (P - 1) - sh - HC2
                    if upper:
                        a = wins[bass.ds(k, 1), r, 0, 0, :]
                        sp.dma_start(Hw[r][:].rearrange("p h w x -> p (h w) x"),
                                     bass.AP(tensor=a.tensor, offset=a.offset + at,
                                             ap=[[1, P], [WLEN, 2 * NWIN], [1, WSB]])).then_inc(h_in[r], 16)
                    else:
                        for hl in range(2):
                            a = wins[bass.ds(k, 1), r, hl, W0, :]
                            sp.dma_start(Hw[r][:, hl], bass.AP(tensor=a.tensor, offset=a.offset + at,
                                                               ap=[[1, P], [WLEN, NW], [1, WSB]])).then_inc(h_in[r], 16)

                for r in range(2):
                    if n:
                        sp.wait_ge(S["conv_done"], 2 * (UNITS * n - NB2 * (1 - r)))
                    load_h(0, r)
                if p == 0:
                    if n:
                        sp.wait_ge(S["o_st"], 16 * NB2 * bh)
                    for b in range(NB2):
                        for a in range(4):
                            sp.dma_start(tT[:, b, CH * a:CH * a + CH],
                                         t_dram[(NB2 * bh + b) * STRIPS + 2 * C0 + a]).then_inc(S["t_in"], 16)
                with sp.Fori(1, KF) as k:
                    for r in range(2):
                        sp.wait_ge(S["conv_done"], k * (2 * 2 * NB2) +
                                   2 * (UNITS * n + LAGS * NB2 - NB2 * (1 - r)))
                        load_h(k, r)
                if p == 1:
                    sp.wait_ge(S["y_read"], NB2 * 2 * (bh + 1))
                    for b in range(NB2):
                        sp.dma_start(out[NB2 * bh + b].rearrange("e h w -> e (h w)")[:, 2 * CH * C0:2 * CH * (C0 + NC2)], tT[:, b, :])\
                            .then_inc(S["o_st"], 16)
            sp.wait_ge(S["o_st"], 16 * B)

        @block.gpsimd
        def _(pool):
            shifts_and_flip(pool, S["shifts"], shift, flip)

        @block.tensor
        def _(pe):
            pe.wait_ge(S["shifts"], 6)

            def turn_blocks(bh):
                pe.wait_ge(S["u_in"], 16 * 2 * NB2 * (bh + 1))
                if bh:
                    pe.wait_ge(S["y_read"], 2 * NB2 * bh)
                for n in range(NSUM):
                    ph, j = summed(n)
                    if n >= 8:
                        pe.wait_ge(S["sum_done"], bh * NSUM + n - 7)
                    for m, (src, hl) in enumerate([(a, hl) for a in range(len(SUMS[j])) for hl in range(2)]):
                        for q in range(2):
                            mm = pe.matmul(banks[n % 8][:, q * HC2:(q + 1) * HC2], flip[:],
                                           u[:, ph, SUMS[j + q][src], :, hl],
                                           start=(m == 0 and q == 0), stop=False, skip_group_check=True)
                    mm.then_inc(S["sum_ps"], 1)
                pe.wait_ge(S["sum_done"], (bh + 1) * NSUM)
                for n in range(NTURN):
                    b, ph, k = turn(n)
                    if n >= 8:
                        pe.wait_ge(S["turned_dve" if n % 2 else "turned_act"], bh * NTURN // 2 + (n - 8) // 2 + 1)
                    pe.matmul(banks[n % 8][:], flip[:], u[:, ph, k:k + 2, b], start=True, stop=True)\
                        .then_inc(S["turned_ps"], 1)
                pe.wait_ge(S["turned_act"], (bh + 1) * NTURN // 2)
                pe.wait_ge(S["turned_dve"], (bh + 1) * NTURN // 2)

            def chunk_free(c, unit):
                if not (isinstance(unit, int) and unit == 0):
                    pe.wait_ge(S["total_ready"], unit * 2 - (1 - c))

            def conv_lag(p, lag, b, unit):
                ph, sh = (p, lag // 2) if lag != 1 else (1 - p, 1 - p)
                for c in range(NC2):
                    chunk_free(c, unit)
                    first = True
                    for i in range(-1 if sh and C0 + c else 0, P_BLKS):
                        for hl in range(2):
                            lo = max(0, P * i)
                            hi = min(CH, P * i + P + (P if sh else 0))
                            mm = pe.matmul(psU[c][:, lo:hi], u[:, ph, P_BLKS * (C0 + c) + i, b, hl, :],
                                           shift[sh][:, lo - P * i:hi - P * i], start=first, stop=False,
                                           skip_group_check=True)
                            first = False
                    mm.then_inc(S["conv_done"], 1)

            def conv(p, r, b, unit, funit):
                ph, _ = half(p, r)

                def product(bank, lo, hi, src, blk, filt_cols, x, first=False):
                    for m, (hu, hh) in enumerate(((0, 0), (0, 1), (1, 0))):
                        mm = pe.matmul(bank[:, lo:hi], src[:, ph, blk, b, hu, :], filt_cols(hh, x, x + hi - lo),
                                       start=(first and m == 0), stop=False, skip_group_check=True)
                    return mm

                def f(hh, x0, x1):
                    return Hf[r][:, hh, x0:x1]

                def win(w):
                    return lambda hh, x0, x1: Hw[r][:, hh, w - W0, x0:x1]

                if not (isinstance(funit, int) and funit == 0):
                    pe.wait_ge(S["ec_copied"], funit)
                if upper:
                    for j in range(2):
                        product(psE, 0, HC2, us_sum, 2 + j, win(6), P - P * j, first=(j == 0))
                        mm = product(psE, HC2, CH, us_sum, j, win(7), P - P * j)
                    mm.then_inc(S["e_done"], 1)
                    for j in range(2):
                        product(psC, 0, HC2, us_sum, HSUM + 2 + j, win(0), P - P * j, first=(j == 0))
                    for j in range(2):
                        product(psC, HC2, CH, us_sum, HSUM + j, win(1), P - P * j)
                for j in range(2):
                    mm = product(psC, HC2, CH, us_sum, HSUM + 2 * C0 + j, f, CH - P * j, first=(not upper and j == 0))
                if upper:
                    mm.then_inc(S["c_done"], 1)
                    pe.wait_ge(S["e_copied"], funit + 1)
                    for j in range(2):
                        mm = product(psE, 0, HC2, us_sum, HSUM + 2 * (C0 + 1) + j, f, 2 * CH - P * j, first=(j == 0))
                mm.then_inc(S["ec_done"], 1)
                rest = (((2, 1),), ((4, 0), (8, 2))) if upper else ((), ((8, 0),))
                for c in range(NC2):
                    chunk_free(c, unit)
                    first = True
                    for w, src in rest[c]:
                        for j in range(2):
                            product(psU[c], 0, HC2, u, P_BLKS * src + 2 + j, win(w), P - P * j, first=first)
                            first = False
                            product(psU[c], HC2, CH, u, P_BLKS * src + j, win(w + 1), P - P * j)
                    for j in range(P_BLKS):
                        mm = product(psU[c], P * j, CH, u, P_BLKS * (C0 + c) + j, f, 0, first=(first and j == 0))
                    mm.then_inc(S["conv_done"], 1)

            def project(slot, b, unit, first=False):
                for c in range(NC2):
                    pe.wait_ge(S["us_ready"], unit * 2 + (c + 1))
                    for mx_, lo, hi in spans[c]:
                        for hm, hu in ((0, 0), (1, 0), (0, 1)):
                            m = Mx[mx_][:, slot, hm, :] if isinstance(slot, int) else \
                                Mx[mx_][:, bass.ds(slot, 1), hm, :].rearrange("d a e -> d (a e)")
                            mm = pe.matmul(psY[b][c][:, lo:hi], m, us[:, b, c, hu, lo:hi],
                                           start=(first and lo == 0 and hm == 0 and hu == 0),
                                           stop=False, skip_group_check=True)
                return mm

            for n, (bh, p) in enumerate(jobs):
                base, fbase = UNITS * n, FUNITS * n
                if p == 0:
                    turn_blocks(bh)
                if n == 0:
                    pe.wait_ge(S["m_in"], 16 * len(mixes))
                else:
                    pe.wait_ge(S["y_read"], NB2 * n)
                queue = [(lag, b) for lag in range(LAGS) for b in range(NB2)]
                for q, (lag, b) in enumerate(queue):
                    conv_lag(p, lag, b, base + q)
                    if q:
                        lg, bb = queue[q - 1]
                        project(lg, bb, base + q - 1, first=(lg == 0))
                with pe.Fori(0, KF) as k:
                    for r in range(2):
                        pe.wait_ge(h_in[r], k * (16 * H_DMAS) + 16 * H_DMAS * (KF * n + 1))
                        for b in range(NB2):
                            q = r * NB2 + b
                            unit = k * (2 * NB2) + (base + LAGS * NB2 + q)
                            conv(p, r, b, unit, k * (2 * NB2) + (fbase + q))
                            project(k * 2 + (LAGS - 1 if q == 0 else LAGS + (q - 1) // NB2), (q - 1) % NB2,
                                    k * (2 * NB2) + (base + LAGS * NB2 + q - 1))
                project(NMAT - 1, NB2 - 1, base + UNITS - 1).then_inc(S["y_done"], 1)

        @block.scalar
        def _(act):
            def hi(b, unit):
                for c in range(NC2):
                    act.wait_ge(S["total_ready"], unit * 2 + (c + 1))
                    act.activation(us[:, b, c, 0, :], Y_sb[:, c, :], ACT.Copy, scale=1.0 / (U_SCALE * F_SCALE))\
                        .then_inc(S["hi_ready"], 1)

            for n, (bh, p) in enumerate(jobs):
                if p == 0:
                    for m in range(NSUM):
                        ph, j = summed(m)
                        act.wait_ge(S["sum_ps"], bh * NSUM + m + 1)
                        act.copy(us_sum[:, ph, j:j + 2, :, 0, :],
                                 banks[m % 8][:].rearrange("p (j b d) -> p j b d", j=2, b=NB2)).then_inc(S["sum_hi"], 1)
                    for m in range(0, NTURN, 2):
                        b, ph, k = turn(m)
                        act.wait_ge(S["turned_ps"], bh * NTURN + m + 1)
                        act.copy(u[:, ph, k:k + 2, b], banks[m % 8][:].rearrange("p (k h d) -> p k h d", k=2, h=2))\
                            .then_inc(S["turned_act"], 1)
                for q in range(LAGS * NB2):
                    hi(q % NB2, UNITS * n + q)
                with act.Fori(0, 2 * KF) as j:
                    for b in range(NB2):
                        after = j * NB2 + (FUNITS * n + b + 1)
                        if upper:
                            act.wait_ge(S["e_done"], after)
                            act.copy(E_sb[:], psE[:]).then_inc(S["e_copied"], 1)
                            act.wait_ge(S["c_done"], after)
                            act.copy(C_sb[:].rearrange("p c x -> p (c x)"), psC[:])
                        act.wait_ge(S["ec_done"], after)
                        if upper:
                            act.copy(EC_sb[:], psE[:, 0:HC2]).then_inc(S["ec_copied"], 1)
                        else:
                            act.copy(C_sb[:, 1, :], psC[:, HC2:]).then_inc(S["ec_copied"], 1)
                        hi(b, j * NB2 + (UNITS * n + LAGS * NB2 + b))

        @block.vector
        def _(v):
            def lo(b, unit):
                for c in range(NC2):
                    v.wait_ge(S["hi_ready"], unit * 2 + (c + 1))
                    v.scalar_tensor_tensor(out=us[:, b, c, 1, :], in0=Y_sb[:, c, :], scalar=1.0 / (U_SCALE * F_SCALE),
                                           in1=us[:, b, c, 0, :], op0=ALU.mult, op1=ALU.subtract)\
                        .then_inc(S["us_ready"], 1)

            for n, (bh, p) in enumerate(jobs):
                if p == 0:
                    for m in range(NSUM):
                        ph, j = summed(m)
                        v.wait_ge(S["sum_hi"], bh * NSUM + m + 1)
                        v.tensor_tensor(us_sum[:, ph, j:j + 2, :, 1, :],
                                        banks[m % 8][:].rearrange("p (j b d) -> p j b d", j=2, b=NB2),
                                        us_sum[:, ph, j:j + 2, :, 0, :], ALU.subtract).then_inc(S["sum_done"], 1)
                    for m in range(1, NTURN, 2):
                        b, ph, k = turn(m)
                        v.wait_ge(S["turned_ps"], bh * NTURN + m + 1)
                        v.tensor_copy(u[:, ph, k:k + 2, b], banks[m % 8][:].rearrange("p (k h d) -> p k h d", k=2, h=2))\
                            .then_inc(S["turned_dve"], 1)
                for q in range(LAGS * NB2):
                    unit = UNITS * n + q
                    for c in range(NC2):
                        if unit:
                            v.wait_ge(S["us_ready"], 2 * unit + c - 1)
                        v.wait_ge(S["conv_done"], 2 * unit + c + 1)
                        v.tensor_copy(Y_sb[:, c, :], psU[c][:]).then_inc(S["total_ready"], 1)
                    lo(q % NB2, unit)
                with v.Fori(0, 2 * KF) as j:
                    for b in range(NB2):
                        unit, funit = j * NB2 + (UNITS * n + LAGS * NB2 + b), j * NB2 + (FUNITS * n + b)
                        for c in range(NC2):
                            own, y1 = psU[c][:], Y_sb[:, c, :]
                            v.wait_ge(S["us_ready"], unit * 2 + (c - 1))
                            if c == 0 and upper or c == 1 and not upper:
                                v.wait_ge(S["ec_copied"], funit + 1)
                            if c == 0 and upper:
                                v.tensor_tensor(C_sb[:], C_sb[:], EC_sb[:].unsqueeze(1).to_broadcast([P, NC2, HC2]),
                                                ALU.add).then_inc(S["c_total"], 1)
                                v.wait_ge(S["c_total"], funit + 1)
                            v.wait_ge(S["conv_done"], unit * 2 + (c + 1))
                            shared = C_sb[:, c, :].unsqueeze(1).to_broadcast([P, 2, HC2])
                            y2 = y1.rearrange("p (a x) -> p a x", a=2)
                            if upper:
                                v.tensor_tensor(y1, own, E_sb[:], ALU.add).then_inc(S["added"], 1)
                                v.wait_ge(S["added"], funit * 2 + (c + 1))
                                v.tensor_tensor(y2, y2, shared, ALU.add).then_inc(S["total_ready"], 1)
                            elif c:
                                v.tensor_tensor(y2, own.rearrange("p (a x) -> p a x", a=2), shared, ALU.add)\
                                    .then_inc(S["total_ready"], 1)
                            else:
                                v.tensor_copy(y1, own).then_inc(S["total_ready"], 1)
                        lo(b, unit)
                v.wait_ge(S["y_done"], n + 1)
                v.wait_ge(S["t_in"], 16 * 4 * NB2 * (bh + 1))
                for b in range(NB2):
                    for c in range(NC2):
                        for mx_, a, z in spans[c]:
                            t2 = tT[:, b, 2 * CH * c:2 * CH * (c + 1)].rearrange("e (m q) -> e q m", q=2)[:, p, a:z]
                            ins = v.scalar_tensor_tensor(out=t2, in0=psY[b][c][:, a:z], scalar=mgain[:, mx_:mx_ + 1],
                                                         in1=t2, op0=ALU.mult, op1=ALU.add)
                    ins.then_inc(S["y_read"], 1)


def program(nc, x, wq, wk, wv, rel_h, rel_w, theta, phi_ffn, w1, b1, w2, b2, g1, be1, g2, be2,
            sigma, phi, m_u, m_plus, m_minus, log_weights, gumbel, out):
    xn_strips = nc.dram_tensor("xn_strips", [NSTRIP, P, KROWS * KCOLS + STOK], F32, kind="Internal").ap()
    u_dram = nc.dram_tensor("u_dram", [NSTRIP, STOK, 2 * P], F16, kind="Internal").ap()
    t_dram = nc.dram_tensor("t_dram", [NSTRIP, P, STOK], F32, kind="Internal").ap()
    filt = nc.dram_tensor("filt", [KF, 2, 2, FLEN], F16, kind="Internal").ap()
    wins = nc.dram_tensor("wins", [KF, 2, 2, NWIN, WLEN], F16, kind="Internal").ap()
    mats = nc.dram_tensor("mats", [NV, P, NMAT * 2 * P], F16, kind="Internal").ap()
    with ExitStack() as ctx:
        def sb(name, shape):
            return ctx.enter_context(nc.sbuf_tensor("k_" + name, shape, F32))

        ident, mgain = sb("ident", [P, P]), sb("mgain", [P, NV])
        with ExitStack() as inner:
            def si(name, shape, dt=F32):
                return inner.enter_context(nc.sbuf_tensor("k_" + name, shape, dt))

            pers = {"ident": ident, "halfpi": si("halfpi", [P, 1]), "wk": si("wk", [P, 2, P]),
                    "LA": si("LA", [P, PQ, P]), "LB": si("LB", [P, 16, P]), "wv": si("wv", [P, P]),
                    "hotA": si("hotA", [P, KROWS, KCOLS]), "hotB": si("hotB", [P, KROWS, KCOLS]),
                    "mask": si("mask", [P, KEYS]), "cosphi": si("cosphi", [P, NQB]),
                    "identb": si("identb", [P, P], BF16)}
            prepare(nc, pers, x, wq, wk, wv, rel_h, rel_w, phi_ffn, xn_strips)
            with ExitStack() as tctx:
                tok = {name: tctx.enter_context(nc.sbuf_tensor("k_" + name, shape, dt)) for name, shape, dt in (
                    ("theta", [P, P], F32), ("w1s", [KST, FF], BF16), ("w2T", [P, FT, P], F32),
                    ("qT", [KST, STOK], BF16), ("g1", [P, P], F32), ("be1", [P, P], F32), ("g2", [P, P], F32),
                    ("be2", [P, P], F32), ("b2", [P, P], F32))}
                load_token_weights(nc, tok, theta, w1, b1, w2, b2, g1, be1, g2, be2, ident, pers["identb"])
                strips(nc, pers, tok, xn_strips, u_dram, t_dram)
        spectral_prepare(nc, ident, phi, sigma, m_u, m_plus, m_minus, log_weights, gumbel, filt, wins, mats,
                         mgain)
        for upper in (False, True):
            spectral_half(nc, upper, u_dram, t_dram, filt, wins, mats, mgain, out)


_INS = ['x', 'L0_conv_Wq', 'L0_conv_Wk', 'L0_conv_Wv', 'L0_conv_rel_h', 'L0_conv_rel_w',
        'L1_attn_theta_attn', 'L1_attn_phi_ffn', 'L1_attn_w1', 'L1_attn_b1', 'L1_attn_w2', 'L1_attn_b2',
        'L1_attn_gamma1', 'L1_attn_beta1', 'L1_attn_gamma2', 'L1_attn_beta2',
        'L1_ffn_sigma', 'L1_ffn_phi', 'L1_ffn_M_u', 'L1_ffn_M_phi_plus', 'L1_ffn_M_phi_minus',
        'L1_ffn_log_weights', 'L1_ffn_gumbel']
_OUTS = [((4, 128, 64, 64), 'float32')]


def kernel(**inputs):
    import numpy as _np
    import concourse.bacc as _bacc
    from concourse import mybir as _mybir
    from concourse.bass_utils import run_bass_kernel_spmd as _run

    nc = _bacc.Bacc("TRN2", target_bir_lowering=False, num_devices=1)
    arrays, args = {}, []
    for name in _INS:
        a = _np.ascontiguousarray(inputs[name])
        arrays[f"in_{name}_dram"] = a
        args.append(nc.dram_tensor(f"in_{name}_dram", a.shape, _mybir.dt.from_np(a.dtype), kind="ExternalInput").ap())
    for i, (shape, dtype) in enumerate(_OUTS):
        dt = _mybir.dt.from_np(_np.dtype(dtype))
        args.append(nc.dram_tensor(f"out_{i}_dram", shape, dt, kind="ExternalOutput").ap())
    program(nc, *args)
    r = _run(nc, [arrays], core_ids=[0])
    return r.results[0]["out_0_dram"]
```
